# Optimizing a Trainium2 kernel written in Bass

```python
import numpy as np
import jax
import jax.numpy as jnp

def _softmax(x, axis=-1):
    return jax.nn.softmax(x, axis=axis)

def _gelu(x):
    return jax.nn.gelu(x, approximate=True)

def _silu(x):
    return jax.nn.silu(x)

def _sigmoid(x):
    return jax.nn.sigmoid(x)

def _layernorm(x, axis=-1, eps=1e-05):
    m = jnp.mean(x, axis=axis, keepdims=True)
    v = jnp.var(x, axis=axis, keepdims=True)
    return (x - m) / jnp.sqrt(v + eps)

def _scatter_add(tgt, idx, src, axis=0):
    return tgt.at[idx].add(src)

def _segment_sum(src, seg, n):
    return jax.ops.segment_sum(src, seg, n)
kernel_name = 'mk_gnn_ffn_d2_gnn_r8_2bf898'

def setup_inputs(seed: int=0):
    np.random.seed(seed)
    _w = jnp.asarray

    def _rec_inputs():
        import jax
        import jax.numpy as jnp
        _gk = jax.random.key(seed)
        x = -0.0003713 + 1 * jax.random.normal(jax.random.fold_in(_gk, 1), (6250, 256), jnp.float32)
        _s = jax.random.randint(jax.random.fold_in(_gk, 2), (50000,), 0, 6250, jnp.int32)
        _d = jax.random.randint(jax.random.fold_in(_gk, 3), (50000,), 0, 6250, jnp.int32)
        _loop = jnp.arange(6250, dtype=jnp.int32)
        src = jnp.concatenate([_s, _d, _loop])
        dst = jnp.concatenate([_d, _s, _loop])
        _o = jnp.argsort(dst, stable=True)
        src = src[_o]
        dst = dst[_o]
        edge_attr_3 = -1.09012e-05 + 0.99985 * jax.random.normal(jax.random.fold_in(_gk, 12), (106250, 3), jnp.float32)
        return (x, src, dst, edge_attr_3)
    x, src, dst, edge_attr_3 = _rec_inputs()

    def _L0_gnn_setup():
        import jax, jax.numpy as jnp
        import numpy as np
        N = 6250
        E = 50000
        IN = 256
        H = 8
        D = 32
        EF = 3
        key = jax.random.key(seed)
        ks = jax.random.split(key, 8)
        x = jax.random.normal(ks[0], (N, IN), dtype=jnp.float32)
        edge_index = jax.random.randint(ks[1], (2, E), 0, N, dtype=jnp.int64)
        edge_attr = jax.random.normal(ks[2], (E, EF), dtype=jnp.float32)
        W = jax.random.normal(ks[3], (H * D, IN), dtype=jnp.float32) * np.float32(np.sqrt(2.0 / (IN + H * D)))
        a_src = jax.random.normal(ks[4], (H, D), dtype=jnp.float32) * np.float32(np.sqrt(2.0 / (H + D)))
        a_dst = jax.random.normal(ks[5], (H, D), dtype=jnp.float32) * np.float32(np.sqrt(2.0 / (H + D)))
        edge_W = jax.random.normal(ks[6], (H * D, EF), dtype=jnp.float32) * np.float32(np.sqrt(2.0 / (EF + H * D)))
        edge_b = jnp.zeros((H * D,), dtype=jnp.float32)
        bias = jnp.zeros((H * D,), dtype=jnp.float32)
        return {'x': x, 'W': W, 'a_src': a_src, 'a_dst': a_dst, 'edge_W': edge_W, 'edge_b': edge_b, 'bias': bias, 'edge_attr': edge_attr, 'edge_index': edge_index}
    _L0_gnn_all = _L0_gnn_setup()
    _L0_gnn_in = {k: v for k, v in _L0_gnn_all.items() if k in ('W', 'a_src', 'a_dst', 'edge_W', 'edge_b', 'bias')}
    del _L0_gnn_all

    def _L0_ffn_setup():
        import jax, jax.numpy as jnp
        import numpy as np
        DIM = 256
        H = 8
        D = 64
        G = 64
        INNER = H * D
        SCALE = D ** (-0.5)
        key = jax.random.key(seed)
        ks = jax.random.split(key, 12)
        B, N = (4, 2048)
        x = jax.random.normal(ks[0], (B, N, DIM), dtype=jnp.float32)
        s = lambda fan_in: 1.0 / np.sqrt(fan_in)
        W_fx = jax.random.normal(ks[1], (DIM, INNER), dtype=jnp.float32) * s(DIM)
        b_fx = jnp.zeros((INNER,), dtype=jnp.float32)
        W_x = jax.random.normal(ks[2], (DIM, INNER), dtype=jnp.float32) * s(DIM)
        b_x = jnp.zeros((INNER,), dtype=jnp.float32)
        A = jax.random.normal(ks[3], (G, D), dtype=jnp.float32)
        Q, _ = jnp.linalg.qr(A.T)
        W_slice = Q[:, :G].astype(jnp.float32)
        b_slice = jnp.zeros((G,), dtype=jnp.float32)
        W_q = jax.random.normal(ks[4], (D, D), dtype=jnp.float32) * s(D)
        W_k = jax.random.normal(ks[5], (D, D), dtype=jnp.float32) * s(D)
        W_v = jax.random.normal(ks[6], (D, D), dtype=jnp.float32) * s(D)
        W_out = jax.random.normal(ks[7], (INNER, DIM), dtype=jnp.float32) * s(INNER)
        b_out = jnp.zeros((DIM,), dtype=jnp.float32)
        temperature = jnp.ones((1, H, 1, 1), dtype=jnp.float32) * 0.5
        return {'x': x, 'W_fx': W_fx, 'b_fx': b_fx, 'W_x': W_x, 'b_x': b_x, 'W_slice': W_slice, 'b_slice': b_slice, 'W_q': W_q, 'W_k': W_k, 'W_v': W_v, 'W_out': W_out, 'b_out': b_out, 'temperature': temperature}
    _L0_ffn_all = _L0_ffn_setup()
    _L0_ffn_in = {k: v for k, v in _L0_ffn_all.items() if k in ('W_fx', 'b_fx', 'W_x', 'b_x', 'W_slice', 'b_slice', 'W_q', 'W_k', 'W_v', 'W_out', 'b_out', 'temperature')}
    del _L0_ffn_all

    def _L1_gnn_setup():
        import jax, jax.numpy as jnp
        import numpy as np
        N_NODES = 6250
        N_EDGES = 100000
        DIM = 256
        NUM_HEADS = 8
        key = jax.random.key(seed)
        k_x, k_wu, k_bu, k_wv, k_src, k_dst = jax.random.split(key, 6)
        x = jax.random.normal(k_x, (N_NODES, DIM), dtype=jnp.float32)
        W_u = jax.random.normal(k_wu, (NUM_HEADS, DIM), dtype=jnp.float32) * (1.0 / np.sqrt(DIM))
        b_u = jax.random.normal(k_bu, (NUM_HEADS,), dtype=jnp.float32) * 0.01
        W_v = jax.random.normal(k_wv, (NUM_HEADS, DIM), dtype=jnp.float32) * (1.0 / np.sqrt(DIM))
        src = jax.random.randint(k_src, (N_EDGES,), 0, N_NODES, dtype=jnp.int32)
        dst = jax.random.randint(k_dst, (N_EDGES,), 0, N_NODES, dtype=jnp.int32)
        return {'x': x, 'W_u': W_u, 'b_u': b_u, 'W_v': W_v, 'src': src, 'dst': dst}
    _L1_gnn_all = _L1_gnn_setup()
    _L1_gnn_in = {k: v for k, v in _L1_gnn_all.items() if k in ('W_u', 'b_u', 'W_v')}
    del _L1_gnn_all

    def _L1_ffn_setup():
        import jax, jax.numpy as jnp
        import numpy as np
        TOP_K = 2
        LN_EPS = 1e-05
        key = jax.random.key(seed)
        ks = jax.random.split(key, 8)
        B, S, D, E, H = (16, 1024, 256, 8, 1024)
        x = jax.random.normal(ks[0], (B, S, D), dtype=jnp.float32)
        Wr = jax.random.normal(ks[1], (D, E), dtype=jnp.float32) * 0.1
        br = jnp.zeros((E,), dtype=jnp.float32)
        ln_g = jnp.ones((E, D), dtype=jnp.float32)
        ln_b = jnp.zeros((E, D), dtype=jnp.float32)
        W1 = jax.random.normal(ks[2], (E, D, H), dtype=jnp.float32) * (1.0 / np.sqrt(D))
        b1 = jnp.zeros((E, H), dtype=jnp.float32)
        W2 = jax.random.normal(ks[3], (E, H, D), dtype=jnp.float32) * (1.0 / np.sqrt(H))
        b2 = jnp.zeros((E, D), dtype=jnp.float32)
        return {'x': x, 'Wr': Wr, 'br': br, 'ln_g': ln_g, 'ln_b': ln_b, 'W1': W1, 'b1': b1, 'W2': W2, 'b2': b2}
    _L1_ffn_all = _L1_ffn_setup()
    _L1_ffn_in = {k: v for k, v in _L1_ffn_all.items() if k in ('Wr', 'br', 'ln_g', 'ln_b', 'W1', 'b1', 'W2', 'b2')}
    del _L1_ffn_all
    return {'x': x, 'src': src, 'dst': dst, 'edge_attr_3': edge_attr_3, 'L0_gnn_W': _L0_gnn_in['W'], 'L0_gnn_a_src': _L0_gnn_in['a_src'], 'L0_gnn_a_dst': _L0_gnn_in['a_dst'], 'L0_gnn_edge_W': _L0_gnn_in['edge_W'], 'L0_gnn_edge_b': _L0_gnn_in['edge_b'], 'L0_gnn_bias': _L0_gnn_in['bias'], 'L0_ffn_W_fx': _L0_ffn_in['W_fx'], 'L0_ffn_b_fx': _L0_ffn_in['b_fx'], 'L0_ffn_W_x': _L0_ffn_in['W_x'], 'L0_ffn_b_x': _L0_ffn_in['b_x'], 'L0_ffn_W_slice': _L0_ffn_in['W_slice'], 'L0_ffn_b_slice': _L0_ffn_in['b_slice'], 'L0_ffn_W_q': _L0_ffn_in['W_q'], 'L0_ffn_W_k': _L0_ffn_in['W_k'], 'L0_ffn_W_v': _L0_ffn_in['W_v'], 'L0_ffn_W_out': _L0_ffn_in['W_out'], 'L0_ffn_b_out': _L0_ffn_in['b_out'], 'L0_ffn_temperature': _L0_ffn_in['temperature'], 'L1_gnn_W_u': _L1_gnn_in['W_u'], 'L1_gnn_b_u': _L1_gnn_in['b_u'], 'L1_gnn_W_v': _L1_gnn_in['W_v'], 'L1_ffn_Wr': _L1_ffn_in['Wr'], 'L1_ffn_br': _L1_ffn_in['br'], 'L1_ffn_ln_g': _L1_ffn_in['ln_g'], 'L1_ffn_ln_b': _L1_ffn_in['ln_b'], 'L1_ffn_W1': _L1_ffn_in['W1'], 'L1_ffn_b1': _L1_ffn_in['b1'], 'L1_ffn_W2': _L1_ffn_in['W2'], 'L1_ffn_b2': _L1_ffn_in['b2']}

def reference(x, src, dst, edge_attr_3, L0_gnn_W, L0_gnn_a_src, L0_gnn_a_dst, L0_gnn_edge_W, L0_gnn_edge_b, L0_gnn_bias, L0_ffn_W_fx, L0_ffn_b_fx, L0_ffn_W_x, L0_ffn_b_x, L0_ffn_W_slice, L0_ffn_b_slice, L0_ffn_W_q, L0_ffn_W_k, L0_ffn_W_v, L0_ffn_W_out, L0_ffn_b_out, L0_ffn_temperature, L1_gnn_W_u, L1_gnn_b_u, L1_gnn_W_v, L1_ffn_Wr, L1_ffn_br, L1_ffn_ln_g, L1_ffn_ln_b, L1_ffn_W1, L1_ffn_b1, L1_ffn_W2, L1_ffn_b2):
    import jax
    import jax.numpy as jnp

    def _L0_gnn_ref(x, W, a_src, a_dst, edge_W, edge_b, bias, edge_attr, edge_index):
        import jax, jax.numpy as jnp
        import numpy as np
        N = 6250
        E = 50000
        IN = 256
        H = 8
        D = 32
        EF = 3
        n = x.shape[0]
        h = (x @ W.T).reshape(n, H, D)
        src, dst = (edge_index[0], edge_index[1])
        h_src = h[src]
        h_dst = h[dst]
        alpha = jnp.einsum('ehd,hd->eh', h_src, a_src) + jnp.einsum('ehd,hd->eh', h_dst, a_dst)
        enc = jax.nn.relu(edge_attr @ edge_W.T + edge_b).reshape(-1, H, D)
        alpha = alpha + jnp.sum(enc * h_dst, axis=-1)
        alpha = jnp.where(alpha >= 0, alpha, 0.2 * alpha)
        amax = jax.ops.segment_max(alpha, dst, num_segments=n)
        ex = jnp.exp(alpha - amax[dst])
        denom = jax.ops.segment_sum(ex, dst, num_segments=n)
        attn = ex / jnp.maximum(denom[dst], 1e-10)
        out = jax.ops.segment_sum(h_src * attn[..., None], dst, num_segments=n)
        return out.reshape(n, H * D) + bias

    def _L0_ffn_ref(x, W_fx, b_fx, W_x, b_x, W_slice, b_slice, W_q, W_k, W_v, W_out, b_out, temperature):
        import jax, jax.numpy as jnp
        import numpy as np
        DIM = 256
        H = 8
        D = 64
        G = 64
        INNER = H * D
        SCALE = D ** (-0.5)
        B, N, _ = x.shape
        fx_mid = (x @ W_fx + b_fx).reshape(B, N, H, D).transpose(0, 2, 1, 3)
        x_mid = (x @ W_x + b_x).reshape(B, N, H, D).transpose(0, 2, 1, 3)
        temp = jnp.clip(temperature, 0.1, 5.0)
        slice_weights = jax.nn.softmax((x_mid @ W_slice + b_slice) / temp, axis=-1)
        slice_norm = slice_weights.sum(axis=2)
        slice_token = jnp.einsum('bhnc,bhng->bhgc', fx_mid, slice_weights)
        slice_token = slice_token / (slice_norm[..., None] + 1e-05)
        q = slice_token @ W_q
        k = slice_token @ W_k
        v = slice_token @ W_v
        attn = jax.nn.softmax(jnp.einsum('bhgc,bhkc->bhgk', q, k) * SCALE, axis=-1)
        out_slice = jnp.einsum('bhgk,bhkc->bhgc', attn, v)
        out_x = jnp.einsum('bhgc,bhng->bhnc', out_slice, slice_weights)
        out_x = out_x.transpose(0, 2, 1, 3).reshape(B, N, INNER)
        return out_x @ W_out + b_out

    def _L1_gnn_ref(x, W_u, b_u, W_v, src, dst):
        import jax, jax.numpy as jnp
        import numpy as np
        N_NODES = 6250
        N_EDGES = 100000
        DIM = 256
        NUM_HEADS = 8
        n_nodes, dim = x.shape
        num_heads = W_u.shape[0]
        head_dim = dim // num_heads
        s_u = x @ W_u.T + b_u
        s_v = x @ W_v.T
        e = s_u[src] + s_v[dst]
        e = jnp.where(e >= 0, e, 0.2 * e)
        m = jax.ops.segment_max(e, dst, num_segments=n_nodes)
        e_exp = jnp.exp(e - m[dst])
        denom = jax.ops.segment_sum(e_exp, dst, num_segments=n_nodes)
        probs = e_exp / denom[dst]
        xh = x.reshape(n_nodes, head_dim, num_heads)
        msg = xh[src] * probs[:, None, :]
        out = jax.ops.segment_sum(msg, dst, num_segments=n_nodes)
        return out.reshape(n_nodes, dim)

    def _L1_ffn_ref(x, Wr, br, ln_g, ln_b, W1, b1, W2, b2):
        import jax, jax.numpy as jnp
        import numpy as np
        TOP_K = 2
        LN_EPS = 1e-05
        B, S, D = x.shape
        N = B * S
        xt = x.reshape(N, D)
        logits = xt @ Wr + br
        probs = jax.nn.softmax(logits, axis=-1)
        top_p, top_idx = jax.lax.top_k(probs, TOP_K)
        weights = top_p / top_p.sum(axis=-1, keepdims=True)
        mu = xt.mean(axis=-1, keepdims=True)
        var = ((xt - mu) ** 2).mean(axis=-1, keepdims=True)
        xn = (xt - mu) * jax.lax.rsqrt(var + LN_EPS)
        xe = xn[None, :, :] * ln_g[:, None, :] + ln_b[:, None, :]
        h = jax.nn.gelu(jnp.einsum('end,edh->enh', xe, W1) + b1[:, None, :], approximate=False)
        y = jnp.einsum('enh,ehd->end', h, W2) + b2[:, None, :]
        y_tok = jnp.transpose(y, (1, 0, 2))
        sel = jnp.take_along_axis(y_tok, top_idx[:, :, None], axis=1)
        out = (weights[:, :, None] * sel).sum(axis=1)
        return out.reshape(B, S, D)
    edge_index = jnp.stack([src, dst])
    x = x + _L0_gnn_ref(_layernorm(x, axis=-1), L0_gnn_W, L0_gnn_a_src, L0_gnn_a_dst, L0_gnn_edge_W, L0_gnn_edge_b, L0_gnn_bias, edge_attr_3, edge_index)
    x = x + _L0_ffn_ref(_layernorm(x, axis=-1)[None], L0_ffn_W_fx, L0_ffn_b_fx, L0_ffn_W_x, L0_ffn_b_x, L0_ffn_W_slice, L0_ffn_b_slice, L0_ffn_W_q, L0_ffn_W_k, L0_ffn_W_v, L0_ffn_W_out, L0_ffn_b_out, L0_ffn_temperature)[0]
    x = x + _L1_gnn_ref(_layernorm(x, axis=-1), L1_gnn_W_u, L1_gnn_b_u, L1_gnn_W_v, src, dst)
    x = x + _L1_ffn_ref(_layernorm(x, axis=-1)[None], L1_ffn_Wr, L1_ffn_br, L1_ffn_ln_g, L1_ffn_ln_b, L1_ffn_W1, L1_ffn_b1, L1_ffn_W2, L1_ffn_b2)[0]
    return x

_drawn_inputs = setup_inputs


def setup_inputs(seed=0):
    import zlib

    import numpy as np

    out = dict(_drawn_inputs(seed))
    spreads = {'L0_gnn_edge_b': (0.0, 0.1),
     'L0_gnn_bias': (0.0, 0.1),
     'L0_ffn_b_fx': (0.0, 0.1),
     'L0_ffn_b_x': (0.0, 0.452),
     'L0_ffn_b_slice': (0.0, 0.414),
     'L0_ffn_b_out': (0.0, 0.1),
     'L0_ffn_temperature': (0.5, 0.6),
     'L1_ffn_br': (0.0, 0.1),
     'L1_ffn_ln_g': (1.0, 0.2),
     'L1_ffn_ln_b': (0.0, 0.1),
     'L1_ffn_b1': (0.0, 0.1),
     'L1_ffn_b2': (0.0, 0.1)}
    factors = {'L0_ffn_W_slice': 3.607, 'L0_ffn_W_q': 8.0, 'L0_ffn_W_k': 8.0, 'L1_gnn_b_u': 39.74}
    for name, (base, spread) in spreads.items():
        noise = np.random.default_rng([zlib.crc32(name.encode()), seed]).standard_normal(out[name].shape)
        drawn = base * np.exp(spread * noise) if base else spread * noise
        out[name] = jnp.asarray(drawn.astype(out[name].dtype))
    for name, factor in factors.items():
        out[name] = (out[name] * factor).astype(out[name].dtype)
    return out
```

```python
import numpy as np
import concourse.bass as bass
from concourse import mybir
from contextlib import ExitStack

F32 = mybir.dt.float32
BF16 = mybir.dt.bfloat16
I32 = mybir.dt.int32
ALU = mybir.AluOpType
ACT = mybir.ActivationFunctionType
AX = mybir.AxisListType.X

N = 6250
E = 106250
D = 256
H = 8
HD = D // H
P = 125
NT = N // P
EP = E // P
Q = 128
QT = -(-N // Q)
NPAD = QT * Q
C = 4
REC = 4 * C
NB = 64
VW = HD + 1
RW = H * VW + 2 * H
CMAX = (E // C + 2 * QT + 8) // 4 * 4
BIG = 1e30
LN_EPS = 1e-5
G = 64
FH = 8
X = 8
HID = 1024
MT = 106
KC = HID // 128


class Chain:

    def __init__(self, eng, sem, base=0):
        self.eng, self.sem, self.base, self.n = eng, sem, base, 0

    def link(self, ins, wait=True):
        ins.then_inc(self.sem, 1)
        self.n += 1
        if wait:
            self.wait()

    def wait(self):
        self.eng.wait_ge(self.sem, self.base + self.n)

    def enter(self, i, k):
        self.outer, self.k, self.n0 = self.base, k, self.n
        self.base, self.n = self.base + self.n + i * k, 0

    def leave(self, times):
        assert self.n == self.k, (self.n, self.k)
        self.base, self.n = self.outer, self.n0 + times * self.k


def over(ap, axis, n):
    a = ap.unsqueeze(axis)
    shape = list(a.shape)
    shape[axis] = n
    return a.broadcast_to(shape)


def peeled(eng, n, body):
    body(0, True)
    with eng.Fori(1, n) as u:
        body(u, False)


class Mem:

    def __init__(self, nc, stack):
        self.nc, self.stack, self.sems = nc, stack, []
        stack.callback(self.clear)

    def clear(self):
        if self.sems:
            self.nc.clear_and_free_semaphores(self.sems)
            self.nc.all_engine_barrier()

    def sb(self, name, shape, dt=F32):
        return self.stack.enter_context(self.nc.sbuf_tensor(name, shape, dt))

    def ps(self, name, shape, dt=F32):
        return self.stack.enter_context(self.nc.psum_tensor(name, shape, dt))

    def sem(self, name):
        self.sems.append(self.nc.alloc_semaphore(name))
        return self.sems[-1]


class Norm:

    def __init__(self, m, name):
        self.st = m.sb(name + "_st", [P, NT, 6])
        self.a, self.b, self.rstd, self.nbias = (m.sb(name + s, [P, NT]) for s in ("_na", "_nb", "_rstd", "_nbias"))

    def tile(self, v, t, x):
        return v.bn_stats(self.st[:, bass.ds(t, 1), :].rearrange("p a c -> p (a c)"), x.rearrange("p a c -> p (a c)"))

    def variance(self, v, ch, done):
        st = self.st
        ch.link(v.tensor_tensor(self.a[:], st[:, :, 1], st[:, :, 4], ALU.subtract))
        ch.link(v.scalar_tensor_tensor(self.a[:], self.a[:], 0.25, self.a[:], ALU.mult, ALU.mult))
        ch.link(v.tensor_tensor(self.b[:], st[:, :, 2], st[:, :, 5], ALU.add))
        ch.link(v.scalar_tensor_tensor(self.a[:], self.b[:], 1.0 / D, self.a[:], ALU.mult, ALU.add))
        ch.link(v.tensor_scalar(self.rstd[:], self.a[:], LN_EPS, None, ALU.add))
        ch.link(v.tensor_tensor(self.b[:], st[:, :, 1], st[:, :, 4], ALU.add))
        v.tensor_scalar(self.nbias[:], self.b[:], -0.5, None, ALU.mult).then_inc(done, 1)

    def scales(self, v, ch, done):
        ch.link(v.reciprocal(self.rstd[:], self.rstd[:]))
        v.tensor_tensor(self.nbias[:], self.nbias[:], self.rstd[:], ALU.mult).then_inc(done, 1)


def prepare(nc, K, ins, dr):
    with ExitStack() as stack:
        m = Mem(nc, stack)
        x = m.sb("p_x", [P, NT, D])
        srcw = m.sb("p_srcw", [P, EP + C - 1], I32)
        attrw = m.sb("p_attrw", [P, 3 * (EP + C - 1)])
        PIECE = EP // 5
        rec = m.sb("p_rec", [P, 2, PIECE, REC])
        dst0 = m.sb("p_dst0", [P, 1], I32)
        dst0f = m.sb("p_dst0f", [P, 1])
        iota_n = m.sb("p_iota_n", [P, N])
        below = m.sb("p_below", [P, N], BF16)
        ones = m.sb("p_ones", [P, 1], BF16)
        node = m.sb("p_node", [P, NT])
        blk = m.sb("p_blk", [P, NT])
        cnt = m.sb("p_cnt", [P, NT])
        blk_i = m.sb("p_blk_i", [P, NT], I32)
        R = 5
        idx = [m.sb(f"p_idx{r}", [P, 1], I32) for r in range(R)]
        drow = m.sb("p_drow", [P, R, EP], I32)
        rp = m.sb("p_rp", [P, NT], I32)
        e_end = m.sb("p_eend", [1, 1], I32)
        zrow = m.sb("p_zrow", [NPAD - N, RW])
        zxs = m.sb("p_zxs", [Q, D])
        wn = m.sb("p_wn", [128, 2, D])
        aa = m.sb("p_aa", [128, 2, 2])
        amask = m.sb("p_amask", [128, 4])
        ablk = m.sb("p_ablk", [128, 2, 2 * H])
        wx = m.sb("p_wx", [128, 2, D + 2 * H])
        norm = Norm(m, "p")
        rstd, nbias = norm.rstd, norm.nbias
        xn = m.sb("p_xn", [P, 2, D])
        xnT = m.sb("p_xnT", [128, 2, 2, P])
        row = m.sb("p_row", [P, 2, RW])
        pT = [m.ps(f"p_pT{r}", [128, 2, 256]) for r in range(2)]
        pH = [m.ps(f"p_pH{r}", [P, 512]) for r in range(2)]
        pW = m.ps("p_pW", [128, 2, 256])
        pC = m.ps("p_pC", [P, 64])

        x_in = m.sem("p_x_in"); e_in = m.sem("p_e_in"); w_in = m.sem("p_w_in"); d_in = m.sem("p_d_in")
        zeroed = m.sem("p_zeroed"); rec_made = m.sem("p_rec_made"); rec_out = [m.sem(f"p_rec_out{b}") for b in range(2)]
        misc_out = m.sem("p_misc_out")
        consts = m.sem("p_consts"); below_ok = m.sem("p_below_ok"); counted = m.sem("p_counted")
        idx_ok = m.sem("p_idx_ok"); landed = [m.sem(f"p_landed{r}") for r in range(R)]
        vch = m.sem("p_vchain"); stats = m.sem("p_stats"); sq = m.sem("p_sqrt"); rst = m.sem("p_rstd_ok")
        ach = m.sem("p_achain")
        ablk_ok = m.sem("p_ablk_ok"); wa_ok = m.sem("p_wa_ok"); wx_ok = m.sem("p_wx_ok")
        xn_ok = m.sem("p_xn_ok"); t_ok = m.sem("p_t_ok"); xnT_ok = m.sem("p_xnT_ok"); h_ok = m.sem("p_h_ok")
        row_ok = m.sem("p_row_ok"); row_out = [m.sem(f"p_row_out{b}") for b in range(2)]
        rp_ok = m.sem("p_rp_ok"); rp_out = m.sem("p_rp_out"); pace = m.sem("p_pace")

        rows0 = dr["rows0"][0:N, :].rearrange("(p t) c -> p t c", t=NT)
        recs = dr["rec"].rearrange("(p g e) c -> p g (e c)", p=P, g=5)

        with nc.Block() as block:
            @block.sync
            def _(sp):
                sp.dma_start(dst0[:], ins["dst"].rearrange("(p e) -> p e", p=P)[:, 0:1], allow_slow_non_contiguous=True).then_inc(d_in, 16)
                sp.dma_start(x[:], ins["x"].rearrange("(p t) c -> p t c", t=NT)).then_inc(x_in, 16)
                sp.wait_ge(zeroed, 2)
                s, a = ins["src"], ins["edge_attr_3"].rearrange("e c -> (e c)")
                sp.dma_start(srcw[0:P - 1, :], bass.AP(s.tensor, 0, [[EP, P - 1], [1, EP + C - 1]])).then_inc(e_in, 16)
                sp.dma_start(srcw[P - 1:P, 0:EP], s[E - EP:E].unsqueeze(0)).then_inc(e_in, 16)
                sp.dma_start(attrw[0:P - 1, :], bass.AP(a.tensor, 0, [[3 * EP, P - 1], [1, 3 * (EP + C - 1)]])).then_inc(e_in, 16)
                sp.dma_start(attrw[P - 1:P, 0:3 * EP], a[3 * (E - EP):3 * E].unsqueeze(0)).then_inc(e_in, 16)
                for g in range(5):
                    sp.wait_ge(rec_made, 2 * g + 2)
                    sp.dma_start(recs[:, g, :], rec[:, g % 2, :, :].rearrange("p e c -> p (e c)")).then_inc(rec_out[g % 2], 16)
                sp.wait_ge(zeroed, 6)
                sp.dma_start(dr["rows0"][N:NPAD, :], zrow[:]).then_inc(misc_out, 16)
                sp.dma_start(dr["rows1"][N:NPAD, :], zrow[:]).then_inc(misc_out, 16)
                sp.dma_start(dr["sv1"][N:NPAD, :], zrow[:, 0:H]).then_inc(misc_out, 16)
                sp.dma_start(dr["xs"].rearrange("(t p) c -> p t c", p=Q), over(zxs[:], 1, MT)).then_inc(misc_out, 16)
                with sp.Fori(0, NT // 2) as u:
                    for b in range(2):
                        sp.wait_ge(row_ok, 2 * u + (b + 1))
                        sp.dma_start(rows0[:, bass.ds(2 * u + b, 1), :].rearrange("p a c -> p (a c)"), row[:, b, :]).then_inc(row_out[b], 16)
                sp.wait_ge(row_out[0], 16 * (NT // 2))
                sp.wait_ge(row_out[1], 16 * (NT // 2))
                sp.wait_ge(rp_ok, 1)
                sp.dma_start(dr["rp"][:, 0:N].rearrange("o (p t) -> (o p) t", t=NT), rp[:]).then_inc(rp_out, 16)
                sp.dma_start(dr["rp"][:, N:N + 1], e_end[:]).then_inc(rp_out, 16)
                sp.wait_ge(rp_out, 32)
                sp.wait_ge(rec_out[0], 48)
                sp.wait_ge(rec_out[1], 32)
                sp.wait_ge(misc_out, 64)

            @block.gpsimd
            def _(pool):
                pool.memset(srcw[:], 0).then_inc(zeroed, 1)
                pool.memset(attrw[:], 0.0).then_inc(zeroed, 1)
                pool.iota(iota_n[:], pattern=[[1, N]], base=0, channel_multiplier=0,
                          allow_small_or_imprecise_dtypes=True).then_inc(consts, 1)
                pool.iota(node[:], pattern=[[1, NT]], base=0, channel_multiplier=NT,
                          allow_small_or_imprecise_dtypes=True).then_inc(consts, 1)
                pool.memset(ones[:], 1.0).then_inc(consts, 1)
                pool.memset(K["ident"][:], 0.0)
                pool.memset(K["tri"][:], 1.0)
                pool.memset(K["ones"][:], 1.0)
                pool.memset(amask[:], 1.0)
                pool.memset(row[:], 1.0)
                pool.iota(K["iota64"][:], pattern=[[1, NB]], base=0, channel_multiplier=0,
                          allow_small_or_imprecise_dtypes=True)
                pool.memset(zrow[:], 0.0)
                pool.memset(zxs[:], 0.0).then_inc(consts, 1)
                pool.wait_ge(consts, 4)
                pool.affine_select(out=K["ident"][:], in_=K["ident"][:], compare_op=ALU.not_equal, fill=1.0, base=0,
                                   pattern=[[-1, 128]], channel_multiplier=1)
                pool.affine_select(out=K["tri"][:], in_=K["tri"][:], compare_op=ALU.is_gt, fill=0.0, base=0,
                                   pattern=[[1, 128]], channel_multiplier=-1)
                pool.affine_select(out=amask[:], in_=amask[:], compare_op=ALU.is_ge, fill=0.0, base=0,
                                   pattern=[[-HD, 4]], channel_multiplier=1).then_inc(consts, 1)
                pool.wait_ge(consts, 5)
                pool.affine_select(out=amask[:], in_=amask[:], compare_op=ALU.is_ge, fill=0.0, base=HD - 1,
                                   pattern=[[HD, 4]], channel_multiplier=-1)
                pool.iota(e_end[:], pattern=[[0, 1]], base=E, channel_multiplier=0).then_inc(consts, 1)
                pool.wait_ge(consts, 6)
                pool.iota(K["padrec"][:], pattern=[[0, 4]], base=N, channel_multiplier=1).then_inc(consts, 1)
                pool.wait_ge(consts, 7)
                pool.memset(K["padrec"][:, 1:4], 0).then_inc(zeroed, 4)
                pool.wait_ge(zeroed, 6)
                dview = ins["dst"].rearrange("(p e) -> p e", p=P)

                def gather(u, r):
                    pool.wait_ge(idx_ok, u * R + (r + 1))
                    pool.sem_inc(pace, 1)
                    pool.indirect_dma_start(out=drow[:, r, :], out_offset=None, in_=dview,
                                            in_offset=bass.IndirectOffsetOnAxis(ap=idx[r][:, 0:1], axis=0)
                                            ).then_inc(landed[r], 16)
                with pool.Fori(0, NT // R) as u:
                    for r in range(R):
                        gather(u, r)

            @block.vector
            def _(dve):
                v = nc.vector
                ch = Chain(dve, vch)
                dve.wait_ge(consts, 7)
                dve.wait_ge(d_in, 16)
                ch.link(v.tensor_copy(dst0f[:], dst0[:]))
                v.tensor_scalar(below[:], iota_n[:], dst0f[:], None, ALU.is_gt).then_inc(below_ok, 1)
                dve.wait_ge(w_in, 64)
                for k in range(2):
                    for s in range(2):
                        if k == 0 and s == 0:
                            ch.link(v.memset(ablk[:], 0.0))
                        last = v.tensor_scalar(ablk[:, k, s * H + 4 * k:s * H + 4 * k + 4], amask[:], aa[:, k, s:s + 1], None, ALU.mult)
                last.then_inc(ablk_ok, 1)
                dve.wait_ge(e_in, 64)
                for g in range(5):
                    if g >= 2:
                        dve.wait_ge(rec_out[g % 2], 16 * (g // 2))
                    o = rec[:, g % 2, :, :]
                    sw = bass.AP(srcw, g * PIECE, [[EP + C - 1, P], [1, PIECE], [1, C]])
                    aw = bass.AP(attrw, 3 * g * PIECE, [[3 * (EP + C - 1), P], [3, PIECE], [1, 3 * C]])
                    v.tensor_copy(o[:, :, 0:C].bitcast(I32), sw).then_inc(rec_made, 1)
                    v.tensor_copy(o[:, :, C:REC], aw).then_inc(rec_made, 1)
                dve.wait_ge(x_in, 16)
                with dve.Fori(0, NT) as t:
                    norm.tile(v, t, x[:, bass.ds(t, 1), :])
                ch.link(v.memset(norm.a[:], 0.0))
                norm.variance(v, ch, stats)
                dve.wait_ge(sq, 1)
                norm.scales(v, ch, rst)
                dve.wait_ge(counted, 1)
                ch.link(v.tensor_scalar(blk[:], pC[:, 0:NT], -1.0, 0.0, ALU.add, ALU.max))
                ch.link(v.tensor_copy(blk_i[:], blk[:]))
                for r in range(R):
                    v.tensor_copy(idx[r][:], blk_i[:, r:r + 1]).then_inc(idx_ok, 1)

                def count(u, r, more):
                    t = u * R + r
                    dve.wait_ge(landed[r], 16 * u + 16)
                    dve.sem_inc(pace, 1)
                    tc = bass.ds(t, 1)
                    last = v.tensor_scalar(drow[:, r, :], drow[:, r, :], node[:, tc], 0.0, ALU.is_lt, ALU.add, accum_out=cnt[:, tc])
                    if more:
                        v.tensor_copy(idx[r][:], blk_i[:, bass.ds(t + R, 1)]).then_inc(idx_ok, 1)
                    return last
                with dve.Fori(0, NT // R - 1) as u:
                    for r in range(R):
                        count(u, r, True)
                for r in range(R):
                    last = count(NT // R - 1, r, False)
                ch.link(last)
                ch.link(v.scalar_tensor_tensor(cnt[:], blk[:], float(EP), cnt[:], ALU.mult, ALU.add))
                v.tensor_copy(rp[:], cnt[:]).then_inc(rp_ok, 1)

            @block.scalar
            def _(act):
                s = nc.scalar
                act.dma_start(wn[:], ins["L0_gnn_W"].rearrange("(k p) i -> p k i", p=128)).then_inc(w_in, 16)
                for q, nm in enumerate(("L0_gnn_a_src", "L0_gnn_a_dst")):
                    act.dma_start(aa[:, :, q:q + 1], ins[nm].rearrange("h (d o) -> (h d) o", o=1).rearrange("(k p) o -> p k o", p=128), allow_slow_non_contiguous=True).then_inc(w_in, 16)
                act.dma_start(wx[:, :, 0:D], ins["L0_gnn_WT"].rearrange("(k p) o -> p k o", p=128), allow_slow_non_contiguous=True).then_inc(w_in, 16)
                act.wait_ge(stats, 1)
                s.activation(rstd[:], rstd[:], ACT.Sqrt).then_inc(sq, 1)
                act.wait_ge(w_in, 64)
                act.wait_ge(wa_ok, 1)
                s.activation(wx[:, :, D:D + 2 * H], pW[:, :, 0:2 * H], ACT.Copy).then_inc(wx_ok, 1)
                act.wait_ge(rst, 1)

                def tile(u, first):
                    for b in range(2):
                        t = 2 * u + b
                        tc = bass.ds(t, 1)
                        s.activation(xn[:, b, :], x[:, tc, :].rearrange("p a c -> p (a c)"), ACT.Identity,
                                     bias=nbias[:, tc], scale=rstd[:, tc]).then_inc(xn_ok, 1)
                        act.wait_ge(t_ok, t + 1)
                        s.activation(xnT[:, b, :, :], pT[b][:, :, 0:P], ACT.Copy).then_inc(xnT_ok, 1)
                        act.wait_ge(h_ok, t + 1)
                        if not first:
                            act.sem_inc(pace, 1)
                            act.wait_ge(row_out[b], 16 * u)
                        s.activation(row[:, b, 0:H * VW].rearrange("p (h c) -> p h c", h=H)[:, :, 0:HD],
                                     pH[b][:, 0:D].rearrange("p (h c) -> p h c", h=H), ACT.Copy)
                        s.activation(row[:, b, H * VW:RW], pH[b][:, D:D + 2 * H], ACT.Copy).then_inc(row_ok, 1)
                peeled(act, NT // 2, tile)

            @block.tensor
            def _(pe):
                t_ = nc.tensor
                pe.wait_ge(below_ok, 1)
                bl = below[:, :].rearrange("p (n t) -> p t n", t=NT)
                for t in range(NT):
                    last = t_.matmul(pC[:, t:t + 1], bl[:, t, :], ones[:], start=True, stop=True)
                last.then_inc(counted, 1)
                pe.wait_ge(ablk_ok, 1)
                for i in range(2):
                    for k in range(2):
                        last = t_.matmul(pW[:, i, 0:2 * H], wn[:, k, i * 128:(i + 1) * 128], ablk[:, k, :], start=(k == 0), stop=(k == 1))
                last.then_inc(wa_ok, 1)
                pe.wait_ge(wx_ok, 1)
                with pe.Fori(0, NT // 2) as u:
                    for b in range(2):
                        t = 2 * u + b
                        pe.wait_ge(xn_ok, t + 1)
                        for k in range(2):
                            last = t_.transpose(pT[b][:, k, 0:P], xn[:, b, k * 128:(k + 1) * 128], K["ident"][0:P, 0:P])
                        last.then_inc(t_ok, 1)
                        pe.wait_ge(xnT_ok, t + 1)
                        for k in range(2):
                            last = t_.matmul(pH[b][:, 0:D + 2 * H], xnT[:, b, k, :], wx[:, k, :], start=(k == 0), stop=(k == 1))
                        last.then_inc(h_ok, 1)


def order(nc, K, ins, dr):
    with ExitStack() as stack:
        m = Mem(nc, stack)
        OHW = NT * NB
        rec = m.sb("o_rec", [P, NT, 4], I32)
        nxt = m.sb("o_nxt", [P, NT], I32)
        rpi = m.sb("o_rpi", [P, NT], I32)
        deg = m.sb("o_deg", [P, NT])
        bkt = m.sb("o_bkt", [P, NT])
        hot = m.sb("o_hot", [P, NT, NB])
        tot = m.sb("o_tot", [P, NB, NT])
        exc = m.sb("o_exc", [P, NB, NT])
        rank = m.sb("o_rank", [P, NT, NB])
        posf = m.sb("o_posf", [P, NT])
        pos = m.sb("o_pos", [P, NT], I32)
        zero = m.sb("o_zero", [P, OHW])
        R = 5
        idx = [m.sb(f"o_idx{r}", [P, 1], I32) for r in range(R)]
        srow = [m.sb(f"o_srow{r}", [P, 4], I32) for r in range(R)]
        dT = m.sb("o_dT", [QT, Q])
        dmax = m.sb("o_dmax", [QT, 1])
        ci = m.sb("o_ci", [QT, 1], I32)
        cf = m.sb("o_cf", [QT, 1])
        tail = m.sb("o_tail", [1, 4], I32)
        ctf = m.sb("o_ctf", [1, QT + 1])
        pR = m.ps("o_pR", [P, 512])
        pTt = m.ps("o_pTt", [P, 512])
        pD = m.ps("o_pD", [QT, Q])
        pC = m.ps("o_pC", [1, 64])

        r_in = m.sem("o_r_in"); vch = m.sem("o_vch"); hot_ok = m.sem("o_hot_ok"); mm_ok = m.sem("o_mm_ok"); taken = m.sem("o_taken")
        ready = m.sem("o_ready"); sent = [m.sem(f"o_sent{r}") for r in range(R)]; pads = m.sem("o_pads"); pt_in = m.sem("o_pt_in")
        deg_ok = m.sem("o_deg_ok"); dT_ok = m.sem("o_dT_ok"); cnt_ok = m.sem("o_cnt_ok"); pre_ok = m.sem("o_pre_ok"); pace = m.sem("o_pace")
        iota_ok = m.sem("o_iota_ok"); all_sent = m.sem("o_all_sent")
        cols = [(a, min(a + 8, NT)) for a in range(0, NT, 8)]

        with nc.Block() as block:
            @block.sync
            def _(sp):
                sp.dma_start(rpi[:], dr["rp"][:, 0:N].rearrange("o (p t) -> (o p) t", t=NT)).then_inc(r_in, 16)
                sp.dma_start(nxt[:], dr["rp"][:, 1:N + 1].rearrange("o (p t) -> (o p) t", t=NT)).then_inc(r_in, 16)
                sp.dma_start(dr["noderec"][N:NPAD, :], K["padrec"][:]).then_inc(pads, 16)
                sp.wait_ge(pads, 16)
                for r in range(R):
                    sp.wait_ge(sent[r], 16 * (NT // R))
                sp.dma_start(K["pt"][:], dr["noderec"].rearrange("(t q) c -> q t c", q=Q)).then_inc(pt_in, 16)
                sp.wait_ge(pt_in, 16)

            @block.gpsimd
            def _(pool):
                pool.iota(rec[:, :, 0], pattern=[[1, NT]], base=0, channel_multiplier=NT).then_inc(iota_ok, 1)

                def scatter(u, r):
                    pool.wait_ge(ready, u * R + (r + 1))
                    pool.sem_inc(pace, 1)
                    pool.indirect_dma_start(out=dr["noderec"], out_offset=bass.IndirectOffsetOnAxis(ap=idx[r][:, 0:1], axis=0),
                                            in_=srow[r][:], in_offset=None).then_inc(sent[r], 16)
                with pool.Fori(0, NT // R) as u:
                    for r in range(R):
                        scatter(u, r)

            @block.vector
            def _(dve):
                v = nc.vector
                ch = Chain(dve, vch)
                v.memset(zero[:], 0.0)
                dve.wait_ge(r_in, 32)
                dve.wait_ge(iota_ok, 1)
                ch.link(v.tensor_tensor(deg[:], nxt[:], rpi[:], ALU.subtract))
                v.tensor_copy(rec[:, :, 1], rpi[:])
                v.tensor_copy(rec[:, :, 2], deg[:])
                ch.link(v.tensor_copy(rec[:, :, 3], deg[:]))
                ch.link(v.tensor_scalar(bkt[:], deg[:], float(NB - 1), None, ALU.min))
                v.tensor_tensor(hot[:], over(bkt[:], 2, NB), over(K["iota64"][0:P, :], 1, NT), ALU.is_equal).then_inc(hot_ok, 1)
                for j, (a, b) in enumerate(cols):
                    w = (b - a) * NB
                    dve.wait_ge(mm_ok, j + 1)
                    v.tensor_copy(rank[:, a:b, :].rearrange("p t b -> p (t b)"), pR[:, 0:w])
                    v.tensor_copy(tot[:, :, a:b].rearrange("p b t -> p t b"), pTt[:, 0:w].rearrange("p (t b) -> p t b", b=NB)).then_inc(taken, 1)
                dve.wait_ge(taken, len(cols))
                flat = "p b t -> p (b t)"
                ch.link(v.tensor_tensor_scan(exc[:].rearrange(flat), tot[:].rearrange(flat), zero[:], 0.0, ALU.add, ALU.add))
                ch.link(v.tensor_tensor(exc[:].rearrange(flat), exc[:].rearrange(flat), tot[:].rearrange(flat), ALU.subtract))
                ch.link(v.tensor_tensor(rank[:], rank[:], exc[:].rearrange("p b t -> p t b"), ALU.add))
                ch.link(v.tensor_tensor(rank[:], rank[:], hot[:], ALU.mult))
                ch.link(v.reduce_sum(posf[:], rank[:], axis=AX))
                ch.link(v.tensor_copy(pos[:], posf[:]))

                def stage(u, first):
                    for r in range(R):
                        t = u * R + r
                        if not first:
                            dve.wait_ge(sent[r], 16 * u)
                            dve.sem_inc(pace, 1)
                        v.tensor_copy(srow[r][:], rec[:, bass.ds(t, 1), :].rearrange("p a c -> p (a c)"))
                        v.tensor_copy(idx[r][:], pos[:, bass.ds(t, 1)]).then_inc(ready, 1)
                peeled(dve, NT // R, stage)
                dve.wait_ge(pt_in, 16)
                v.tensor_copy(K["rp"][:], K["pt"][:, :, 1])
                v.tensor_copy(K["deg"][:], K["pt"][:, :, 2]).then_inc(deg_ok, 1)
                dve.wait_ge(dT_ok, 1)
                ch.link(v.reduce_max(dmax[:], pD[:], axis=AX))
                ch.link(v.tensor_scalar(ci[:], dmax[:], float(C - 1), None, ALU.add))
                ch.link(v.tensor_scalar(ci[:], ci[:], 2, None, ALU.arith_shift_right))
                ch.link(v.tensor_copy(cf[:], ci[:]))
                v.tensor_scalar(cf[:], cf[:], 2.0, None, ALU.max).then_inc(cnt_ok, 1)
                dve.wait_ge(pre_ok, 1)
                v.tensor_copy(K["ct"][:, 0:QT], pC[:, 0:QT])
                ch.link(v.tensor_scalar(tail[:, 0:1], pC[:, QT:QT + 1], 3.0, None, ALU.add))
                ch.link(v.tensor_scalar(tail[:, 1:2], tail[:, 0:1], 2, None, ALU.arith_shift_right))
                v.tensor_scalar(K["ct"][:, QT + 1:QT + 2], tail[:, 1:2], -2.0, None, ALU.add)
                ch.link(v.tensor_scalar(K["ct"][:, QT:QT + 1], tail[:, 1:2], 4.0, None, ALU.mult))

            @block.tensor
            def _(pe):
                t_ = nc.tensor
                pe.wait_ge(hot_ok, 1)
                for j, (a, b) in enumerate(cols):
                    w = (b - a) * NB
                    h = hot[:, a:b, :].rearrange("p t b -> p (t b)")
                    if j:
                        pe.wait_ge(taken, j)
                    t_.matmul(pR[:, 0:w], K["tri"][0:P, 0:P], h, start=True, stop=True)
                    t_.matmul(pTt[:, 0:w], K["ones"][0:P, 0:P], h, start=True, stop=True).then_inc(mm_ok, 1)
                pe.wait_ge(deg_ok, 1)
                t_.transpose(pD[:], K["deg"][:], K["ident"][:]).then_inc(dT_ok, 1)
                pe.wait_ge(cnt_ok, 1)
                t_.matmul(pC[0:1, 0:QT + 1], cf[:], K["tri"][0:QT, 0:QT + 1], start=True, stop=True).then_inc(pre_ok, 1)


def groups(eng, K):
    return eng.value_load(K["ct"][0:1, QT + 1:QT + 2], min_val=1, max_val=CMAX // 4 - 3)


def slots(nc, K, ins, dr):
    with ExitStack() as stack:
        m = Mem(nc, stack)
        R = 4
        idx = m.sb("s_idx", [Q, R], I32)
        cur = m.sb("s_cur", [Q, 1])
        land = m.sb("s_land", [Q, R, REC])
        vch = m.sem("s_vch"); tch = m.sem("s_tch"); ready = m.sem("s_ready"); free = m.sem("s_free")
        got = [m.sem(f"s_got{r}") for r in range(R)]; put = [m.sem(f"s_put{r}") for r in range(R)]; pace = m.sem("s_pace")
        with nc.Block() as block:
            @block.sync
            def _(sp):
                n4 = groups(sp, K) + 2
                with sp.Fori(0, n4) as u:
                    for r in range(R):
                        sp.wait_ge(got[r], 16 * u + 16)
                        sp.sem_inc(free, 1)
                        sp.dma_start(dr["slots"][bass.ds(4 * u + r, 1), :, :].rearrange("a q c -> (a q) c"), land[:, r, :]).then_inc(put[r], 16)
                for r in range(R):
                    sp.wait_ge(put[r], 16 * n4)
                    sp.sem_inc(pace, 1)

            @block.gpsimd
            def _(pool):
                n4 = groups(pool, K) + 2

                def gather(u, first):
                    for r in range(R):
                        pool.wait_ge(ready, 4 * u + (r + 1))
                        pool.sem_inc(pace, 1)
                        if not first:
                            pool.wait_ge(put[r], 16 * u)
                            pool.sem_inc(pace, 1)
                        pool.indirect_dma_start(out=land[:, r, :], out_offset=None, in_=dr["rec"],
                                                in_offset=bass.IndirectOffsetOnAxis(ap=idx[:, r:r + 1], axis=0)
                                                ).then_inc(got[r], 16)
                peeled(pool, n4, gather)

            @block.vector
            def _(dve):
                v = nc.vector
                dve.sem_inc(free, R)
                dve.sem_inc(tch, 1)
                with dve.Fori(0, QT) as t:
                    lo = dve.value_load(K["ct"][0:1, bass.ds(t, 1)], min_val=0, max_val=CMAX)
                    hi = dve.value_load(K["ct"][0:1, bass.ds(t + 1, 1)], min_val=2, max_val=CMAX)
                    dve.wait_ge(tch, t + lo + 1)
                    dve.sem_inc(pace, 1)
                    v.tensor_copy(cur[:], K["rp"][:, bass.ds(t, 1)]).then_inc(tch, 1)
                    with dve.Fori(lo, hi) as i:
                        dve.wait_ge(tch, t + i + 2)
                        dve.sem_inc(pace, 1)
                        dve.wait_ge(free, i + 1)
                        dve.sem_inc(pace, 1)
                        v.tensor_scalar(idx[:, bass.ds(i % R, 1)], cur[:], float(E - 1), None, ALU.min).then_inc(ready, 1)
                        v.tensor_scalar(cur[:], cur[:], float(C), None, ALU.add).then_inc(tch, 1)


def graph(nc, K, ins, dr, layer):
    first_layer = layer == 0
    rows_d, agg_d = dr[f"rows{layer}"], dr[f"agg{layer}"]
    L = f"g{layer}_"
    with ExitStack() as stack:
        m = Mem(nc, stack)
        R = 4
        HR = 4
        DW = RW if first_layer else H
        dall = m.sb(L + "dall", [Q, QT, DW if first_layer else D])
        sdst = m.sb(L + "sdst", [Q, QT, H])
        nidx = [m.sb(f"{L}nidx{r}", [Q, 1], I32) for r in range(HR)]
        nrow = m.sb(L + "nrow", [Q, HR, DW])
        orow = m.sb(L + "orow", [Q, HR, D])
        recs = m.sb(L + "recs", [Q, R, REC])
        rows = m.sb(L + "rows", [Q, R, C, RW])
        msg = m.sb(L + "msg", [Q, 2, C, H * VW])
        prod = m.sb(L + "prod", [Q, C * D])
        al = m.sb(L + "al", [Q, C * H])
        mask = m.sb(L + "mask", [Q, C])
        left = m.sb(L + "left", [Q, 1])
        mx = m.sb(L + "mx", [Q, H])
        mn = m.sb(L + "mn", [Q, H])
        cm = m.sb(L + "cm", [Q, H])
        dd = m.sb(L + "dd", [Q, 2, (C + 1) * H])
        pp = m.sb(L + "pp", [Q, 2, (C + 1) * H])
        acc = m.sb(L + "acc", [Q, H * VW])
        den = m.sb(L + "den", [Q, H])
        pA = m.ps(L + "pA", [Q, 2, 512])
        if first_layer:
            ew = m.sb(L + "ew", [REC + 1, C, D])
            recT = m.sb(L + "recT", [REC + 1, 2, Q])
            pE = m.ps(L + "pE", [Q, C * D])
            pRT = m.ps(L + "pRT", [REC, 2, 512])

        S = lambda n: m.sem(L + n)
        nready = S("nready"); ngot = [S(f"ngot{r}") for r in range(HR)]
        rec_in = [S(f"rec_in{r}") for r in range(R)]; rows_in = [S(f"rows_in{r}") for r in range(R)]
        rows_ok = S("rows_ok"); w_in = S("w_in"); w_zero = S("w_zero"); pace = S("pace"); vch = S("vch"); tch = S("tch"); cch = S("cch")
        recT_ps = S("recT_ps"); recT_ok = S("recT_ok"); enc_ok = S("enc_ok"); enc_free = S("enc_free")
        dd_ok = S("dd_ok"); pp_ok = S("pp_ok"); msg_ok = S("msg_ok"); agg_ok = S("agg_ok")
        oready = S("oready"); oput = [S(f"oput{r}") for r in range(HR)]
        NG = QT // HR
        TAIL = QT - NG * HR

        with nc.Block() as block:
            src_d = rows_d if first_layer else dr["sv1"]

            @block.gpsimd
            def _(pool):
                def gather(u, r):
                    pool.wait_ge(nready, u * HR + (r + 1))
                    pool.sem_inc(pace, 1)
                    pool.indirect_dma_start(out=nrow[:, r, :], out_offset=None, in_=src_d,
                                            in_offset=bass.IndirectOffsetOnAxis(ap=nidx[r][:, 0:1], axis=0)
                                            ).then_inc(ngot[r], 16)
                with pool.Fori(0, NG) as u:
                    for r in range(HR):
                        gather(u, r)
                for r in range(TAIL):
                    gather(NG, r)

            @block.vector
            def _(dve):
                v = nc.vector

                def put_index(t, r):
                    v.tensor_copy(nidx[r][:], K["pt"][:, bass.ds(t, 1), 0]).then_inc(nready, 1)

                def keep(u, r, more):
                    t = u * HR + r
                    dve.wait_ge(ngot[r], 16 * u + 16)
                    dve.sem_inc(pace, 1)
                    row = nrow[:, r:r + 1, :]
                    if first_layer:
                        v.tensor_copy(dall[:, bass.ds(t, 1), :], row)
                    else:
                        v.tensor_copy(sdst[:, bass.ds(t, 1), :], row)
                    if more:
                        put_index(t + HR, r)
                for r in range(HR):
                    put_index(r, r)
                with dve.Fori(0, NG - 1) as u:
                    for r in range(HR):
                        keep(u, r, True)
                for r in range(HR):
                    keep(NG - 1, r, r < TAIL)
                for r in range(TAIL):
                    keep(NG, r, False)
                if first_layer:
                    Chain(dve, vch).link(v.memset(cm[:], 0.0))
                    v.tensor_copy(sdst[:], dall[:, :, H * VW + H:RW])

        with nc.Block() as block:
            @block.sync
            def _(sp):
                n2 = groups(sp, K)
                if first_layer:
                    sp.wait_ge(w_zero, 1)
                    for j in range(C):
                        sp.dma_start(ew[C + 3 * j:C + 3 * j + 3, j, :], ins["L0_gnn_edge_WT"]).then_inc(w_in, 16)
                        sp.dma_start(ew[REC:REC + 1, j, :], ins["L0_gnn_edge_b"].unsqueeze(0)).then_inc(w_in, 16)

                def load(u, r):
                    sp.dma_start(recs[:, r, :], dr["slots"][bass.ds(4 * u + r, 1), :, :].rearrange("a q c -> (a q) c")).then_inc(rec_in[r], 16)

                def relay(u, r):
                    sp.wait_ge(rows_in[r], 16 * C * (u + 1))
                    sp.sem_inc(rows_ok, 1)
                for r in range(R):
                    load(0, r)
                with sp.Fori(0, n2 + 1) as u:
                    for r in range(R):
                        relay(u, r)
                        if first_layer:
                            sp.wait_ge(recT_ps, 4 * u + (r + 1))
                            sp.sem_inc(pace, 1)
                        load(u + 1, r)
                for r in range(R):
                    relay(n2 + 1, r)

            @block.gpsimd
            def _(pool):
                n2 = groups(pool, K)

                def gather(u, first):
                    for r in range(R):
                        pool.wait_ge(rec_in[r], 16 * u + 16)
                        pool.sem_inc(pace, 1)
                        if not first:
                            pool.wait_ge(msg_ok, 4 * (u - 1) + (r + 1))
                            pool.sem_inc(pace, 1)
                        for j in range(C):
                            pool.indirect_dma_start(out=rows[:, r, j, :], out_offset=None, in_=rows_d,
                                                    in_offset=bass.IndirectOffsetOnAxis(ap=recs[:, r, j:j + 1].bitcast(I32), axis=0)
                                                    ).then_inc(rows_in[r], 16)
                peeled(pool, n2 + 2, gather)

            @block.tensor
            def _(pe):
                t_ = nc.tensor
                n2 = groups(pe, K)

                def transpose(u, r):
                    pe.wait_ge(rec_in[r % R], 16 * u + 16)
                    t_.transpose(pRT[:, r % 2, 0:Q], recs[:, r % R, :], K["ident"][:]).then_inc(recT_ps, 1)

                def aggregate(u, r):
                    pe.wait_ge(msg_ok, 4 * u + (r + 1))
                    for j in range(C):
                        last = t_.matmul(pA[:, r % 2, 0:H * VW], K["ident"][:], msg[:, r % 2, j, :], start=(j == 0), stop=(j == C - 1))
                    last.then_inc(agg_ok, 1)

                def group(u, first, last_group):
                    for r in range(R):
                        i = 4 * u + r
                        if first_layer:
                            if r < R - 1:
                                transpose(u, r + 1)
                            elif not last_group:
                                transpose(u + 1, 0)
                            pe.wait_ge(recT_ok, i + 1)
                            if not (first and r == 0):
                                pe.wait_ge(enc_free, i)
                            for half in range(2):
                                last = t_.matmul(pE[:, half * 512:(half + 1) * 512], recT[:, r % 2, :],
                                                 ew[:].rearrange("p c d -> p (c d)")[:, half * 512:(half + 1) * 512], start=True, stop=True)
                            last.then_inc(enc_ok, 1)
                        if r > 0:
                            aggregate(u, r - 1)
                        elif not first:
                            aggregate(u - 1, R - 1)
                if first_layer:
                    pe.wait_ge(w_in, 32 * C)
                    transpose(0, 0)
                group(0, True, False)
                with pe.Fori(1, n2 + 1) as u:
                    group(u, False, False)
                group(n2 + 1, False, True)
                aggregate(n2 + 1, R - 1)

            @block.scalar
            def _(act):
                s = nc.scalar
                n2 = groups(act, K)

                def record(u, r):
                    act.wait_ge(recT_ps, 4 * u + (r + 1))
                    if not (isinstance(u, int) and 4 * u + r < 2):
                        act.sem_inc(pace, 1)
                        act.wait_ge(enc_ok, 4 * u + (r - 1))
                    s.activation(recT[0:REC, r % 2, :], pRT[:, r % 2, 0:Q], ACT.Copy).then_inc(recT_ok, 1)

                def group(u, last_group):
                    for r in range(R):
                        if first_layer:
                            if r < R - 1:
                                record(u, r + 1)
                            elif not last_group:
                                record(u + 1, 0)
                        act.wait_ge(dd_ok, 4 * u + (r + 1))
                        s.activation(pp[:, r % 2, :], dd[:, r % 2, :], ACT.Exp).then_inc(pp_ok, 1)
                if first_layer:
                    act.wait_ge(w_zero, 2)
                    record(0, 0)
                group(0, False)
                with act.Fori(1, n2 + 1) as u:
                    group(u, False)
                group(n2 + 1, True)

            @block.vector
            def _(dve):
                v = nc.vector
                if first_layer:
                    v.memset(ew[:], 0.0).then_inc(w_zero, 1)
                    v.memset(recT[:], 1.0).then_inc(w_zero, 1)
                NL = 13 if first_layer else 11
                bch = lambda ap: ap.rearrange("p (c h) -> p c h", c=C)
                iota = K["iota64"][:, 0:C]

                def update(i, ch):
                    b = bass.ds(i % 2, 1)
                    a3 = acc[:].rearrange("p (h c) -> p h c", h=H)
                    sc = over(pp[:, b, C * H:].rearrange("p a h -> p (a h)"), 2, VW)
                    ch.link(v.tensor_tensor(a3, a3, sc, ALU.mult))
                    dve.wait_ge(agg_ok, i + 1)
                    dve.sem_inc(pace, 1)
                    ch.link(v.tensor_tensor(acc[:], acc[:], pA[:, b, 0:H * VW].rearrange("p a c -> p (a c)"), ALU.add))

                def chunk(t, i, peel):
                    b2, b4 = bass.ds(i % 2, 1), bass.ds(i % R, 1)
                    ch = Chain(dve, cch, i * NL)
                    dt = dall[:, bass.ds(t, 1), 0:H * VW] if first_layer else None
                    row4 = rows[:, b4, :, :].rearrange("p a c w -> p (a c) w")
                    a3 = bch(al[:])
                    ch.link(v.tensor_scalar(mask[:], iota, left[:], -BIG, ALU.is_ge, ALU.mult), wait=False)
                    if first_layer:
                        dve.wait_ge(enc_ok, i + 1)
                        dve.sem_inc(pace, 1)
                        for j in range(C):
                            dst = dt.rearrange("p a (h c) -> p (a h) c", h=H)[:, :, 0:HD]
                            sl = slice(j * D, (j + 1) * D)
                            last = v.scalar_tensor_tensor(prod[:, sl].rearrange("p (h c) -> p h c", h=H),
                                                          pE[:, sl].rearrange("p (h c) -> p h c", h=H), 0.0, dst, ALU.max, ALU.mult)
                        last.then_inc(enc_free, 1)
                        ch.link(v.tensor_scalar(left[:], left[:], -float(C), None, ALU.add))
                        ch.link(v.reduce_sum(al[:], prod[:].rearrange("p (g c) -> p g c", c=HD), axis=AX))
                        dve.wait_ge(rows_ok, i + 1)
                        dve.sem_inc(pace, 1)
                        ch.link(v.tensor_tensor(a3, a3, row4[:, :, H * VW:H * VW + H], ALU.add))
                        ch.link(v.tensor_tensor(a3, a3, over(sdst[:, bass.ds(t, 1), :].rearrange("p a h -> p (a h)"), 1, C), ALU.add))
                    else:
                        ch.link(v.tensor_scalar(left[:], left[:], -float(C), None, ALU.add))
                        dve.wait_ge(rows_ok, i + 1)
                        dve.sem_inc(pace, 1)
                        ch.link(v.tensor_tensor(a3, row4[:, :, H * VW:H * VW + H], over(sdst[:, bass.ds(t, 1), :].rearrange("p a h -> p (a h)"), 1, C), ALU.add))
                    ch.link(v.scalar_tensor_tensor(al[:], al[:], 0.2, al[:], ALU.mult, ALU.max))
                    ch.link(v.tensor_tensor(a3, a3, over(mask[:], 2, H), ALU.add))
                    ch.link(v.reduce_max(cm[:], a3.rearrange("p c h -> p h c"), axis=AX))
                    ch.link(v.tensor_tensor(mn[:], mx[:], cm[:], ALU.max))
                    ddb = dd[:, b2, :].rearrange("p a c -> p (a c)")
                    ch.link(v.tensor_tensor(ddb[:, C * H:], mx[:], mn[:], ALU.subtract), wait=False)
                    v.tensor_tensor(bch(ddb[:, 0:C * H]), a3, over(mn[:], 1, C), ALU.subtract).then_inc(dd_ok, 1)
                    if peel:
                        ch.n += 2
                        dve.sem_inc(cch, 2)
                        ch.wait()
                    else:
                        update(i - 1, ch)
                    ch.link(v.tensor_copy(mx[:], mn[:]))
                    assert ch.n == NL, ch.n
                    dve.wait_ge(pp_ok, i + 1)
                    dve.sem_inc(pace, 1)
                    pv = pp[:, b2, 0:C * H].rearrange("p a (c h) -> p (a c) h", c=C)
                    v.tensor_tensor(msg[:, b2, :, :].rearrange("p a c (h w) -> p (a c) h w", h=H),
                                    row4[:, :, 0:H * VW].rearrange("p c (h w) -> p c h w", h=H), over(pv, 3, VW), ALU.mult).then_inc(msg_ok, 1)

                TL = 7
                with dve.Fori(0, QT) as t:
                    lo = dve.value_load(K["ct"][0:1, bass.ds(t, 1)], min_val=0, max_val=CMAX - 2)
                    hi = dve.value_load(K["ct"][0:1, bass.ds(t + 1, 1)], min_val=2, max_val=CMAX)
                    tc = Chain(dve, tch, t * TL)
                    v.memset(mx[:], -BIG / 10)
                    v.memset(acc[:], 0.0)
                    tc.link(v.tensor_copy(left[:], K["deg"][:, bass.ds(t, 1)]))
                    chunk(t, lo, True)
                    with dve.Fori(lo + 1, hi) as i:
                        chunk(t, i, False)
                    update(hi - 1, tc)
                    a3 = acc[:].rearrange("p (h c) -> p h c", h=H)
                    tc.link(v.tensor_scalar(den[:], a3[:, :, HD], 1e-10, None, ALU.max))
                    tc.link(v.reciprocal(den[:], den[:]))
                    tc.link(v.tensor_tensor(dall[:, bass.ds(t, 1), 0:D].rearrange("p a (h c) -> p (a h) c", h=H),
                                            a3[:, :, 0:HD], over(den[:], 2, HD), ALU.mult))
                    tc.link(v.memset(cm[:], 0.0))

        with nc.Block() as block:
            @block.gpsimd
            def _(pool):
                def scatter(u, r):
                    pool.wait_ge(oready, u * HR + (r + 1))
                    pool.sem_inc(pace, 1)
                    pool.indirect_dma_start(out=agg_d, out_offset=bass.IndirectOffsetOnAxis(ap=nidx[r][:, 0:1], axis=0),
                                            in_=orow[:, r, :], in_offset=None).then_inc(oput[r], 16)
                with pool.Fori(0, NG) as u:
                    for r in range(HR):
                        scatter(u, r)
                for r in range(TAIL):
                    scatter(NG, r)
                for r in range(HR):
                    pool.wait_ge(oput[r], 16 * (NG + (r < TAIL)))

            @block.vector
            def _(dve):
                v = nc.vector

                def stage(u, r, first):
                    t = u * HR + r
                    if not first:
                        dve.wait_ge(oput[r], 16 * u)
                        dve.sem_inc(pace, 1)
                    v.tensor_copy(orow[:, r:r + 1, :], dall[:, bass.ds(t, 1), 0:D])
                    v.tensor_copy(nidx[r][:], K["pt"][:, bass.ds(t, 1), 0]).then_inc(oready, 1)

                def group(u, first):
                    for r in range(HR):
                        stage(u, r, first)
                peeled(dve, NG, group)
                for r in range(TAIL):
                    stage(NG, r, False)


def paired(eng, n, body):
    body(0, True, False)
    with eng.Fori(1, n - 1) as u:
        body(u, False, False)
    body(n - 1, False, True)


def slice_ffn(nc, K, ins, dr):
    with ExitStack() as stack:
        m = Mem(nc, stack)
        S = lambda n: m.sem("f_" + n)
        INNER = FH * G
        NU = NT // 2
        x1 = m.sb("f_x1", [P, NT, D])
        swT = m.sb("f_swT", [128, 4, NT, P])
        bias = m.sb("f_bias", [P, D])
        norm = Norm(m, "f")
        wfx = m.sb("f_wfx", [128, 2, INNER])
        wout = m.sb("f_wout", [G, FH, D])
        wc = m.sb("f_wc", [128, 2, INNER])
        bc = m.sb("f_bc", [P, INNER])
        mm = m.sb("f_mm", [128, 4, D])
        bfx = m.sb("f_bfx", [1, INNER])
        wqkv = m.sb("f_wqkv", [G, 3, G])
        flat = lambda ap: ap.rearrange("p a c -> p (a c)")

        with ExitStack() as s2:
            m2 = Mem(nc, s2)
            T = lambda n: m2.sem("f0_" + n)
            agg = m2.sb("f0_agg", [P, 2, 5, D])
            wxT = m2.sb("f0_wxT", [G, FH, D])
            wsl = m2.sb("f0_wsl", [G, G])
            bx = m2.sb("f0_bx", [G, FH])
            bxb = m2.sb("f0_bxb", [G, FH, P])
            bsl = m2.sb("f0_bsl", [P, G])
            temp = m2.sb("f0_temp", [128, FH])
            pW = [m2.ps(f"f0_pW{k}", [128, 512]) for k in range(2)]
            pB = m2.ps("f0_pB", [P, 512])
            x_in = T("x_in"); a_in = [T("a_in0"), T("a_in1")]; w_in = T("w_in"); a_used = T("a_used")
            bxb_ok = T("bxb_ok"); w_ok = T("w_ok"); vch = T("vch"); stats = T("stats"); sq = T("sq"); done = T("done")
            with nc.Block() as block:
                @block.sync
                def _(sp):
                    sp.dma_start(x1[:], ins["x"].rearrange("(p t) c -> p t c", t=NT)).then_inc(x_in, 16)
                    sp.dma_start(bias[:], ins["L0_gnn_bias"].unsqueeze(0).broadcast_to([P, D])).then_inc(x_in, 16)
                    av = dr["agg0"][0:N, :].rearrange("(p t) c -> p t c", t=NT)
                    for g in range(NT // 5):
                        if g >= 2:
                            sp.wait_ge(a_used, g - 1)
                        sp.dma_start(agg[:, g % 2, :, :], av[:, 5 * g:5 * g + 5, :]).then_inc(a_in[g % 2], 16)

                @block.scalar
                def _(act):
                    act.dma_start(wxT[:], ins["L0_ffn_WxT"].rearrange("(h c) i -> c h i", c=G)).then_inc(w_in, 16)
                    act.dma_start(wsl[:], ins["L0_ffn_W_slice"]).then_inc(w_in, 16)
                    act.dma_start(bx[:], ins["L0_ffn_b_x"].rearrange("(h c) -> c h", c=G), allow_slow_non_contiguous=True).then_inc(w_in, 16)
                    act.dma_start(bsl[:], ins["L0_ffn_b_slice"].unsqueeze(0).broadcast_to([P, G])).then_inc(w_in, 16)
                    act.dma_start(temp[:], ins["L0_ffn_temperature"].rearrange("a h b c -> a (h b c)").broadcast_to([128, FH])).then_inc(w_in, 16)
                    act.dma_start(wfx[:], ins["L0_ffn_W_fx"].rearrange("(k p) o -> p k o", p=128)).then_inc(w_in, 16)
                    act.dma_start(wout[:], ins["L0_ffn_W_out"].rearrange("(h c) o -> c h o", c=G)).then_inc(w_in, 16)
                    act.dma_start(bfx[:], ins["L0_ffn_b_fx"].unsqueeze(0)).then_inc(w_in, 16)
                    for q, nm in enumerate("qkv"):
                        act.dma_start(wqkv[:, q, :], ins["L0_ffn_W_" + nm]).then_inc(w_in, 16)
                    act.wait_ge(w_in, 176)
                    act.wait_ge(stats, 1)
                    nc.scalar.activation(norm.rstd[:], norm.rstd[:], ACT.Sqrt).then_inc(sq, 1)

                @block.tensor
                def _(pe):
                    t_ = nc.tensor
                    pe.wait_ge(bxb_ok, 1)
                    for h in range(FH):
                        c = slice(h * G, (h + 1) * G)
                        for k in range(2):
                            t_.matmul(pW[k][:, c], wxT[:, h, k * 128:(k + 1) * 128], wsl[:], start=True, stop=True)
                        last = t_.matmul(pB[:, c], bxb[:, h, :], wsl[:], start=True, stop=True)
                    last.then_inc(w_ok, 1)

                @block.vector
                def _(dve):
                    v = nc.vector
                    ch = Chain(dve, vch)
                    dve.wait_ge(w_in, 176)
                    v.tensor_copy(bxb[:], over(bx[:], 2, P)).then_inc(bxb_ok, 1)
                    ch.link(v.tensor_scalar(temp[:], temp[:], 0.1, 5.0, ALU.max, ALU.min))
                    ch.link(v.reciprocal(temp[:], temp[:]))
                    dve.wait_ge(w_ok, 1)
                    g3 = lambda ap: ap.rearrange("p (h g) -> p h g", h=FH)
                    for k in range(2):
                        v.tensor_tensor(g3(wc[:, k, :]), g3(pW[k][:]), over(temp[:], 2, G), ALU.mult)
                    ch.link(v.tensor_tensor(g3(bc[:]), g3(pB[:]), over(bsl[:], 1, FH), ALU.add))
                    ch.link(v.tensor_tensor(g3(bc[:]), g3(bc[:]), over(temp[0:P, :], 2, G), ALU.mult))
                    dve.wait_ge(x_in, 32)
                    for g in range(NT // 5):
                        dve.wait_ge(a_in[g % 2], 16 * (g // 2 + 1))
                        xs = x1[:, 5 * g:5 * g + 5, :]
                        ch.link(v.tensor_tensor(xs, xs, over(bias[:], 1, 5), ALU.add))
                        v.tensor_tensor(xs, xs, agg[:, g % 2, :, :], ALU.add).then_inc(a_used, 1)
                    dve.wait_ge(a_used, NT // 5)
                    with dve.Fori(0, NT) as t:
                        norm.tile(v, t, x1[:, bass.ds(t, 1), :])
                    ch.link(v.memset(norm.a[:], 0.0))
                    norm.variance(v, ch, stats)
                    dve.wait_ge(sq, 1)
                    norm.scales(v, ch, done)

        st = m.sb("f_sums", [128, 4, D + 1])
        with ExitStack() as s2:
            m2 = Mem(nc, s2)
            T = lambda n: m2.sem("f1_" + n)
            xn = m2.sb("f1_xn", [P, 2, D + 1])
            xnT = m2.sb("f1_xnT", [128, 2, 2, P])
            lg = m2.sb("f1_lg", [P, 2, INNER])
            sw = m2.sb("f1_sw", [P, 2, INNER])
            red = m2.sb("f1_red", [P, 2, FH])
            pT = m2.ps("f1_pT", [128, 2, 2, 128])
            pL = [m2.ps(f"f1_pL{b}", [P, 512]) for b in range(2)]
            pS = m2.ps("f1_pS", [128, 4, 128])
            pTok = [m2.ps(f"f1_pTok{k}", [128, 512]) for k in range(4)]
            one = T("one"); xn_ok = T("xn_ok"); t_ok = T("t_ok"); xnT_ok = T("xnT_ok"); lg_ok = T("lg_ok"); sub_ok = T("sub_ok")
            exp_ok = T("exp_ok"); sw_ok = T("sw_ok"); s_ok = T("s_ok"); swT_ok = T("swT_ok"); vch = T("vch"); pace = T("pace"); tok = T("tok")
            g3 = lambda ap: ap.rearrange("p (h g) -> p h g", h=FH)
            with nc.Block() as block:
                @block.tensor
                def _(pe):
                    t_ = nc.tensor

                    def logits(t, b):
                        pe.wait_ge(xn_ok, t + 1)
                        for k in range(2):
                            last = t_.transpose(pT[:, b, k, 0:P], xn[:, b, k * 128:(k + 1) * 128], K["ident"][0:P, 0:P])
                        last.then_inc(t_ok, 1)
                        pe.wait_ge(xnT_ok, t + 1)
                        for k in range(2):
                            last = t_.matmul(pL[b][:], xnT[:, b, k, :], wc[:, k, :], start=(k == 0), stop=(k == 1))
                        last.then_inc(lg_ok, 1)

                    def group(u, first, last_group):
                        for b in range(2):
                            t = 2 * u + b
                            if b == 0 or not last_group:
                                logits(t + 1, 1 - b)
                            pe.wait_ge(sw_ok, t + 1)
                            for k in range(4):
                                t_.matmul(pTok[k][:, 0:D + 1], sw[:, b, k * 128:(k + 1) * 128], xn[:, b, :],
                                          start=first and b == 0, stop=last_group and b == 1, skip_group_check=True)
                            if not (first and b == 0):
                                pe.wait_ge(swT_ok, t)
                            for k in range(4):
                                last = t_.transpose(pS[:, k, 0:P], sw[:, b, k * 128:(k + 1) * 128], K["ident"][0:P, 0:P])
                            last.then_inc(s_ok, 1)
                    logits(0, 0)
                    paired(pe, NU, group)

                @block.scalar
                def _(act):
                    s = nc.scalar

                    def normed(t, b, early):
                        tc = bass.ds(t, 1)
                        if not early:
                            act.wait_ge(s_ok, t - 1)
                            act.sem_inc(pace, 1)
                        s.activation(xn[:, b, 0:D], flat(x1[:, tc, :]), ACT.Identity, bias=norm.nbias[:, tc],
                                     scale=norm.rstd[:, tc]).then_inc(xn_ok, 1)
                        act.wait_ge(t_ok, t + 1)
                        s.activation(xnT[:, b, :, :], pT[:, b, :, 0:P], ACT.Copy).then_inc(xnT_ok, 1)

                    def keep(t):
                        act.wait_ge(s_ok, t + 1)
                        act.sem_inc(pace, 1)
                        s.activation(swT[:, :, bass.ds(t, 1), :].rearrange("p k a c -> p (k a) c"), pS[:, :, 0:P], ACT.Copy).then_inc(swT_ok, 1)

                    def group(u, first, last_group):
                        for b in range(2):
                            t = 2 * u + b
                            if not (first and b == 0):
                                keep(t - 1)
                            if b == 0 or not last_group:
                                normed(t + 1, 1 - b, first and b == 0)
                            act.wait_ge(sub_ok, t + 1)
                            s.activation(lg[:, b, :], lg[:, b, :], ACT.Exp).then_inc(exp_ok, 1)
                    act.wait_ge(one, 1)
                    normed(0, 0, True)
                    paired(act, NU, group)
                    keep(NT - 1)

                @block.vector
                def _(dve):
                    v = nc.vector
                    v.memset(xn[:, :, D:D + 1], 1.0).then_inc(one, 1)
                    NL = 6

                    def tile(u, b, early):
                        t = 2 * u + b
                        ch = Chain(dve, vch, NL * t)
                        dve.wait_ge(lg_ok, t + 1)
                        dve.sem_inc(pace, 1)
                        ch.link(v.tensor_tensor(lg[:, b, :], pL[b][:], bc[:], ALU.add))
                        ch.link(v.reduce_max(red[:, b, :], g3(lg[:, b, :]), axis=AX))
                        ch.link(v.tensor_tensor(g3(lg[:, b, :]), g3(lg[:, b, :]), over(red[:, b, :], 2, G), ALU.subtract), wait=False)
                        ch.wait()
                        dve.sem_inc(sub_ok, 1)
                        dve.wait_ge(exp_ok, t + 1)
                        dve.sem_inc(pace, 1)
                        ch.link(v.reduce_sum(red[:, b, :], g3(lg[:, b, :]), axis=AX))
                        ch.link(v.reciprocal(red[:, b, :], red[:, b, :]))
                        if not early:
                            dve.wait_ge(s_ok, t - 1)
                            dve.sem_inc(pace, 1)
                        ch.link(v.tensor_tensor(g3(sw[:, b, :]), g3(lg[:, b, :]), over(red[:, b, :], 2, G), ALU.mult))
                        dve.sem_inc(sw_ok, 1)
                        assert ch.n == NL
                    for b in range(2):
                        tile(0, b, True)
                    with dve.Fori(1, NU) as u:
                        for b in range(2):
                            tile(u, b, False)
                    dve.wait_ge(s_ok, NT)
                    for k in range(4):
                        v.tensor_copy(st[:, k, :], pTok[k][:, 0:D + 1])

        with ExitStack() as s2:
            m2 = Mem(nc, s2)
            T = lambda n: m2.sem("f2_" + n)
            rn = m2.sb("f2_rn", [128, 4])
            stT = m2.sb("f2_stT", [128, 2, INNER])
            nrow = m2.sb("f2_nrow", [1, INNER])
            tok = m2.sb("f2_tok", [G, INNER])
            q = m2.sb("f2_q", [G, INNER])
            k_ = m2.sb("f2_k", [G, INNER])
            vv = m2.sb("f2_v", [G, INNER])
            at = m2.sb("f2_at", [G, INNER])
            atT = m2.sb("f2_atT", [G, INNER])
            red = m2.sb("f2_red", [G, FH])
            oz = m2.sb("f2_oz", [G, FH, 128])
            pA = m2.ps("f2_pA", [128, 2, 512])
            pN = m2.ps("f2_pN", [1, 512])
            pq = m2.ps("f2_pq", [G, 512])
            pk = m2.ps("f2_pk", [G, 512])
            pv = m2.ps("f2_pv", [G, 512])
            pM = m2.ps("f2_pM", [128, 2, 512])
            toP = T("toP"); toV = T("toV"); vch = T("vch"); exp_in = T("exp_in"); exp_out = T("exp_out")
            g3 = lambda ap: ap.rearrange("p (h g) -> p h g", h=FH)
            hs = lambda h: slice(h * G, (h + 1) * G)
            with nc.Block() as block:
                @block.tensor
                def _(pe):
                    t_ = nc.tensor
                    pe.wait_ge(toP, 1)
                    for k in range(4):
                        for i in range(2):
                            t_.transpose(pA[:, i, k * 128:(k + 1) * 128], st[:, k, i * 128:(i + 1) * 128], K["ident"][:])
                        last = t_.transpose(pN[:, k * 128:(k + 1) * 128], st[:, k, D:D + 1], K["ident"][:])
                    last.then_inc(toV, 1)
                    pe.wait_ge(toP, 2)
                    for h in range(FH):
                        for i in range(2):
                            t_.matmul(pq[:, hs(h)], wfx[:, i, hs(h)], stT[:, i, hs(h)], start=(i == 0), stop=False)
                        last = t_.matmul(pq[:, hs(h)], bfx[:, hs(h)], nrow[:, hs(h)], start=False, stop=True)
                    last.then_inc(toV, 1)
                    pe.wait_ge(toP, 3)
                    t_.matmul(pq[:], wqkv[:, 0, :], tok[:], start=True, stop=True)
                    t_.matmul(pk[:], wqkv[:, 1, :], tok[:], start=True, stop=True)
                    for h in range(FH):
                        last = t_.matmul(pv[:, hs(h)], tok[:, hs(h)], wqkv[:, 2, :], start=True, stop=True)
                    last.then_inc(toV, 1)
                    pe.wait_ge(toP, 4)
                    for h in range(FH):
                        last = t_.matmul(pq[:, hs(h)], q[:, hs(h)], k_[:, hs(h)], start=True, stop=True)
                    last.then_inc(toV, 1)
                    pe.wait_ge(toP, 5)
                    for h in range(FH):
                        last = t_.transpose(pk[:, hs(h)], at[:, hs(h)], K["ident"][0:G, 0:G])
                    last.then_inc(toV, 1)
                    pe.wait_ge(toP, 6)
                    for h in range(FH):
                        last = t_.matmul(pq[:, hs(h)], vv[:, hs(h)], atT[:, hs(h)], start=True, stop=True)
                    last.then_inc(toV, 1)
                    pe.wait_ge(toP, 7)
                    for k in range(4):
                        for j in range(2):
                            last = t_.matmul(pM[:, k // 2, (k % 2) * D:(k % 2 + 1) * D], oz[:, 2 * k + j, :], wout[:, 2 * k + j, :],
                                             start=(j == 0), stop=(j == 1))
                    last.then_inc(toV, 1)

                @block.scalar
                def _(act):
                    act.wait_ge(exp_in, 1)
                    nc.scalar.activation(at[:], at[:], ACT.Exp, scale=float(G) ** -0.5).then_inc(exp_out, 1)

                @block.vector
                def _(dve):
                    v = nc.vector
                    ch = Chain(dve, vch)
                    v.memset(oz[:], 0.0)
                    ch.link(v.tensor_scalar(rn[:], st[:, :, D], 1e-5, None, ALU.add))
                    ch.link(v.reciprocal(rn[:], rn[:]))
                    for k in range(4):
                        last = v.tensor_scalar(st[:, k, :], st[:, k, :], rn[:, k:k + 1], None, ALU.mult)
                    last.then_inc(toP, 1)
                    dve.wait_ge(toV, 1)
                    v.tensor_copy(stT[:], pA[:])
                    v.tensor_copy(nrow[:], pN[:]).then_inc(toP, 1)
                    dve.wait_ge(toV, 2)
                    v.tensor_copy(tok[:], pq[:]).then_inc(toP, 1)
                    dve.wait_ge(toV, 3)
                    v.tensor_copy(q[:], pq[:])
                    v.tensor_copy(k_[:], pk[:])
                    v.tensor_copy(vv[:], pv[:]).then_inc(toP, 1)
                    dve.wait_ge(toV, 4)
                    ch.link(v.reduce_max(red[:], g3(pq[:]), axis=AX))
                    v.tensor_tensor(g3(at[:]), g3(pq[:]), over(red[:], 2, G), ALU.subtract).then_inc(exp_in, 1)
                    dve.wait_ge(exp_out, 1)
                    ch.link(v.reduce_sum(red[:], g3(at[:]), axis=AX))
                    ch.link(v.reciprocal(red[:], red[:]))
                    v.tensor_tensor(g3(at[:]), g3(at[:]), over(red[:], 2, G), ALU.mult).then_inc(toP, 1)
                    dve.wait_ge(toV, 5)
                    v.tensor_copy(atT[:], pk[:]).then_inc(toP, 1)
                    dve.wait_ge(toV, 6)
                    for h in range(FH):
                        last = v.tensor_copy(oz[:, h, (h % 2) * G:(h % 2 + 1) * G], pq[:, hs(h)])
                    last.then_inc(toP, 1)
                    dve.wait_ge(toV, 7)
                    v.tensor_copy(mm[:].rearrange("p (a b) c -> p a (b c)", a=2), pM[:])

        with ExitStack() as s2:
            m2 = Mem(nc, s2)
            T = lambda n: m2.sem("f3_" + n)
            swb = m2.sb("f3_swb", [128, 2, 4, P])
            bout = m2.sb("f3_bout", [P, D])
            wuv = m2.sb("f3_wuv", [128, 2, 2 * H])
            bu = m2.sb("f3_bu", [P, 2 * H])
            xn = m2.sb("f3_xn", [P, 2, D])
            xnT = m2.sb("f3_xnT", [128, 2, 2, P])
            row = m2.sb("f3_row", [P, 2, RW])
            pY = [m2.ps(f"f3_pY{b}", [P, D]) for b in range(2)]
            pT = [m2.ps(f"f3_pT{b}", [128, 2, 128]) for b in range(2)]
            pU = [m2.ps(f"f3_pU{b}", [P, 2 * H]) for b in range(2)]
            w_in = T("w_in"); init = T("init"); swb_ok = T("swb_ok"); y_ok = T("y_ok"); y_used = T("y_used"); vch = T("vch"); pace = T("pace")
            stats = T("stats"); sq = T("sq"); rst = T("rst"); xn_ok = T("xn_ok"); t_ok = T("t_ok"); xnT_ok = T("xnT_ok"); u_ok = T("u_ok")
            row_ok = T("row_ok"); row_out = [T("row_out0"), T("row_out1")]; x_out = T("x_out")
            rows1 = dr["rows1"][0:N, :].rearrange("(p t) c -> p t c", t=NT)
            sv1 = dr["sv1"][0:N, :].rearrange("(p t) c -> p t c", t=NT)
            with nc.Block() as block:
                @block.sync
                def _(sp):
                    sp.dma_start(bout[:], ins["L0_ffn_b_out"].unsqueeze(0).broadcast_to([P, D])).then_inc(w_in, 16)
                    sp.dma_start(wuv[:, :, 0:H], ins["L1_gnn_WuT"].rearrange("(k p) h -> p k h", p=128)).then_inc(w_in, 16)
                    sp.dma_start(wuv[:, :, H:2 * H], ins["L1_gnn_WvT"].rearrange("(k p) h -> p k h", p=128)).then_inc(w_in, 16)
                    sp.wait_ge(init, 2)
                    sp.dma_start(bu[:, 0:H], ins["L1_gnn_b_u"].unsqueeze(0).broadcast_to([P, H])).then_inc(w_in, 16)
                    sp.wait_ge(stats, 1)
                    sp.dma_start(dr["x2"].rearrange("(p t) c -> p t c", t=NT), x1[:]).then_inc(x_out, 16)
                    with sp.Fori(0, NU) as u:
                        for b in range(2):
                            sp.wait_ge(row_ok, 2 * u + (b + 1))
                            sp.sem_inc(pace, 1)
                            sp.dma_start(rows1[:, bass.ds(2 * u + b, 1), :].rearrange("p a c -> p (a c)"), row[:, b, :]).then_inc(row_out[b], 16)
                            sp.dma_start(sv1[:, bass.ds(2 * u + b, 1), :].rearrange("p a c -> p (a c)"), row[:, b, RW - H:RW]).then_inc(row_out[b], 16)
                    for b in range(2):
                        sp.wait_ge(row_out[b], 32 * NU)
                    sp.wait_ge(x_out, 16)

                @block.gpsimd
                def _(pool):
                    def copy(u, first):
                        for b in range(2):
                            t = 2 * u + b
                            if not first:
                                pool.wait_ge(y_ok, t - 1)
                                pool.sem_inc(pace, 1)
                            nc.gpsimd.tensor_copy(swb[:, b, :, :], swT[:, :, bass.ds(t, 1), :].rearrange("p k a c -> p (k a) c")).then_inc(swb_ok, 1)
                    nc.gpsimd.memset(row[:], 1.0).then_inc(init, 1)
                    nc.gpsimd.memset(bu[:], 0.0).then_inc(init, 1)
                    peeled(pool, NU, copy)

                @block.tensor
                def _(pe):
                    t_ = nc.tensor
                    pe.wait_ge(w_in, 64)

                    def product(u, first):
                        for b in range(2):
                            t = 2 * u + b
                            pe.wait_ge(swb_ok, t + 1)
                            if not first:
                                pe.sem_inc(pace, 1)
                                pe.wait_ge(y_used, t - 1)
                            for k in range(4):
                                last = t_.matmul(pY[b][:], swb[:, b, k, :], mm[:, k, :], start=(k == 0), stop=(k == 3))
                            last.then_inc(y_ok, 1)
                    peeled(pe, NU, product)
                    with pe.Fori(0, NU) as u:
                        for b in range(2):
                            t = 2 * u + b
                            pe.wait_ge(xn_ok, t + 1)
                            for k in range(2):
                                last = t_.transpose(pT[b][:, k, 0:P], xn[:, b, k * 128:(k + 1) * 128], K["ident"][0:P, 0:P])
                            last.then_inc(t_ok, 1)
                            pe.wait_ge(xnT_ok, t + 1)
                            for k in range(2):
                                last = t_.matmul(pU[b][:], xnT[:, b, k, :], wuv[:, k, :], start=(k == 0), stop=(k == 1))
                            last.then_inc(u_ok, 1)

                @block.scalar
                def _(act):
                    s = nc.scalar
                    act.wait_ge(stats, 1)
                    s.activation(norm.rstd[:], norm.rstd[:], ACT.Sqrt).then_inc(sq, 1)
                    act.wait_ge(rst, 1)

                    def tile(u, first):
                        for b in range(2):
                            t = 2 * u + b
                            tc = bass.ds(t, 1)
                            if not first:
                                act.wait_ge(row_ok, t - 1)
                                act.sem_inc(pace, 1)
                            s.activation(xn[:, b, :], flat(x1[:, tc, :]), ACT.Identity, bias=norm.nbias[:, tc],
                                         scale=norm.rstd[:, tc]).then_inc(xn_ok, 1)
                            act.wait_ge(t_ok, t + 1)
                            s.activation(xnT[:, b, :, :], pT[b][:, :, 0:P], ACT.Copy).then_inc(xnT_ok, 1)
                    peeled(act, NU, tile)

                @block.vector
                def _(dve):
                    v = nc.vector
                    dve.wait_ge(w_in, 64)
                    with dve.Fori(0, NU) as u:
                        for b in range(2):
                            t = 2 * u + b
                            ch = Chain(dve, vch, 2 * t)
                            xt = flat(x1[:, bass.ds(t, 1), :])
                            ch.link(v.tensor_tensor(xt, xt, bout[:], ALU.add))
                            dve.wait_ge(y_ok, t + 1)
                            dve.sem_inc(pace, 1)
                            ch.link(v.tensor_tensor(xt, xt, pY[b][:], ALU.add))
                            dve.sem_inc(y_used, 1)
                            norm.tile(v, t, x1[:, bass.ds(t, 1), :])
                    ch = Chain(dve, vch, 2 * NT)
                    ch.link(v.memset(norm.a[:], 0.0))
                    norm.variance(v, ch, stats)
                    dve.wait_ge(sq, 1)
                    norm.scales(v, ch, rst)

                    def tile(u, first):
                        for b in range(2):
                            t = 2 * u + b
                            if not first:
                                dve.wait_ge(row_out[b], 32 * u)
                                dve.sem_inc(pace, 1)
                            dve.wait_ge(xn_ok, t + 1)
                            v.tensor_copy(row[:, b, 0:H * VW].rearrange("p (h c) -> p h c", h=H)[:, :, 0:HD],
                                          xn[:, b, :].rearrange("p (c h) -> p h c", h=H))
                            dve.wait_ge(u_ok, t + 1)
                            v.tensor_tensor(row[:, b, H * VW:RW], pU[b][:], bu[:], ALU.add).then_inc(row_ok, 1)
                    peeled(dve, NU, tile)


def experts(nc, K, ins, dr, out):
    with ExitStack() as stack:
        m = Mem(nc, stack)
        NU = NT // 2
        flat = lambda ap: ap.rearrange("p a c -> p (a c)")
        pos = [m.sb(f"e_pos{k}", [P, NT], I32) for k in range(2)]
        wgt = [m.sb(f"e_wgt{k}", [P, NT]) for k in range(2)]
        owner = m.sb("e_owner", [1, MT], I32)
        ew = {}

        with ExitStack() as s2:
            m2 = Mem(nc, s2)
            T = lambda n: m2.sem("e0_" + n)
            x3 = m2.sb("e0_x3", [P, NT, D])
            xt = m2.sb("e0_xt", [P, NT, D])
            agg = m2.sb("e0_agg", [P, 2, 5, D])
            norm1, norm2 = Norm(m2, "e0a"), Norm(m2, "e0b")
            wr = m2.sb("e0_wr", [128, 2, X])
            br = m2.sb("e0_br", [P, X])
            xtT = m2.sb("e0_xtT", [128, 2, 2, P])
            lg = m2.sb("e0_lg", [P, NT, X])
            l2 = m2.sb("e0_l2", [P, NT, X])
            tmp = m2.sb("e0_tmp", [P, NT, X])
            hot = [m2.sb(f"e0_hot{k}", [P, NT, X]) for k in range(2)]
            both = m2.sb("e0_both", [P, NT, X])
            best = [m2.sb(f"e0_best{k}", [P, NT]) for k in range(2)]
            pick = m2.sb("e0_pick", [P, NT])
            rank = m2.sb("e0_rank", [P, NT, X])
            tot = m2.sb("e0_tot", [P, X, NT])
            exc = m2.sb("e0_exc", [P, X, NT])
            zero = m2.sb("e0_zero", [P, X * NT])
            cnt = m2.sb("e0_cnt", [P, X])
            tiles_i = m2.sb("e0_tiles_i", [P, X], I32)
            tiles = m2.sb("e0_tiles", [P, X])
            ends = m2.sb("e0_ends", [P, X])
            shift = m2.sb("e0_shift", [P, X])
            iota_e = m2.sb("e0_iota_e", [P, X])
            iota_t = m2.sb("e0_iota_t", [1, MT])
            own = m2.sb("e0_own", [1, MT, X])
            ownf = m2.sb("e0_ownf", [1, MT])
            posf = m2.sb("e0_posf", [P, NT])
            R = 5
            idx = [[m2.sb(f"e0_idx{r}{k}", [P, 1], I32) for k in range(2)] for r in range(R)]
            xrow = m2.sb("e0_xrow", [P, R, D])
            pT = [m2.ps(f"e0_pT{b}", [128, 2, 128]) for b in range(2)]
            pG = [m2.ps(f"e0_pG{b}", [P, X]) for b in range(2)]
            pR = m2.ps("e0_pR", [P, 512])
            pC = m2.ps("e0_pC", [P, 512])
            x_in = T("x_in"); a_in = [T("a_in0"), T("a_in1")]; a_used = T("a_used"); w_in = T("w_in"); x_out = T("x_out"); iotas = T("iotas")
            vch = T("vch"); lch = T("lch"); stats1 = T("stats1"); sq1 = T("sq1"); rst1 = T("rst1"); stats2 = T("stats2"); sq2 = T("sq2"); rst2 = T("rst2")
            xt_ok = T("xt_ok"); t_ok = T("t_ok"); xtT_ok = T("xtT_ok"); g_ok = T("g_ok"); g_used = T("g_used"); pace = T("pace")
            both_ok = T("both_ok"); r_ok = T("r_ok"); e_in = T("e_in"); e_out = T("e_out"); row_ok = T("row_ok"); idx_ok = T("idx_ok")
            sent = [T(f"sent{r}") for r in range(R)]
            x3_ok = T("x3_ok")
            with nc.Block() as block:
                @block.sync
                def _(sp):
                    sp.dma_start(x3[:], dr["x2"].rearrange("(p t) c -> p t c", t=NT)).then_inc(x_in, 16)
                    sp.dma_start(wr[:], ins["L1_ffn_Wr"].rearrange("(k p) e -> p k e", p=128)).then_inc(w_in, 16)
                    sp.dma_start(br[:], ins["L1_ffn_br"].unsqueeze(0).broadcast_to([P, X])).then_inc(w_in, 16)
                    av = dr["agg1"][0:N, :].rearrange("(p t) c -> p t c", t=NT)
                    for g in range(NT // 5):
                        if g >= 2:
                            sp.wait_ge(a_used, g - 1)
                        sp.dma_start(agg[:, g % 2, :, :], av[:, 5 * g:5 * g + 5, :]).then_inc(a_in[g % 2], 16)
                    sp.wait_ge(x3_ok, 1)
                    sp.dma_start(dr["x3"].rearrange("(p t) c -> p t c", t=NT), x3[:]).then_inc(x_out, 16)
                    sp.wait_ge(x_out, 16)

                @block.tensor
                def _(pe):
                    t_ = nc.tensor
                    pe.wait_ge(w_in, 32)

                    def tile(u, first):
                        for b in range(2):
                            t = 2 * u + b
                            pe.wait_ge(xt_ok, t + 1)
                            if not first:
                                pe.sem_inc(pace, 1)
                                pe.wait_ge(g_used, t - 1)
                            for k in range(2):
                                last = t_.transpose(pT[b][:, k, 0:P], xrow[:, b, k * 128:(k + 1) * 128], K["ident"][0:P, 0:P])
                            last.then_inc(t_ok, 1)
                            pe.wait_ge(xtT_ok, t + 1)
                            for k in range(2):
                                last = t_.matmul(pG[b][:], xtT[:, b, k, :], wr[:, k, :], start=(k == 0), stop=(k == 1))
                            last.then_inc(g_ok, 1)
                    peeled(pe, NU, tile)
                    pe.wait_ge(both_ok, 1)
                    t_.matmul(pR[:, 0:NT * X], K["tri"][0:P, 0:P], both[:].rearrange("p t e -> p (t e)"), start=True, stop=True)
                    t_.matmul(pC[:, 0:NT * X], K["ones"][0:P, 0:P], both[:].rearrange("p t e -> p (t e)"), start=True, stop=True).then_inc(r_ok, 1)

                @block.scalar
                def _(act):
                    s = nc.scalar
                    act.wait_ge(stats1, 1)
                    s.activation(norm1.rstd[:], norm1.rstd[:], ACT.Sqrt).then_inc(sq1, 1)
                    act.wait_ge(rst1, 1)

                    def tile(u, first):
                        for b in range(2):
                            t = 2 * u + b
                            tc = bass.ds(t, 1)
                            if not first:
                                act.wait_ge(t_ok, t - 1)
                                act.sem_inc(pace, 1)
                            s.activation(xrow[:, b, :], flat(x3[:, tc, :]), ACT.Identity, bias=norm1.nbias[:, tc], scale=norm1.rstd[:, tc])
                            s.activation(flat(xt[:, tc, :]), flat(x3[:, tc, :]), ACT.Identity, bias=norm1.nbias[:, tc],
                                         scale=norm1.rstd[:, tc]).then_inc(xt_ok, 1)
                            act.wait_ge(t_ok, t + 1)
                            s.activation(xtT[:, b, :, :], pT[b][:, :, 0:P], ACT.Copy).then_inc(xtT_ok, 1)
                    peeled(act, NU, tile)
                    act.wait_ge(stats2, 1)
                    s.activation(norm2.rstd[:], norm2.rstd[:], ACT.Sqrt).then_inc(sq2, 1)
                    act.wait_ge(e_in, 1)
                    s.activation(best[1][:], best[1][:], ACT.Exp).then_inc(e_out, 1)
                    act.wait_ge(rst2, 1)

                    def row(u, first):
                        for r in range(R):
                            t = u * R + r
                            tc = bass.ds(t, 1)
                            if not first:
                                act.wait_ge(sent[r], 32 * u)
                                act.sem_inc(pace, 1)
                            s.activation(xrow[:, r, :], flat(xt[:, tc, :]), ACT.Identity, bias=norm2.nbias[:, tc],
                                         scale=norm2.rstd[:, tc]).then_inc(row_ok, 1)
                    peeled(act, NT // R, row)

                @block.vector
                def _(dve):
                    v = nc.vector
                    ch = Chain(dve, vch)
                    dve.wait_ge(x_in, 16)
                    for g in range(NT // 5):
                        dve.wait_ge(a_in[g % 2], 16 * (g // 2 + 1))
                        for j in range(5):
                            xs = x3[:, 5 * g + j, :].rearrange("p (c h) -> p c h", h=H)
                            last = v.tensor_tensor(xs, xs, agg[:, g % 2, j, :].rearrange("p (h c) -> p c h", h=H), ALU.add)
                        last.then_inc(a_used, 1)
                    dve.wait_ge(a_used, NT // 5)
                    dve.sem_inc(x3_ok, 1)
                    with dve.Fori(0, NT) as t:
                        norm1.tile(v, t, x3[:, bass.ds(t, 1), :])
                    ch.link(v.memset(norm1.a[:], 0.0))
                    norm1.variance(v, ch, stats1)
                    dve.wait_ge(sq1, 1)
                    norm1.scales(v, ch, rst1)
                    dve.wait_ge(w_in, 32)
                    with dve.Fori(0, NU) as u:
                        for b in range(2):
                            t = 2 * u + b
                            dve.wait_ge(xt_ok, t + 1)
                            norm2.tile(v, t, xt[:, bass.ds(t, 1), :])
                            dve.wait_ge(g_ok, t + 1)
                            dve.sem_inc(pace, 1)
                            v.tensor_tensor(lg[:, bass.ds(t, 1), :].rearrange("p a c -> p (a c)"), pG[b][:], br[:], ALU.add).then_inc(g_used, 1)
                    ch.link(v.memset(norm2.a[:], 0.0))
                    norm2.variance(v, ch, stats2)
                    dve.wait_ge(iotas, 2)
                    src = lg
                    for k in range(2):
                        ch.link(v.reduce_max(best[k][:], src[:], axis=AX))
                        ch.link(v.tensor_tensor(tmp[:], src[:], over(best[k][:], 2, X), ALU.is_lt))
                        ch.link(v.scalar_tensor_tensor(tmp[:], tmp[:], float(X), over(iota_e[:], 1, NT), ALU.mult, ALU.add))
                        ch.link(v.tensor_reduce(pick[:], tmp[:], AX, ALU.min))
                        ch.link(v.tensor_tensor(hot[k][:], over(iota_e[:], 1, NT), over(pick[:], 2, X), ALU.is_equal))
                        if k == 0:
                            ch.link(v.scalar_tensor_tensor(l2[:], hot[0][:], -BIG, lg[:], ALU.mult, ALU.add))
                            src = l2
                    v.tensor_tensor(both[:], hot[0][:], hot[1][:], ALU.add).then_inc(both_ok, 1)
                    dve.wait_ge(sq2, 1)
                    v.tensor_tensor(best[1][:], best[1][:], best[0][:], ALU.subtract).then_inc(e_in, 1)
                    norm2.scales(v, ch, rst2)
                    dve.wait_ge(e_out, 1)
                    ch.link(v.tensor_scalar(wgt[0][:], best[1][:], 1.0, None, ALU.add))
                    ch.link(v.reciprocal(wgt[0][:], wgt[0][:]))
                    v.tensor_tensor(wgt[1][:], best[1][:], wgt[0][:], ALU.mult)
                    ch.link(v.memset(zero[:], 0.0))
                    dve.wait_ge(r_ok, 1)
                    v.tensor_copy(rank[:].rearrange("p t e -> p (t e)"), pR[:, 0:NT * X])
                    ch.link(v.tensor_copy(tot[:].rearrange("p e t -> p t e"), pC[:, 0:NT * X].rearrange("p (t e) -> p t e", e=X)))
                    fl = "p e t -> p (e t)"
                    ch.link(v.tensor_tensor_scan(exc[:].rearrange(fl), tot[:].rearrange(fl), zero[:], 0.0, ALU.add, ALU.add))
                    ch.link(v.tensor_tensor(exc[:].rearrange(fl), exc[:].rearrange(fl), tot[:].rearrange(fl), ALU.subtract))
                    ch.link(v.reduce_sum(cnt[:], tot[:], axis=AX))
                    ch.link(v.tensor_scalar(tiles_i[:], cnt[:], float(Q - 1), None, ALU.add))
                    ch.link(v.tensor_scalar(tiles_i[:], tiles_i[:], 7, None, ALU.arith_shift_right))
                    ch.link(v.tensor_copy(tiles[:], tiles_i[:]))
                    ch.link(v.tensor_tensor_scan(ends[:], tiles[:], zero[:, 0:X], 0.0, ALU.add, ALU.add))
                    ch.link(v.tensor_tensor(shift[:], ends[:], tiles[:], ALU.subtract))
                    ch.link(v.scalar_tensor_tensor(shift[:], shift[:], float(Q), exc[:, :, 0], ALU.mult, ALU.subtract))
                    ch.link(v.tensor_tensor(exc[:], exc[:], over(shift[:], 2, NT), ALU.add))
                    ch.link(v.tensor_tensor(rank[:], rank[:], exc[:].rearrange("p e t -> p t e"), ALU.add))
                    for k in range(2):
                        ch.link(v.tensor_tensor(tmp[:], rank[:], hot[k][:], ALU.mult))
                        ch.link(v.reduce_sum(posf[:], tmp[:], axis=AX))
                        ch.link(v.tensor_copy(pos[k][:], posf[:]))

                    def index(u, first):
                        for r in range(R):
                            t = u * R + r
                            if not first:
                                dve.wait_ge(sent[r], 32 * u)
                                dve.sem_inc(pace, 1)
                            v.tensor_copy(idx[r][0][:], pos[0][:, bass.ds(t, 1)])
                            v.tensor_copy(idx[r][1][:], pos[1][:, bass.ds(t, 1)]).then_inc(idx_ok, 1)
                    peeled(dve, NT // R, index)
                    ch.link(v.tensor_tensor(own[:], over(iota_t[:], 2, X), over(ends[0:1, :], 1, MT), ALU.is_ge))
                    ch.link(v.reduce_sum(ownf[:], own[:], axis=AX))
                    ch.link(v.tensor_scalar(owner[:], ownf[:], float(X - 1), None, ALU.min))

                @block.gpsimd
                def _(pool):
                    pool.iota(iota_e[:], pattern=[[1, X]], base=0, channel_multiplier=0, allow_small_or_imprecise_dtypes=True).then_inc(iotas, 1)
                    pool.iota(iota_t[:], pattern=[[1, MT]], base=0, channel_multiplier=0, allow_small_or_imprecise_dtypes=True).then_inc(iotas, 1)
                    with pool.Fori(0, NT // R) as u:
                        for r in range(R):
                            pool.wait_ge(idx_ok, u * R + (r + 1))
                            pool.sem_inc(pace, 1)
                            pool.wait_ge(row_ok, u * R + (r + 1))
                            pool.sem_inc(pace, 1)
                            for k in range(2):
                                pool.indirect_dma_start(out=dr["xs"], out_offset=bass.IndirectOffsetOnAxis(ap=idx[r][k][:, 0:1], axis=0),
                                                        in_=xrow[:, r, :], in_offset=None).then_inc(sent[r], 16)
                    for r in range(R):
                        pool.wait_ge(sent[r], 32 * (NT // R))

        with ExitStack() as s2:
            m2 = Mem(nc, s2)
            T = lambda n: m2.sem("e1_" + n)
            w1 = m2.sb("e1_w1", [128, X, 2, HID])
            w2 = m2.sb("e1_w2", [128, X, KC, D])
            b1 = m2.sb("e1_b1", [1, X, HID])
            b2 = m2.sb("e1_b2", [1, X, D])
            gl = m2.sb("e1_gl", [128, X, 2])
            bl = m2.sb("e1_bl", [128, X, 2])
            xs = m2.sb("e1_xs", [Q, 2, D])
            xT = m2.sb("e1_xT", [128, 2, 2, Q])
            hh = m2.sb("e1_hh", [Q, 2, HID])
            hT = m2.sb("e1_hT", [128, 2, KC, Q])
            ys = m2.sb("e1_ys", [Q, 2, D])
            pX = m2.ps("e1_pX", [128, 2, Q])
            pH = m2.ps("e1_pH", [Q, HID])
            pHT = m2.ps("e1_pHT", [128, KC, Q])
            pY = m2.ps("e1_pY", [Q, 2, D])
            w_in = T("w_in"); x_in = [T("x_in0"), T("x_in1")]; xT_ps = T("xT_ps"); xT_ok = T("xT_ok"); h_ok = T("h_ok"); g_ok = T("g_ok")
            hT_ps = T("hT_ps"); hT_ok = T("hT_ok"); y_ok = T("y_ok"); ys_ok = T("ys_ok"); y_out = [T("y_out0"), T("y_out1")]; pace = T("pace")
            MU = MT // 2
            with nc.Block() as block:
                @block.sync
                def _(sp):
                    def load(u, b):
                        sp.dma_start(xs[:, b, :], dr["xs"].rearrange("(t q) c -> t q c", q=Q)[bass.ds(2 * u + b, 1), :, :].rearrange("a q c -> (a q) c")).then_inc(x_in[b], 16)

                    def store(u, b):
                        sp.wait_ge(ys_ok, 2 * u + (b + 1))
                        sp.sem_inc(pace, 1)
                        sp.dma_start(dr["ys"].rearrange("(t q) c -> t q c", q=Q)[bass.ds(2 * u + b, 1), :, :].rearrange("a q c -> (a q) c"), ys[:, b, :]).then_inc(y_out[b], 16)
                    load(0, 0)
                    load(0, 1)
                    for e in range(X):
                        sp.dma_start(w1[:, e, :, :], ins["L1_ffn_W1"][e].rearrange("(k p) h -> p k h", p=128)).then_inc(w_in, 16)
                        sp.dma_start(w2[:, e, :, :], ins["L1_ffn_W2"][e].rearrange("(k p) o -> p k o", p=128)).then_inc(w_in, 16)
                    with sp.Fori(0, MU - 1) as u:
                        for b in range(2):
                            sp.wait_ge(xT_ps, 2 * u + (b + 1))
                            sp.sem_inc(pace, 1)
                            load(u + 1, b)
                            store(u, b)
                    for b in range(2):
                        store(MU - 1, b)
                    for b in range(2):
                        sp.wait_ge(y_out[b], 16 * MU)

                @block.tensor
                def _(pe):
                    t_ = nc.tensor

                    def front(u, b):
                        t = 2 * u + b
                        pe.wait_ge(x_in[b], 16 * u + 16)
                        for k in range(2):
                            last = t_.transpose(pX[:, k, :], xs[:, b, k * 128:(k + 1) * 128], K["ident"][:])
                        last.then_inc(xT_ps, 1)
                        e = pe.value_load(owner[0:1, bass.ds(t, 1)], min_val=0, max_val=X - 1)
                        pe.wait_ge(xT_ok, t + 1)
                        if not (isinstance(t, int) and t == 0):
                            pe.sem_inc(pace, 1)
                            pe.wait_ge(g_ok, t)
                        for c in range(2):
                            sl = slice(c * 512, (c + 1) * 512)
                            for k in range(2):
                                t_.matmul(pH[:, sl], xT[:, b, k, :], w1[:, bass.ds(e, 1), k, sl].rearrange("p a h -> p (a h)"), start=(k == 0), stop=False)
                            last = t_.matmul(pH[:, sl], K["ones"][0:1, :], b1[:, bass.ds(e, 1), sl].rearrange("p a h -> p (a h)"), start=False, stop=True)
                        last.then_inc(h_ok, 1)
                        return e

                    def back(u, b, e):
                        t = 2 * u + b
                        pe.wait_ge(g_ok, t + 1)
                        if not (isinstance(t, int) and t == 0):
                            pe.sem_inc(pace, 1)
                            pe.wait_ge(hT_ok, t)
                        for k in range(KC):
                            last = t_.transpose(pHT[:, k, :], hh[:, b, k * 128:(k + 1) * 128], K["ident"][:])
                        last.then_inc(hT_ps, 1)
                        pe.wait_ge(hT_ok, t + 1)
                        if not (isinstance(t, int) and t < 2):
                            pe.sem_inc(pace, 1)
                            pe.wait_ge(ys_ok, t - 1)
                        for k in range(KC):
                            t_.matmul(pY[:, b, :], hT[:, b, k, :], w2[:, bass.ds(e, 1), k, :].rearrange("p a h -> p (a h)"), start=(k == 0), stop=False)
                        t_.matmul(pY[:, b, :], K["ones"][0:1, :], b2[:, bass.ds(e, 1), :].rearrange("p a h -> p (a h)"), start=False, stop=True).then_inc(y_ok, 1)
                    pe.wait_ge(w_in, 32 * X + 64)

                    def group(u, first):
                        for b in range(2):
                            e = front(u, b)
                            back(u, b, e)
                    peeled(pe, MU, group)

                @block.scalar
                def _(act):
                    s = nc.scalar
                    act.dma_start(b1[:], ins["L1_ffn_b1"].rearrange("(o e) h -> o e h", o=1)).then_inc(w_in, 16)
                    act.dma_start(b2[:], ins["L1_ffn_b2"].rearrange("(o e) h -> o e h", o=1)).then_inc(w_in, 16)
                    act.dma_start(gl[:], ins["L1_ffn_ln_g"].rearrange("e (k p) -> p e k", p=128), allow_slow_non_contiguous=True).then_inc(w_in, 16)
                    act.dma_start(bl[:], ins["L1_ffn_ln_b"].rearrange("e (k p) -> p e k", p=128), allow_slow_non_contiguous=True).then_inc(w_in, 16)
                    act.wait_ge(w_in, 32 * X + 64)

                    def group(u, first):
                        for b in range(2):
                            t = 2 * u + b
                            e = act.value_load(owner[0:1, bass.ds(t, 1)], min_val=0, max_val=X - 1)
                            act.wait_ge(xT_ps, t + 1)
                            for k in range(2):
                                last = s.activation(xT[:, b, k, :], pX[:, k, :], ACT.Identity, bias=bl[:, bass.ds(e, 1), k], scale=gl[:, bass.ds(e, 1), k])
                            last.then_inc(xT_ok, 1)
                            act.wait_ge(h_ok, t + 1)
                            s.activation(hh[:, b, :], pH[:], ACT.Gelu).then_inc(g_ok, 1)
                    peeled(act, MU, group)

                @block.vector
                def _(dve):
                    v = nc.vector

                    def group(u, first):
                        for b in range(2):
                            t = 2 * u + b
                            dve.wait_ge(hT_ps, t + 1)
                            v.tensor_copy(hT[:, b, :, :], pHT[:]).then_inc(hT_ok, 1)
                            dve.wait_ge(y_ok, t + 1)
                            if not first:
                                dve.sem_inc(pace, 1)
                                dve.wait_ge(y_out[b], 16 * u)
                            v.tensor_copy(ys[:, b, :], pY[:, b, :]).then_inc(ys_ok, 1)
                    peeled(dve, MU, group)

        with ExitStack() as s2:
            m2 = Mem(nc, s2)
            T = lambda n: m2.sem("e2_" + n)
            R = 5
            x3 = m2.sb("e2_x3", [P, NT, D])
            idx = [[m2.sb(f"e2_idx{r}{k}", [P, 1], I32) for k in range(2)] for r in range(R)]
            yr = m2.sb("e2_yr", [P, R, 2, D])
            x_in = T("x_in"); idx_ok = T("idx_ok"); got = [T(f"got{r}") for r in range(R)]; pace = T("pace"); vch = T("vch"); done = T("done"); o_out = T("o_out")
            with nc.Block() as block:
                @block.sync
                def _(sp):
                    sp.dma_start(x3[:], dr["x3"].rearrange("(p t) c -> p t c", t=NT)).then_inc(x_in, 16)
                    ov = out.rearrange("(p t) c -> p t c", t=NT)
                    for g in range(NT // R):
                        sp.wait_ge(done, g + 1)
                        sp.dma_start(ov[:, g * R:(g + 1) * R, :], x3[:, g * R:(g + 1) * R, :]).then_inc(o_out, 16)
                    sp.wait_ge(o_out, 16 * (NT // R))

                @block.gpsimd
                def _(pool):
                    with pool.Fori(0, NT // R) as u:
                        for r in range(R):
                            pool.wait_ge(idx_ok, u * R + (r + 1))
                            pool.sem_inc(pace, 1)
                            for k in range(2):
                                pool.indirect_dma_start(out=yr[:, r, k, :], out_offset=None, in_=dr["ys"],
                                                        in_offset=bass.IndirectOffsetOnAxis(ap=idx[r][k][:, 0:1], axis=0)).then_inc(got[r], 16)

                @block.vector
                def _(dve):
                    v = nc.vector

                    def index(t, r):
                        v.tensor_copy(idx[r][0][:], pos[0][:, bass.ds(t, 1)])
                        v.tensor_copy(idx[r][1][:], pos[1][:, bass.ds(t, 1)]).then_inc(idx_ok, 1)

                    def add(u, more):
                        for r in range(R):
                            t = u * R + r
                            tc = bass.ds(t, 1)
                            ch = Chain(dve, vch, 2 * t)
                            dve.wait_ge(got[r], 32 * u + 32)
                            dve.sem_inc(pace, 1)
                            xs = flat(x3[:, tc, :])
                            for k in range(2):
                                ch.link(v.scalar_tensor_tensor(xs, yr[:, r, k, :], wgt[k][:, tc], xs, ALU.mult, ALU.add))
                            if more:
                                index(t + R, r)
                        dve.sem_inc(done, 1)
                    dve.wait_ge(x_in, 16)
                    for r in range(R):
                        index(r, r)
                    with dve.Fori(0, NT // R - 1) as u:
                        add(u, True)
                    add(NT // R - 1, False)


def layouts(inputs):
    T = np.ascontiguousarray
    return {
        "L0_gnn_WT": T(np.asarray(inputs["L0_gnn_W"]).T),
        "L0_gnn_edge_WT": T(np.asarray(inputs["L0_gnn_edge_W"]).T),
        "L1_gnn_WuT": T(np.asarray(inputs["L1_gnn_W_u"]).T),
        "L1_gnn_WvT": T(np.asarray(inputs["L1_gnn_W_v"]).T),
        "L0_ffn_WxT": T(np.asarray(inputs["L0_ffn_W_x"]).T),
    }


def program(nc, ins, out):
    with ExitStack() as stack:
        m = Mem(nc, stack)
        K = {"ident": m.sb("k_ident", [128, 128]), "tri": m.sb("k_tri", [128, 128]), "ones": m.sb("k_ones", [128, 128]),
             "iota64": m.sb("k_iota64", [128, NB]), "padrec": m.sb("k_padrec", [NPAD - N, 4], I32), "pt": m.sb("k_pt", [Q, QT, 4], I32), "rp": m.sb("k_rp", [Q, QT]),
             "deg": m.sb("k_deg", [Q, QT]), "ct": m.sb("k_ct", [1, QT + 2], I32)}

        def scratch(name, shape, dt=F32):
            return nc.dram_tensor(name, shape, dt, kind="Internal").ap()
        dr = {"rows0": scratch("rows0", (NPAD, RW)), "rows1": scratch("rows1", (NPAD, RW)), "sv1": scratch("sv1", (NPAD, H)),
              "rec": scratch("rec", (E, REC)), "rp": scratch("rp", (1, N + 1), I32),
              "noderec": scratch("noderec", (NPAD, 4), I32), "slots": scratch("slots", (CMAX, Q, REC)),
              "agg0": scratch("agg0", (NPAD, D)), "agg1": scratch("agg1", (NPAD, D)), "x2": scratch("x2", (N, D)), "x3": scratch("x3", (N, D)),
              "xs": scratch("xs", (MT * Q, D)), "ys": scratch("ys", (MT * Q, D))}
        prepare(nc, K, ins, dr)
        order(nc, K, ins, dr)
        slots(nc, K, ins, dr)
        graph(nc, K, ins, dr, 0)
        slice_ffn(nc, K, ins, dr)
        graph(nc, K, ins, dr, 1)
        experts(nc, K, ins, dr, out)


_INS = ["x", "src", "dst", "edge_attr_3", "L0_gnn_W", "L0_gnn_a_src", "L0_gnn_a_dst", "L0_gnn_edge_b", "L0_gnn_bias",
        "L0_ffn_W_fx", "L0_ffn_b_fx", "L0_ffn_b_x", "L0_ffn_W_slice", "L0_ffn_b_slice", "L0_ffn_W_q", "L0_ffn_W_k",
        "L0_ffn_W_v", "L0_ffn_W_out", "L0_ffn_b_out", "L0_ffn_temperature", "L1_gnn_b_u", "L1_ffn_Wr", "L1_ffn_br",
        "L1_ffn_ln_g", "L1_ffn_ln_b", "L1_ffn_W1", "L1_ffn_b1", "L1_ffn_W2", "L1_ffn_b2"]


def kernel(**inputs):
    import concourse.bacc as bacc
    from concourse.bass_utils import run_bass_kernel_spmd

    nc = bacc.Bacc("TRN2", target_bir_lowering=False, num_devices=1)
    given = {name: np.ascontiguousarray(inputs[name]) for name in _INS}
    given.update(layouts(inputs))
    arrays, aps = {}, {}
    for name, a in given.items():
        arrays[f"in_{name}"] = a
        aps[name] = nc.dram_tensor(f"in_{name}", a.shape, mybir.dt.from_np(a.dtype), kind="ExternalInput").ap()
    out = nc.dram_tensor("out_0", (N, D), F32, kind="ExternalOutput").ap()
    program(nc, aps, out)
    r = run_bass_kernel_spmd(nc, [arrays], core_ids=[0])
    return r.results[0]["out_0"]
```

```python
import numpy as np
import concourse.bass as bass
from concourse import mybir
from contextlib import ExitStack

F32 = mybir.dt.float32
BF16 = mybir.dt.bfloat16
I32 = mybir.dt.int32
ALU = mybir.AluOpType
ACT = mybir.ActivationFunctionType
AX = mybir.AxisListType.X

N = 6250
E = 106250
D = 256
H = 8
HD = D // H
P = 125
NT = N // P
EP = E // P
Q = 128
QT = -(-N // Q)
NPAD = QT * Q
C = 8
CLOG = 3
REC = 4 * C
NB = 64
VW = HD + 1
RW = H * VW + 2 * H
CMAX = (E // C + 2 * QT + 8) // 4 * 4
BLOG = 9
BLK = 1 << BLOG
BIG = 1e30
LN_EPS = 1e-5
G = 64
FH = 8
X = 8
HID = 1024
MT = 106
KC = HID // 128


class Chain:

    def __init__(self, eng, sem, base=0):
        self.eng, self.sem, self.base, self.n = eng, sem, base, 0

    def link(self, ins, wait=True):
        ins.then_inc(self.sem, 1)
        self.n += 1
        if wait:
            self.wait()

    def wait(self, n=None):
        self.eng.wait_ge(self.sem, self.base + (self.n if n is None else n))

    def enter(self, i, k):
        self.outer, self.k, self.n0 = self.base, k, self.n
        self.base, self.n = self.base + self.n + i * k, 0

    def leave(self, times):
        assert self.n == self.k, (self.n, self.k)
        self.base, self.n = self.outer, self.n0 + times * self.k


def over(ap, axis, n):
    a = ap.unsqueeze(axis)
    shape = list(a.shape)
    shape[axis] = n
    return a.broadcast_to(shape)


def peeled(eng, n, body):
    body(0, True)
    with eng.Fori(1, n) as u:
        body(u, False)


class Mem:

    def __init__(self, nc, stack):
        self.nc, self.stack, self.sems = nc, stack, []
        stack.callback(self.clear)

    def clear(self):
        if self.sems:
            self.nc.clear_and_free_semaphores(self.sems)
            self.nc.all_engine_barrier()

    def sb(self, name, shape, dt=F32):
        return self.stack.enter_context(self.nc.sbuf_tensor(name, shape, dt))

    def ps(self, name, shape, dt=F32):
        return self.stack.enter_context(self.nc.psum_tensor(name, shape, dt))

    def sem(self, name):
        self.sems.append(self.nc.alloc_semaphore(name))
        return self.sems[-1]


class Norm:

    def __init__(self, m, name):
        self.st = m.sb(name + "_st", [P, NT, 6])
        self.a, self.b, self.rstd, self.nbias = (m.sb(name + s, [P, NT]) for s in ("_na", "_nb", "_rstd", "_nbias"))

    def tile(self, v, t, x):
        return v.bn_stats(self.st[:, bass.ds(t, 1), :].rearrange("p a c -> p (a c)"), x.rearrange("p a c -> p (a c)"))

    def variance(self, v, ch, done):
        st = self.st
        ch.link(v.tensor_tensor(self.a[:], st[:, :, 1], st[:, :, 4], ALU.subtract))
        ch.link(v.scalar_tensor_tensor(self.a[:], self.a[:], 0.25, self.a[:], ALU.mult, ALU.mult))
        ch.link(v.tensor_tensor(self.b[:], st[:, :, 2], st[:, :, 5], ALU.add))
        ch.link(v.scalar_tensor_tensor(self.a[:], self.b[:], 1.0 / D, self.a[:], ALU.mult, ALU.add))
        ch.link(v.tensor_scalar(self.rstd[:], self.a[:], LN_EPS, None, ALU.add))
        ch.link(v.tensor_tensor(self.b[:], st[:, :, 1], st[:, :, 4], ALU.add))
        v.tensor_scalar(self.nbias[:], self.b[:], -0.5, None, ALU.mult).then_inc(done, 1)

    def scales(self, v, ch, done):
        ch.link(v.reciprocal(self.rstd[:], self.rstd[:]))
        v.tensor_tensor(self.nbias[:], self.nbias[:], self.rstd[:], ALU.mult).then_inc(done, 1)


def prepare(nc, K, ins, dr):
    with ExitStack() as stack:
        m = Mem(nc, stack)
        x = m.sb("p_x", [P, NT, D])
        srcw = m.sb("p_srcw", [P, EP + C - 1], I32)
        attrw = m.sb("p_attrw", [P, 3 * (EP + C - 1)])
        PIECE = EP // 5
        rec = m.sb("p_rec", [P, 2, PIECE, REC])
        dst0 = m.sb("p_dst0", [P, 1], I32)
        dst0f = m.sb("p_dst0f", [P, 1])
        iota_n = m.sb("p_iota_n", [P, N])
        below = m.sb("p_below", [P, N], BF16)
        ones = m.sb("p_ones", [P, 1], BF16)
        node = m.sb("p_node", [P, NT])
        blk = m.sb("p_blk", [P, NT])
        cnt = m.sb("p_cnt", [P, NT])
        blk_i = m.sb("p_blk_i", [P, NT], I32)
        R = 5
        idx = [m.sb(f"p_idx{r}", [P, 1], I32) for r in range(R)]
        drow = m.sb("p_drow", [P, R, EP], I32)
        rp = m.sb("p_rp", [P, NT], I32)
        e_end = m.sb("p_eend", [1, 1], I32)
        zrow = m.sb("p_zrow", [NPAD - N, RW])
        zxs = m.sb("p_zxs", [Q, D])
        wn = m.sb("p_wn", [128, 2, D])
        aa = m.sb("p_aa", [128, 2, 2])
        amask = m.sb("p_amask", [128, 4])
        ablk = m.sb("p_ablk", [128, 2, 2 * H])
        wx = m.sb("p_wx", [128, 2, D + 2 * H])
        norm = Norm(m, "p")
        rstd, nbias = norm.rstd, norm.nbias
        xn = m.sb("p_xn", [P, 2, D])
        xnT = m.sb("p_xnT", [128, 2, 2, P])
        row = m.sb("p_row", [P, 2, RW])
        pT = [m.ps(f"p_pT{r}", [128, 2, 256]) for r in range(2)]
        pH = [m.ps(f"p_pH{r}", [P, 512]) for r in range(2)]
        pW = m.ps("p_pW", [128, 2, 256])
        pC = m.ps("p_pC", [P, 64])

        x_in = m.sem("p_x_in"); e_in = m.sem("p_e_in"); w_in = m.sem("p_w_in"); d_in = m.sem("p_d_in")
        zeroed = m.sem("p_zeroed"); rec_made = m.sem("p_rec_made"); rec_out = [m.sem(f"p_rec_out{b}") for b in range(2)]
        misc_out = m.sem("p_misc_out")
        consts = m.sem("p_consts"); below_ok = m.sem("p_below_ok"); counted = m.sem("p_counted")
        idx_ok = m.sem("p_idx_ok"); landed = [m.sem(f"p_landed{r}") for r in range(R)]
        vch = m.sem("p_vchain"); stats = m.sem("p_stats"); sq = m.sem("p_sqrt"); rst = m.sem("p_rstd_ok")
        ach = m.sem("p_achain")
        ablk_ok = m.sem("p_ablk_ok"); wa_ok = m.sem("p_wa_ok"); wx_ok = m.sem("p_wx_ok")
        xn_ok = m.sem("p_xn_ok"); t_ok = m.sem("p_t_ok"); xnT_ok = m.sem("p_xnT_ok"); h_ok = m.sem("p_h_ok")
        row_ok = m.sem("p_row_ok"); row_out = [m.sem(f"p_row_out{b}") for b in range(2)]
        rp_ok = m.sem("p_rp_ok"); rp_out = m.sem("p_rp_out"); pace = m.sem("p_pace")

        rows0 = dr["rows0"][0:N, :].rearrange("(p t) c -> p t c", t=NT)
        recs = dr["rec"].rearrange("(p g e) c -> p g (e c)", p=P, g=5)

        with nc.Block() as block:
            @block.sync
            def _(sp):
                sp.dma_start(dst0[:], ins["dst"].rearrange("(p e) -> p e", p=P)[:, 0:1], allow_slow_non_contiguous=True).then_inc(d_in, 16)
                sp.dma_start(x[:], ins["x"].rearrange("(p t) c -> p t c", t=NT)).then_inc(x_in, 16)
                sp.wait_ge(zeroed, 2)
                s, a = ins["src"], ins["edge_attr_3"].rearrange("e c -> (e c)")
                sp.dma_start(srcw[0:P - 1, :], bass.AP(s.tensor, 0, [[EP, P - 1], [1, EP + C - 1]])).then_inc(e_in, 16)
                sp.dma_start(srcw[P - 1:P, 0:EP], s[E - EP:E].unsqueeze(0)).then_inc(e_in, 16)
                sp.dma_start(attrw[0:P - 1, :], bass.AP(a.tensor, 0, [[3 * EP, P - 1], [1, 3 * (EP + C - 1)]])).then_inc(e_in, 16)
                sp.dma_start(attrw[P - 1:P, 0:3 * EP], a[3 * (E - EP):3 * E].unsqueeze(0)).then_inc(e_in, 16)
                for g in range(5):
                    sp.wait_ge(rec_made, 2 * g + 2)
                    sp.dma_start(recs[:, g, :], rec[:, g % 2, :, :].rearrange("p e c -> p (e c)")).then_inc(rec_out[g % 2], 16)
                sp.wait_ge(zeroed, 6)
                sp.dma_start(dr["rows0"][N:NPAD, :], zrow[:]).then_inc(misc_out, 16)
                sp.dma_start(dr["rows1"][N:NPAD, :], zrow[:]).then_inc(misc_out, 16)
                sp.dma_start(dr["sv1"][N:NPAD, :], zrow[:, 0:H]).then_inc(misc_out, 16)
                sp.dma_start(dr["xs"].rearrange("(t p) c -> p t c", p=Q), over(zxs[:], 1, MT)).then_inc(misc_out, 16)
                with sp.Fori(0, NT // 2) as u:
                    for b in range(2):
                        sp.wait_ge(row_ok, 2 * u + (b + 1))
                        sp.dma_start(rows0[:, bass.ds(2 * u + b, 1), :].rearrange("p a c -> p (a c)"), row[:, b, :]).then_inc(row_out[b], 16)
                for b in range(2):
                    sp.wait_ge(row_out[b], 16 * (NT // 2 + 1))
                sp.wait_ge(rp_ok, 1)
                sp.dma_start(dr["rp"][:, 0:N].rearrange("o (p t) -> (o p) t", t=NT), rp[:]).then_inc(rp_out, 16)
                sp.dma_start(dr["rp"][:, N:N + 1], e_end[:]).then_inc(rp_out, 16)
                sp.wait_ge(rp_out, 32)
                sp.wait_ge(rec_out[0], 48)
                sp.wait_ge(rec_out[1], 32)
                sp.wait_ge(misc_out, 64)

            @block.gpsimd
            def _(pool):
                pool.memset(srcw[:], 0).then_inc(zeroed, 1)
                pool.memset(attrw[:], 0.0).then_inc(zeroed, 1)
                pool.iota(iota_n[:], pattern=[[1, N]], base=0, channel_multiplier=0,
                          allow_small_or_imprecise_dtypes=True).then_inc(consts, 1)
                pool.iota(node[:], pattern=[[1, NT]], base=0, channel_multiplier=NT,
                          allow_small_or_imprecise_dtypes=True).then_inc(consts, 1)
                pool.memset(ones[:], 1.0).then_inc(consts, 1)
                pool.memset(K["ident"][:], 0.0)
                pool.memset(K["tri"][:], 1.0)
                pool.memset(K["ones"][:], 1.0)
                pool.memset(amask[:], 1.0)
                pool.memset(row[:], 1.0)
                pool.iota(K["iota64"][:], pattern=[[1, NB]], base=0, channel_multiplier=0,
                          allow_small_or_imprecise_dtypes=True)
                pool.memset(zrow[:], 0.0)
                pool.memset(zxs[:], 0.0).then_inc(consts, 1)
                pool.wait_ge(consts, 4)
                pool.affine_select(out=K["ident"][:], in_=K["ident"][:], compare_op=ALU.not_equal, fill=1.0, base=0,
                                   pattern=[[-1, 128]], channel_multiplier=1)
                pool.affine_select(out=K["tri"][:], in_=K["tri"][:], compare_op=ALU.is_gt, fill=0.0, base=0,
                                   pattern=[[1, 128]], channel_multiplier=-1)
                pool.affine_select(out=amask[:], in_=amask[:], compare_op=ALU.is_ge, fill=0.0, base=0,
                                   pattern=[[-HD, 4]], channel_multiplier=1).then_inc(consts, 1)
                pool.wait_ge(consts, 5)
                pool.affine_select(out=amask[:], in_=amask[:], compare_op=ALU.is_ge, fill=0.0, base=HD - 1,
                                   pattern=[[HD, 4]], channel_multiplier=-1)
                pool.iota(e_end[:], pattern=[[0, 1]], base=E, channel_multiplier=0).then_inc(consts, 1)
                pool.wait_ge(consts, 6)
                pool.iota(K["padrec"][:], pattern=[[0, 4]], base=N, channel_multiplier=1).then_inc(consts, 1)
                pool.wait_ge(consts, 7)
                pool.memset(K["padrec"][:, 1:4], 0).then_inc(zeroed, 4)
                pool.wait_ge(zeroed, 6)
                dview = ins["dst"].rearrange("(p e) -> p e", p=P)

                def gather(u, r):
                    pool.wait_ge(idx_ok, u * R + (r + 1))
                    pool.sem_inc(pace, 1)
                    pool.indirect_dma_start(out=drow[:, r, :], out_offset=None, in_=dview,
                                            in_offset=bass.IndirectOffsetOnAxis(ap=idx[r][:, 0:1], axis=0)
                                            ).then_inc(landed[r], 16)
                with pool.Fori(0, NT // R) as u:
                    for r in range(R):
                        gather(u, r)

            @block.vector
            def _(dve):
                v = nc.vector
                ch = Chain(dve, vch)
                dve.wait_ge(consts, 7)
                dve.wait_ge(d_in, 16)
                ch.link(v.tensor_copy(dst0f[:], dst0[:]))
                v.tensor_scalar(below[:], iota_n[:], dst0f[:], None, ALU.is_gt).then_inc(below_ok, 1)
                dve.wait_ge(w_in, 64)
                for k in range(2):
                    for s in range(2):
                        if k == 0 and s == 0:
                            ch.link(v.memset(ablk[:], 0.0))
                        last = v.tensor_scalar(ablk[:, k, s * H + 4 * k:s * H + 4 * k + 4], amask[:], aa[:, k, s:s + 1], None, ALU.mult)
                last.then_inc(ablk_ok, 1)
                dve.wait_ge(e_in, 64)
                for g in range(5):
                    if g >= 2:
                        dve.wait_ge(rec_out[g % 2], 16 * (g // 2))
                    o = rec[:, g % 2, :, :]
                    sw = bass.AP(srcw, g * PIECE, [[EP + C - 1, P], [1, PIECE], [1, C]])
                    aw = bass.AP(attrw, 3 * g * PIECE, [[3 * (EP + C - 1), P], [3, PIECE], [1, 3 * C]])
                    v.tensor_copy(o[:, :, 0:C].bitcast(I32), sw).then_inc(rec_made, 1)
                    v.tensor_copy(o[:, :, C:REC], aw).then_inc(rec_made, 1)
                dve.wait_ge(x_in, 16)
                with dve.Fori(0, NT) as t:
                    norm.tile(v, t, x[:, bass.ds(t, 1), :])
                ch.link(v.memset(norm.a[:], 0.0))
                norm.variance(v, ch, stats)
                dve.wait_ge(sq, 1)
                norm.scales(v, ch, rst)
                dve.wait_ge(counted, 1)
                ch.link(v.tensor_scalar(blk[:], pC[:, 0:NT], -1.0, 0.0, ALU.add, ALU.max))
                ch.link(v.tensor_copy(blk_i[:], blk[:]))
                for r in range(R):
                    v.tensor_copy(idx[r][:], blk_i[:, r:r + 1]).then_inc(idx_ok, 1)

                def count(u, r, more):
                    t = u * R + r
                    dve.wait_ge(landed[r], 16 * u + 16)
                    dve.sem_inc(pace, 1)
                    tc = bass.ds(t, 1)
                    last = v.tensor_scalar(drow[:, r, :], drow[:, r, :], node[:, tc], 0.0, ALU.is_lt, ALU.add, accum_out=cnt[:, tc])
                    if more:
                        v.tensor_copy(idx[r][:], blk_i[:, bass.ds(t + R, 1)]).then_inc(idx_ok, 1)
                    return last
                with dve.Fori(0, NT // R - 1) as u:
                    for r in range(R):
                        count(u, r, True)
                for r in range(R):
                    last = count(NT // R - 1, r, False)
                ch.link(last)
                ch.link(v.scalar_tensor_tensor(cnt[:], blk[:], float(EP), cnt[:], ALU.mult, ALU.add))
                v.tensor_copy(rp[:], cnt[:]).then_inc(rp_ok, 1)

            @block.scalar
            def _(act):
                s = nc.scalar
                act.dma_start(wn[:], ins["L0_gnn_W"].rearrange("(k p) i -> p k i", p=128)).then_inc(w_in, 16)
                for q, nm in enumerate(("L0_gnn_a_src", "L0_gnn_a_dst")):
                    act.dma_start(aa[:, :, q:q + 1], ins[nm].rearrange("h (d o) -> (h d) o", o=1).rearrange("(k p) o -> p k o", p=128), allow_slow_non_contiguous=True).then_inc(w_in, 16)
                act.dma_start(wx[:, :, 0:D], ins["L0_gnn_WT"].rearrange("(k p) o -> p k o", p=128), allow_slow_non_contiguous=True).then_inc(w_in, 16)
                act.wait_ge(stats, 1)
                s.activation(rstd[:], rstd[:], ACT.Sqrt).then_inc(sq, 1)
                act.wait_ge(w_in, 64)
                act.wait_ge(wa_ok, 1)
                s.activation(wx[:, :, D:D + 2 * H], pW[:, :, 0:2 * H], ACT.Copy).then_inc(wx_ok, 1)
                act.wait_ge(rst, 1)

                def normed(t, b):
                    tc = bass.ds(t, 1)
                    s.activation(xn[:, b, :], x[:, tc, :].rearrange("p a c -> p (a c)"), ACT.Identity,
                                 bias=nbias[:, tc], scale=rstd[:, tc]).then_inc(xn_ok, 1)

                def turned(t, b):
                    act.wait_ge(t_ok, t + 1)
                    s.activation(xnT[:, b, :, :], pT[b][:, :, 0:P], ACT.Copy).then_inc(xnT_ok, 1)

                def rows(u, b, early):
                    act.wait_ge(h_ok, 2 * u + (b + 1))
                    if not early:
                        act.sem_inc(pace, 1)
                        act.wait_ge(row_out[b], 16 * (u + 1))
                    s.activation(row[:, b, 0:H * VW].rearrange("p (h c) -> p h c", h=H)[:, :, 0:HD],
                                 pH[b][:, 0:D].rearrange("p (h c) -> p h c", h=H), ACT.Copy)
                    s.activation(row[:, b, H * VW:RW], pH[b][:, D:D + 2 * H], ACT.Copy).then_inc(row_ok, 1)

                def group(u, first, last_group):
                    for b in range(2):
                        if b == 0 or not last_group:
                            normed(2 * u + (b + 1), 1 - b)
                        turned(2 * u + b, b)
                        if b == 1:
                            rows(u, 0, first)
                        elif not first:
                            rows(u - 1, 1, False)
                for b in range(2):
                    act.sem_inc(row_out[b], 16)
                normed(0, 0)
                paired(act, NT // 2, group)
                rows(NT // 2 - 1, 1, False)

            @block.tensor
            def _(pe):
                t_ = nc.tensor
                pe.wait_ge(below_ok, 1)
                bl = below[:, :].rearrange("p (n t) -> p t n", t=NT)
                for t in range(NT):
                    last = t_.matmul(pC[:, t:t + 1], bl[:, t, :], ones[:], start=True, stop=True)
                last.then_inc(counted, 1)
                pe.wait_ge(ablk_ok, 1)
                for i in range(2):
                    for k in range(2):
                        last = t_.matmul(pW[:, i, 0:2 * H], wn[:, k, i * 128:(i + 1) * 128], ablk[:, k, :], start=(k == 0), stop=(k == 1))
                last.then_inc(wa_ok, 1)
                pe.wait_ge(wx_ok, 1)

                def turn(t, b):
                    pe.wait_ge(xn_ok, t + 1)
                    for k in range(2):
                        last = t_.transpose(pT[b][:, k, 0:P], xn[:, b, k * 128:(k + 1) * 128], K["ident"][0:P, 0:P])
                    last.then_inc(t_ok, 1)

                def product(t, b, early):
                    pe.wait_ge(xnT_ok, t + 1)
                    if not early:
                        pe.sem_inc(pace, 1)
                        pe.wait_ge(row_ok, t - 1)
                    for k in range(2):
                        last = t_.matmul(pH[b][:, 0:D + 2 * H], xnT[:, b, k, :], wx[:, k, :], start=(k == 0), stop=(k == 1))
                    last.then_inc(h_ok, 1)

                def group(u, first, last_group):
                    for b in range(2):
                        if b == 0 or not last_group:
                            turn(2 * u + (b + 1), 1 - b)
                        product(2 * u + b, b, first)
                turn(0, 0)
                paired(pe, NT // 2, group)


def order(nc, K, ins, dr):
    with ExitStack() as stack:
        m = Mem(nc, stack)
        OHW = NT * NB
        rec = m.sb("o_rec", [P, NT, 4], I32)
        nxt = m.sb("o_nxt", [P, NT], I32)
        rpi = m.sb("o_rpi", [P, NT], I32)
        deg = m.sb("o_deg", [P, NT])
        bkt = m.sb("o_bkt", [P, NT])
        hot = m.sb("o_hot", [P, NT, NB])
        tot = m.sb("o_tot", [P, NB, NT])
        exc = m.sb("o_exc", [P, NB, NT])
        rank = m.sb("o_rank", [P, NT, NB])
        posf = m.sb("o_posf", [P, NT])
        pos = m.sb("o_pos", [P, NT], I32)
        zero = m.sb("o_zero", [P, OHW])
        R = 5
        idx = [m.sb(f"o_idx{r}", [P, 1], I32) for r in range(R)]
        srow = [m.sb(f"o_srow{r}", [P, 4], I32) for r in range(R)]
        dT = m.sb("o_dT", [QT, Q])
        dmax = m.sb("o_dmax", [QT, 1])
        ci = m.sb("o_ci", [QT, 1], I32)
        cf = m.sb("o_cf", [QT, 1])
        tail = m.sb("o_tail", [1, 4], I32)
        ctf = m.sb("o_ctf", [1, QT + 1])
        pR = m.ps("o_pR", [P, 512])
        pTt = m.ps("o_pTt", [P, 512])
        pD = m.ps("o_pD", [QT, Q])
        pC = m.ps("o_pC", [1, 64])

        r_in = m.sem("o_r_in"); vch = m.sem("o_vch"); hot_ok = m.sem("o_hot_ok"); mm_ok = m.sem("o_mm_ok"); taken = m.sem("o_taken")
        ready = m.sem("o_ready"); sent = [m.sem(f"o_sent{r}") for r in range(R)]; pads = m.sem("o_pads"); pt_in = m.sem("o_pt_in")
        deg_ok = m.sem("o_deg_ok"); dT_ok = m.sem("o_dT_ok"); cnt_ok = m.sem("o_cnt_ok"); pre_ok = m.sem("o_pre_ok"); pace = m.sem("o_pace")
        iota_ok = m.sem("o_iota_ok"); all_sent = m.sem("o_all_sent")
        cols = [(a, min(a + 8, NT)) for a in range(0, NT, 8)]

        with nc.Block() as block:
            @block.sync
            def _(sp):
                sp.dma_start(rpi[:], dr["rp"][:, 0:N].rearrange("o (p t) -> (o p) t", t=NT)).then_inc(r_in, 16)
                sp.dma_start(nxt[:], dr["rp"][:, 1:N + 1].rearrange("o (p t) -> (o p) t", t=NT)).then_inc(r_in, 16)
                sp.dma_start(dr["noderec"][N:NPAD, :], K["padrec"][:]).then_inc(pads, 16)
                sp.wait_ge(pads, 16)
                for r in range(R):
                    sp.wait_ge(sent[r], 16 * (NT // R))
                sp.dma_start(K["pt"][:], dr["noderec"].rearrange("(t q) c -> q t c", q=Q)).then_inc(pt_in, 16)
                sp.wait_ge(pt_in, 16)

            @block.gpsimd
            def _(pool):
                pool.iota(rec[:, :, 0], pattern=[[1, NT]], base=0, channel_multiplier=NT).then_inc(iota_ok, 1)

                def scatter(u, r):
                    pool.wait_ge(ready, u * R + (r + 1))
                    pool.sem_inc(pace, 1)
                    pool.indirect_dma_start(out=dr["noderec"], out_offset=bass.IndirectOffsetOnAxis(ap=idx[r][:, 0:1], axis=0),
                                            in_=srow[r][:], in_offset=None).then_inc(sent[r], 16)
                with pool.Fori(0, NT // R) as u:
                    for r in range(R):
                        scatter(u, r)

            @block.vector
            def _(dve):
                v = nc.vector
                ch = Chain(dve, vch)
                v.memset(zero[:], 0.0)
                dve.wait_ge(r_in, 32)
                dve.wait_ge(iota_ok, 1)
                ch.link(v.tensor_tensor(deg[:], nxt[:], rpi[:], ALU.subtract))
                v.tensor_copy(rec[:, :, 1], rpi[:])
                v.tensor_copy(rec[:, :, 2], deg[:])
                ch.link(v.tensor_copy(rec[:, :, 3], deg[:]))
                ch.link(v.tensor_scalar(bkt[:], deg[:], float(NB - 1), None, ALU.min))
                v.tensor_tensor(hot[:], over(bkt[:], 2, NB), over(K["iota64"][0:P, :], 1, NT), ALU.is_equal).then_inc(hot_ok, 1)
                for j, (a, b) in enumerate(cols):
                    w = (b - a) * NB
                    dve.wait_ge(mm_ok, j + 1)
                    v.tensor_copy(rank[:, a:b, :].rearrange("p t b -> p (t b)"), pR[:, 0:w])
                    v.tensor_copy(tot[:, :, a:b].rearrange("p b t -> p t b"), pTt[:, 0:w].rearrange("p (t b) -> p t b", b=NB)).then_inc(taken, 1)
                dve.wait_ge(taken, len(cols))
                flat = "p b t -> p (b t)"
                ch.link(v.tensor_tensor_scan(exc[:].rearrange(flat), tot[:].rearrange(flat), zero[:], 0.0, ALU.add, ALU.add))
                ch.link(v.tensor_tensor(exc[:].rearrange(flat), exc[:].rearrange(flat), tot[:].rearrange(flat), ALU.subtract))
                ch.link(v.tensor_tensor(rank[:], rank[:], exc[:].rearrange("p b t -> p t b"), ALU.add))
                ch.link(v.tensor_tensor(rank[:], rank[:], hot[:], ALU.mult))
                ch.link(v.reduce_sum(posf[:], rank[:], axis=AX))
                ch.link(v.tensor_copy(pos[:], posf[:]))

                def stage(u, first):
                    for r in range(R):
                        t = u * R + r
                        if not first:
                            dve.wait_ge(sent[r], 16 * u)
                            dve.sem_inc(pace, 1)
                        v.tensor_copy(srow[r][:], rec[:, bass.ds(t, 1), :].rearrange("p a c -> p (a c)"))
                        v.tensor_copy(idx[r][:], pos[:, bass.ds(t, 1)]).then_inc(ready, 1)
                peeled(dve, NT // R, stage)
                dve.wait_ge(pt_in, 16)
                v.tensor_copy(K["rp"][:], K["pt"][:, :, 1])
                v.tensor_copy(K["deg"][:], K["pt"][:, :, 2]).then_inc(deg_ok, 1)
                dve.wait_ge(dT_ok, 1)
                ch.link(v.reduce_max(dmax[:], pD[:], axis=AX))
                ch.link(v.tensor_scalar(ci[:], dmax[:], float(C - 1), None, ALU.add))
                ch.link(v.tensor_scalar(ci[:], ci[:], CLOG, None, ALU.arith_shift_right))
                ch.link(v.tensor_copy(cf[:], ci[:]))
                v.tensor_scalar(cf[:], cf[:], 2.0, None, ALU.max).then_inc(cnt_ok, 1)
                dve.wait_ge(pre_ok, 1)
                v.tensor_copy(K["ct"][:, 0:QT], pC[:, 0:QT])
                ch.link(v.tensor_scalar(tail[:, 0:1], pC[:, QT:QT + 1], 3.0, None, ALU.add))
                ch.link(v.tensor_scalar(tail[:, 1:2], tail[:, 0:1], 2, None, ALU.arith_shift_right))
                v.tensor_scalar(K["ct"][:, QT + 1:QT + 2], tail[:, 1:2], -2.0, None, ALU.add)
                ch.link(v.tensor_scalar(K["ct"][:, QT:QT + 1], tail[:, 1:2], 4.0, None, ALU.mult))

            @block.tensor
            def _(pe):
                t_ = nc.tensor
                pe.wait_ge(hot_ok, 1)
                for j, (a, b) in enumerate(cols):
                    w = (b - a) * NB
                    h = hot[:, a:b, :].rearrange("p t b -> p (t b)")
                    if j:
                        pe.wait_ge(taken, j)
                    t_.matmul(pR[:, 0:w], K["tri"][0:P, 0:P], h, start=True, stop=True)
                    t_.matmul(pTt[:, 0:w], K["ones"][0:P, 0:P], h, start=True, stop=True).then_inc(mm_ok, 1)
                pe.wait_ge(deg_ok, 1)
                t_.transpose(pD[:], K["deg"][:], K["ident"][:]).then_inc(dT_ok, 1)
                pe.wait_ge(cnt_ok, 1)
                t_.matmul(pC[0:1, 0:QT + 1], cf[:], K["tri"][0:QT, 0:QT + 1], start=True, stop=True).then_inc(pre_ok, 1)


def groups(eng, K):
    return eng.value_load(K["ct"][0:1, QT + 1:QT + 2], min_val=1, max_val=CMAX // 4 - 3)


def edge_index(nc, K, eidx):
    with ExitStack() as stack:
        m = Mem(nc, stack)
        T = lambda n: m.sem("x_" + n)
        start = m.sb("x_start", [1, QT])
        v_ = m.sb("x_v", [Q, QT])
        dv = m.sb("x_dv", [Q, QT])
        dvT = m.sb("x_dvT", [QT, Q])
        lo = m.sb("x_lo", [QT, 1])
        nb_i = m.sb("x_nb", [1, 1], I32)
        iota = m.sb("x_iota", [Q, BLK])
        edge = m.sb("x_edge", [Q, BLK])
        step = m.sb("x_step", [QT, BLK])
        iota_ok = T("iota_ok"); s_ok = T("s_ok"); b_ok = T("b_ok"); d_ok = T("d_ok"); t_ok = T("t_ok"); nb_ok = T("nb_ok")
        step_ok = T("step_ok"); e_ok = T("e_ok"); vch = T("vch"); bch = T("bch"); pace = T("pace")
        pB = m.ps("x_pB", [Q, QT])
        pV = m.ps("x_pV", [QT, Q])
        pL = m.ps("x_pL", [QT, 1])
        pE = m.ps("x_pE", [Q, BLK])
        blocks = lambda eng: eng.value_load(nb_i[0:1, 0:1], min_val=1, max_val=-(-CMAX // BLK))
        with nc.Block() as block:
            @block.gpsimd
            def _(pool):
                pool.iota(iota[:], pattern=[[1, BLK]], base=0, channel_multiplier=0, allow_small_or_imprecise_dtypes=True).then_inc(iota_ok, 1)

            @block.tensor
            def _(pe):
                t_ = nc.tensor
                pe.wait_ge(s_ok, 1)
                t_.matmul(pB[:], K["ones"][0:1, :], start[:], start=True, stop=True)
                t_.matmul(pL[:], start[:], K["ones"][0:1, 0:1], start=True, stop=True).then_inc(b_ok, 1)
                pe.wait_ge(d_ok, 1)
                t_.transpose(pV[:], dv[:], K["ident"][:]).then_inc(t_ok, 1)
                pe.wait_ge(nb_ok, 1)
                with pe.Fori(0, blocks(pe)) as k:
                    pe.wait_ge(step_ok, k + 1)
                    t_.matmul(pE[:], dvT[:], step[:], start=True, stop=True).then_inc(e_ok, 1)

            @block.vector
            def _(dve):
                v = nc.vector
                ch = Chain(dve, vch)
                v.tensor_copy(start[:], K["ct"][0:1, 0:QT]).then_inc(s_ok, 1)
                ch.link(v.tensor_scalar(nb_i[:], K["ct"][0:1, QT:QT + 1], float(BLK - 1), None, ALU.add))
                ch.link(v.tensor_scalar(nb_i[:], nb_i[:], BLOG, None, ALU.arith_shift_right))
                dve.sem_inc(nb_ok, 1)
                dve.wait_ge(b_ok, 1)
                ch.link(v.scalar_tensor_tensor(v_[:], pB[:], -float(C), K["rp"][:], ALU.mult, ALU.add))
                v.tensor_copy(lo[:], pL[:])
                v.tensor_copy(dv[:, 0:1], v_[:, 0:1])
                v.tensor_tensor(dv[:, 1:QT], v_[:, 1:QT], v_[:, 0:QT - 1], ALU.subtract).then_inc(d_ok, 1)
                dve.wait_ge(iota_ok, 1)
                v.tensor_scalar(edge[:], iota[:], float(C), None, ALU.mult)
                dve.wait_ge(t_ok, 1)
                ch.link(v.tensor_copy(dvT[:], pV[:]))
                NL = 4
                with dve.Fori(0, blocks(dve)) as k:
                    bc = Chain(dve, bch, NL * k)
                    v.tensor_scalar(step[:], iota[0:QT, :], lo[:], None, ALU.is_ge).then_inc(step_ok, 1)
                    dve.wait_ge(e_ok, k + 1)
                    dve.sem_inc(pace, 1)
                    e = eidx[:, bass.ds(k * BLK, BLK)]
                    bc.link(v.tensor_tensor(e, pE[:], edge[:], ALU.add))
                    bc.link(v.tensor_scalar(e, e, float(E - 1), None, ALU.min))
                    bc.link(v.tensor_scalar(lo[:], lo[:], -float(BLK), None, ALU.add))
                    bc.link(v.tensor_scalar(edge[:], edge[:], float(C * BLK), None, ALU.add))


def graph(nc, K, ins, dr, layer):
    first_layer = layer == 0
    rows_d, agg_d = dr[f"rows{layer}"], dr[f"agg{layer}"]
    L = f"g{layer}_"
    with ExitStack() as stack:
        m = Mem(nc, stack)
        if first_layer:
            eidx = m.sb(L + "eidx", [Q, -(-CMAX // BLK) * BLK])
            edge_index(nc, K, eidx)
        R = 4
        HR = 4
        DW = RW if first_layer else H
        dall = m.sb(L + "dall", [Q, QT, DW if first_layer else D])
        sdst = m.sb(L + "sdst", [Q, QT, H])
        nidx = [m.sb(f"{L}nidx{r}", [Q, 1], I32) for r in range(HR)]
        nrow = m.sb(L + "nrow", [Q, HR, DW])
        orow = m.sb(L + "orow", [Q, HR, D])
        recs = m.sb(L + "recs", [Q, R, REC])
        rows = m.sb(L + "rows", [Q, R, C, RW])
        msg = m.sb(L + "msg", [Q, 2, C, H * VW])
        al = m.sb(L + "al", [Q, 2, (C + 1) * H])
        part = m.sb(L + "part", [Q, C * H])
        lowest = m.sb(L + "lowest", [Q, H])
        mask = m.sb(L + "mask", [Q, C])
        left = m.sb(L + "left", [Q, 1])
        dd = m.sb(L + "dd", [Q, 2, (C + 1) * H])
        pp = m.sb(L + "pp", [Q, 2, (C + 1) * H])
        acc = m.sb(L + "acc", [Q, H * VW])
        den = m.sb(L + "den", [Q, H])
        pA = m.ps(L + "pA", [Q, 2, 512])
        if first_layer:
            ew = m.sb(L + "ew", [REC + 1, C, D])
            prod = m.sb(L + "prod", [Q, 2, C * D])
            recT = m.sb(L + "recT", [REC + 1, 2, Q])
            pE = m.ps(L + "pE", [Q, C * D])
            pRT = m.ps(L + "pRT", [REC, 2, 512])

        S = lambda n: m.sem(L + n)
        nready = S("nready"); ngot = [S(f"ngot{r}") for r in range(HR)]
        rec_in = [S(f"rec_in{r}") for r in range(R)]; rows_in = [S(f"rows_in{r}") for r in range(R)]
        rows_ok = S("rows_ok"); w_in = S("w_in"); w_zero = S("w_zero"); pace = S("pace"); vch = S("vch"); tch = S("tch"); cch = S("cch"); och = S("och"); uch = S("uch")
        recT_ps = S("recT_ps"); recT_ok = S("recT_ok"); enc_ok = S("enc_ok"); enc_free = S("enc_free")
        dd_ok = S("dd_ok"); pp_ok = S("pp_ok"); msg_ok = S("msg_ok"); agg_ok = S("agg_ok")
        oready = S("oready"); oput = [S(f"oput{r}") for r in range(HR)]
        NG = QT // HR
        TAIL = QT - NG * HR

        if first_layer:
            ridx = [m.sb(f"{L}ridx{r}", [Q, 1], I32) for r in range(R)]
            ridx_ok = S("ridx_ok"); rec_free = S("rec_free"); rec_put = [S(f"rec_put{r}") for r in range(R)]
        with nc.Block() as block:
            src_d = rows_d if first_layer else dr["sv1"]

            @block.gpsimd
            def _(pool):
                def gather(u, r):
                    pool.wait_ge(nready, u * HR + (r + 1))
                    pool.sem_inc(pace, 1)
                    pool.indirect_dma_start(out=nrow[:, r, :], out_offset=None, in_=src_d,
                                            in_offset=bass.IndirectOffsetOnAxis(ap=nidx[r][:, 0:1], axis=0)
                                            ).then_inc(ngot[r], 16)
                with pool.Fori(0, NG) as u:
                    for r in range(HR):
                        gather(u, r)
                for r in range(TAIL):
                    gather(NG, r)

            @block.vector
            def _(dve):
                v = nc.vector

                def put_index(t, r):
                    v.tensor_copy(nidx[r][:], K["pt"][:, bass.ds(t, 1), 0]).then_inc(nready, 1)

                def keep(u, r, more):
                    t = u * HR + r
                    dve.wait_ge(ngot[r], 16 * u + 16)
                    dve.sem_inc(pace, 1)
                    row = nrow[:, r:r + 1, :]
                    if first_layer:
                        v.tensor_copy(dall[:, bass.ds(t, 1), :], row)
                    else:
                        v.tensor_copy(sdst[:, bass.ds(t, 1), :], row)
                    if more:
                        put_index(t + HR, r)
                for r in range(HR):
                    put_index(r, r)
                with dve.Fori(0, NG - 1) as u:
                    for r in range(HR):
                        keep(u, r, True)
                for r in range(HR):
                    keep(NG - 1, r, r < TAIL)
                for r in range(TAIL):
                    keep(NG, r, False)
                Chain(dve, vch).link(v.memset(lowest[:], -BIG / 10))
                if first_layer:
                    v.tensor_copy(sdst[:], dall[:, :, H * VW + H:RW])

        with nc.Block() as block:
            @block.sync
            def _(sp):
                n2 = groups(sp, K)
                if first_layer:
                    sp.wait_ge(w_zero, 1)
                    for j in range(C):
                        sp.dma_start(ew[C + 3 * j:C + 3 * j + 3, j, :], ins["L0_gnn_edge_WT"]).then_inc(w_in, 16)
                        sp.dma_start(ew[REC:REC + 1, j, :], ins["L0_gnn_edge_b"].unsqueeze(0)).then_inc(w_in, 16)

                def load(u, r):
                    sp.dma_start(recs[:, r, :], dr["slots"][bass.ds(4 * u + r, 1), :, :].rearrange("a q c -> (a q) c")).then_inc(rec_in[r], 16)

                def relay(u, r):
                    sp.wait_ge(rows_in[r], 16 * C * (u + 1))
                    sp.sem_inc(rows_ok, 1)
                if not first_layer:
                    for r in range(R):
                        load(0, r)
                    with sp.Fori(0, n2 + 1) as u:
                        for r in range(R):
                            relay(u, r)
                            load(u + 1, r)
                    for r in range(R):
                        relay(n2 + 1, r)

                def keep(u, first):
                    for r in range(R):
                        relay(u, r)
                        sp.dma_start(dr["slots"][bass.ds(4 * u + r, 1), :, :].rearrange("a q c -> (a q) c"), recs[:, r, :]).then_inc(rec_put[r], 16)
                        sp.wait_ge(recT_ps, 4 * u + (r + 1))
                        sp.sem_inc(pace, 1)
                        if r > 0:
                            sp.wait_ge(rec_put[r - 1], 16 * u + 16)
                            sp.sem_inc(rec_free, 1)
                        elif not first:
                            sp.wait_ge(rec_put[R - 1], 16 * u)
                            sp.sem_inc(rec_free, 1)
                if first_layer:
                    peeled(sp, n2 + 2, keep)
                    for r in range(R):
                        sp.wait_ge(rec_put[r], 16 * (n2 + 2))
                        sp.sem_inc(pace, 1)

            @block.gpsimd
            def _(pool):
                n2 = groups(pool, K)

                def record(u, r, early):
                    u, r = u + r // R, r % R
                    pool.wait_ge(ridx_ok, 4 * u + (r + 1))
                    pool.sem_inc(pace, 1)
                    if not early:
                        pool.wait_ge(rec_free, 4 * (u - 1) + (r + 1))
                        pool.sem_inc(pace, 1)
                    pool.indirect_dma_start(out=recs[:, r, :], out_offset=None, in_=dr["rec"],
                                            in_offset=bass.IndirectOffsetOnAxis(ap=ridx[r][:, 0:1], axis=0)
                                            ).then_inc(rec_in[r], 16)

                def gather(u, first, last_group):
                    for r in range(R):
                        pool.wait_ge(rec_in[r], 16 * u + 16)
                        pool.sem_inc(pace, 1)
                        if not first:
                            pool.wait_ge(msg_ok, 4 * (u - 1) + (r + 1))
                            pool.sem_inc(pace, 1)
                        for j in range(C):
                            pool.indirect_dma_start(out=rows[:, r, j, :], out_offset=None, in_=rows_d,
                                                    in_offset=bass.IndirectOffsetOnAxis(ap=recs[:, r, j:j + 1].bitcast(I32), axis=0)
                                                    ).then_inc(rows_in[r], 16)
                        if first_layer and (r < R - 2 or not last_group):
                            record(u, r + 2, first and r < 2)
                if first_layer:
                    record(0, 0, True)
                    record(0, 1, True)
                gather(0, True, False)
                with pool.Fori(1, n2 + 1) as u:
                    gather(u, False, False)
                gather(n2 + 1, False, True)

            @block.tensor
            def _(pe):
                t_ = nc.tensor
                n2 = groups(pe, K)

                def transpose(u, r):
                    u, r = u + r // R, r % R
                    pe.wait_ge(rec_in[r], 16 * u + 16)
                    t_.transpose(pRT[:, r % 2, 0:Q], recs[:, r, :], K["ident"][:]).then_inc(recT_ps, 1)

                def encode(i, b, first):
                    pe.wait_ge(recT_ok, i + 1)
                    if not first:
                        pe.wait_ge(enc_free, i)
                    for bank in range(C * D // 512):
                        cols = slice(bank * 512, (bank + 1) * 512)
                        last = t_.matmul(pE[:, cols], recT[:, b, :], ew[:].rearrange("p c d -> p (c d)")[:, cols], start=True, stop=True)
                    last.then_inc(enc_ok, 1)

                def aggregate(u, r):
                    pe.wait_ge(msg_ok, 4 * u + (r + 1))
                    for j in range(C):
                        last = t_.matmul(pA[:, r % 2, 0:H * VW], K["ident"][:], msg[:, r % 2, j, :], start=(j == 0), stop=(j == C - 1))
                    last.then_inc(agg_ok, 1)

                def group(u, first, last_group):
                    for r in range(R):
                        if first_layer:
                            if r < R - 2 or not last_group:
                                transpose(u, r + 2)
                            if r < R - 1 or not last_group:
                                encode(4 * u + (r + 1), (r + 1) % 2, False)
                        if r > 0:
                            aggregate(u, r - 1)
                        elif not first:
                            aggregate(u - 1, R - 1)
                if first_layer:
                    pe.wait_ge(w_in, 32 * C)
                    transpose(0, 0)
                    transpose(0, 1)
                    encode(0, 0, True)
                group(0, True, False)
                with pe.Fori(1, n2 + 1) as u:
                    group(u, False, False)
                group(n2 + 1, False, True)
                aggregate(n2 + 1, R - 1)

            @block.scalar
            def _(act):
                s = nc.scalar
                n2 = groups(act, K)

                def index(u, r, early):
                    u, r = u + r // R, r % R
                    if not early:
                        act.wait_ge(rec_in[r], 16 * u)
                        act.sem_inc(pace, 1)
                    s.activation(ridx[r][:], eidx[:, bass.ds(4 * u + r, 1)], ACT.Copy).then_inc(ridx_ok, 1)

                def record(i, b, early):
                    act.wait_ge(recT_ps, i + 1)
                    if not early:
                        act.sem_inc(pace, 1)
                        act.wait_ge(enc_ok, i - 1)
                    s.activation(recT[0:REC, b, :], pRT[:, b, 0:Q], ACT.Copy).then_inc(recT_ok, 1)

                def encoding(i, b):
                    act.wait_ge(enc_ok, i + 1)
                    act.sem_inc(pace, 1)
                    s.activation(prod[:, b, :], pE[:], ACT.Relu).then_inc(enc_free, 1)

                def group(u, last_group):
                    for r in range(R):
                        i = 4 * u + r
                        if first_layer:
                            if r < R - 2 or not last_group:
                                record(4 * u + (r + 2), r % 2, False)
                            if r < R - 1 or not last_group:
                                encoding(4 * u + (r + 1), (r + 1) % 2)
                        act.wait_ge(dd_ok, 4 * u + (r + 1))
                        s.activation(pp[:, r % 2, :], dd[:, r % 2, :], ACT.Exp).then_inc(pp_ok, 1)
                        if first_layer and not last_group:
                            index(u + 1, r, False)
                if first_layer:
                    act.wait_ge(w_zero, 2)
                    for r in range(R):
                        index(0, r, True)
                    record(0, 0, True)
                    record(1, 1, True)
                    encoding(0, 0)
                group(0, False)
                with act.Fori(1, n2 + 1) as u:
                    group(u, False)
                group(n2 + 1, True)

            @block.vector
            def _(dve):
                v = nc.vector
                if first_layer:
                    v.memset(ew[:], 0.0).then_inc(w_zero, 1)
                    v.memset(recT[:], 1.0).then_inc(w_zero, 1)
                NL = 8 if first_layer else 5
                TL = 4
                heads = lambda ap: ap.rearrange("p (c h) -> p c h", h=H)
                row_of = lambda ap: ap.rearrange("p a h -> p (a h)")
                iota = K["iota64"][:, 0:C]
                acc3 = acc[:].rearrange("p (h c) -> p h c", h=H)

                def messages(i):
                    b2, b4 = bass.ds(i % 2, 1), bass.ds(i % R, 1)
                    dve.wait_ge(pp_ok, i + 1)
                    dve.sem_inc(pace, 1)
                    pv = heads(row_of(pp[:, b2, 0:C * H]))
                    row4 = rows[:, b4, :, 0:H * VW].rearrange("p a c (h w) -> p (a c) h w", h=H)
                    v.tensor_tensor(msg[:, b2, :, :].rearrange("p a c (h w) -> p (a c) h w", h=H), row4, over(pv, 3, VW), ALU.mult).then_inc(msg_ok, 1)

                def rescale(i):
                    dve.wait_ge(uch, 2 * i + 3)
                    dve.sem_inc(pace, 1)
                    v.tensor_tensor(acc3, acc3, over(row_of(pp[:, bass.ds(i % 2, 1), C * H:]), 2, VW), ALU.mult).then_inc(uch, 1)

                def gather_in(i):
                    dve.wait_ge(agg_ok, i + 1)
                    dve.sem_inc(pace, 1)
                    dve.wait_ge(uch, 2 * i + 4)
                    dve.sem_inc(pace, 1)
                    v.tensor_tensor(acc[:], acc[:], row_of(pA[:, bass.ds(i % 2, 1), 0:H * VW]), ALU.add).then_inc(uch, 1)

                def finish(t, i):
                    dve.wait_ge(uch, 2 * i + 5)
                    dve.sem_inc(pace, 1)
                    tc = Chain(dve, tch, t * TL)
                    tc.link(v.tensor_scalar(den[:], acc3[:, :, HD], 1e-10, None, ALU.max))
                    tc.link(v.reciprocal(den[:], den[:]))
                    tc.link(v.tensor_tensor(dall[:, bass.ds(t, 1), 0:D].rearrange("p a (h c) -> p (a h) c", h=H),
                                            acc3[:, :, 0:HD], over(den[:], 2, HD), ALU.mult))
                    tc.link(v.memset(acc[:], 0.0))

                def chunk(t, i, opens, closes=None):
                    start = isinstance(i, int) and i == 0
                    b2 = bass.ds(i % 2, 1)
                    ch = Chain(dve, cch, i * NL)
                    alb = row_of(al[:, b2, :])
                    mnb = row_of(al[:, bass.ds((i + 1) % 2, 1), C * H:])
                    sc = heads(alb[:, 0:C * H])
                    sd = over(row_of(sdst[:, bass.ds(t, 1), :]), 1, C)
                    src = rows[:, bass.ds(i % R, 1), :, H * VW:H * VW + H].rearrange("p a c w -> p (a c) w")
                    if opens:
                        if not start:
                            dve.wait_ge(dd_ok, i)
                            dve.sem_inc(pace, 1)
                        v.tensor_copy(alb[:, C * H:], lowest[:])
                        Chain(dve, och, t).link(v.tensor_copy(left[:], K["deg"][:, bass.ds(t, 1)]))
                    v.tensor_scalar(mask[:], iota, left[:], -BIG, ALU.is_ge, ALU.mult)
                    if first_layer:
                        dst = dall[:, bass.ds(t, 1), 0:H * VW].rearrange("p a (h c) -> p (a h) c", h=H)[:, :, 0:HD]
                        pr = row_of(prod[:, b2, :])
                        p4 = pr.rearrange("p (c h w) -> p c h w", c=C, h=H)
                        dve.wait_ge(enc_free, i + 1)
                        dve.sem_inc(pace, 1)
                        ch.link(v.tensor_tensor(p4, p4, over(dst, 1, C), ALU.mult), wait=False)
                    ssc = heads(part[:]) if first_layer else sc
                    dve.wait_ge(rows_ok, i + 1)
                    dve.sem_inc(pace, 1)
                    ch.link(v.tensor_tensor(ssc, src, sd, ALU.add), wait=False)
                    if first_layer:
                        ch.wait(1)
                        ch.link(v.reduce_sum(alb[:, 0:C * H], pr.rearrange("p (g c) -> p g c", c=HD), axis=AX), wait=False)
                    ch.wait(2 if first_layer else 1)
                    ch.link(v.tensor_tensor(ssc, ssc, over(mask[:], 2, H), ALU.add), wait=False)
                    if first_layer:
                        if not start:
                            rescale(i - 1)
                        ch.wait()
                        ch.link(v.tensor_tensor(sc, sc, ssc, ALU.add), wait=False)
                    ch.wait()
                    ch.link(v.scalar_tensor_tensor(sc, sc, 0.2, sc, ALU.mult, ALU.max))
                    ch.link(v.reduce_max(mnb, alb.rearrange("p (c h) -> p h c", h=H), axis=AX), wait=False)
                    if first_layer and not start:
                        gather_in(i - 1)
                    ch.wait()
                    v.tensor_tensor(heads(row_of(dd[:, b2, :])), heads(alb), over(mnb, 1, C + 1), ALU.subtract).then_inc(dd_ok, 1)
                    ch.link(v.tensor_scalar(left[:], left[:], -float(C), None, ALU.add), wait=False)
                    assert ch.n == NL, ch.n
                    if first_layer:
                        if closes is not None:
                            finish(closes, i - 1)
                        messages(i)
                    else:
                        if not start:
                            rescale(i - 1)
                        messages(i)
                        if not start:
                            gather_in(i - 1)
                        if closes is not None:
                            finish(closes, i - 1)
                    ch.wait()

                def bounds(t):
                    return (dve.value_load(K["ct"][0:1, bass.ds(t, 1)], min_val=0, max_val=CMAX - 2),
                            dve.value_load(K["ct"][0:1, bass.ds(t + 1, 1)], min_val=2, max_val=CMAX))

                v.memset(acc[:], 0.0).then_inc(uch, 3)
                chunk(0, 0, True)
                with dve.Fori(0, QT - 1) as t:
                    lo, hi = bounds(t)
                    with dve.Fori(lo + 1, hi) as i:
                        chunk(t, i, False)
                    chunk(t + 1, hi, True, closes=t)
                lo, hi = bounds(QT - 1)
                with dve.Fori(lo + 1, hi) as i:
                    chunk(QT - 1, i, False)
                rescale(hi - 1)
                gather_in(hi - 1)
                finish(QT - 1, hi - 1)

        with nc.Block() as block:
            @block.gpsimd
            def _(pool):
                def scatter(u, r):
                    pool.wait_ge(oready, u * HR + (r + 1))
                    pool.sem_inc(pace, 1)
                    pool.indirect_dma_start(out=agg_d, out_offset=bass.IndirectOffsetOnAxis(ap=nidx[r][:, 0:1], axis=0),
                                            in_=orow[:, r, :], in_offset=None).then_inc(oput[r], 16)
                with pool.Fori(0, NG) as u:
                    for r in range(HR):
                        scatter(u, r)
                for r in range(TAIL):
                    scatter(NG, r)
                for r in range(HR):
                    pool.wait_ge(oput[r], 16 * (NG + (r < TAIL)))

            @block.vector
            def _(dve):
                v = nc.vector

                def stage(u, r, first):
                    t = u * HR + r
                    if not first:
                        dve.wait_ge(oput[r], 16 * u)
                        dve.sem_inc(pace, 1)
                    v.tensor_copy(orow[:, r:r + 1, :], dall[:, bass.ds(t, 1), 0:D])
                    v.tensor_copy(nidx[r][:], K["pt"][:, bass.ds(t, 1), 0]).then_inc(oready, 1)

                def group(u, first):
                    for r in range(HR):
                        stage(u, r, first)
                peeled(dve, NG, group)
                for r in range(TAIL):
                    stage(NG, r, False)


def paired(eng, n, body):
    body(0, True, False)
    with eng.Fori(1, n - 1) as u:
        body(u, False, False)
    body(n - 1, False, True)


def slice_ffn(nc, K, ins, dr):
    with ExitStack() as stack:
        m = Mem(nc, stack)
        S = lambda n: m.sem("f_" + n)
        INNER = FH * G
        NU = NT // 2
        x1 = m.sb("f_x1", [P, NT, D])
        swT = m.sb("f_swT", [128, 4, NT, P])
        bias = m.sb("f_bias", [P, D])
        norm = Norm(m, "f")
        wfx = m.sb("f_wfx", [128, 2, INNER])
        wout = m.sb("f_wout", [G, FH, D])
        wc = m.sb("f_wc", [128, 2, INNER])
        bc = m.sb("f_bc", [P, INNER])
        mm = m.sb("f_mm", [128, 4, D])
        bfx = m.sb("f_bfx", [1, INNER])
        wqkv = m.sb("f_wqkv", [G, 3, G])
        flat = lambda ap: ap.rearrange("p a c -> p (a c)")

        with ExitStack() as s2:
            m2 = Mem(nc, s2)
            T = lambda n: m2.sem("f0_" + n)
            agg = m2.sb("f0_agg", [P, 2, 5, D])
            wxT = m2.sb("f0_wxT", [G, FH, D])
            wsl = m2.sb("f0_wsl", [G, G])
            bx = m2.sb("f0_bx", [G, FH])
            bxb = m2.sb("f0_bxb", [G, FH, P])
            bsl = m2.sb("f0_bsl", [P, G])
            temp = m2.sb("f0_temp", [128, FH])
            pW = [m2.ps(f"f0_pW{k}", [128, 512]) for k in range(2)]
            pB = m2.ps("f0_pB", [P, 512])
            x_in = T("x_in"); a_in = [T("a_in0"), T("a_in1")]; w_in = T("w_in"); a_used = T("a_used")
            bxb_ok = T("bxb_ok"); w_ok = T("w_ok"); vch = T("vch"); stats = T("stats"); sq = T("sq"); done = T("done")
            with nc.Block() as block:
                @block.sync
                def _(sp):
                    sp.dma_start(x1[:], ins["x"].rearrange("(p t) c -> p t c", t=NT)).then_inc(x_in, 16)
                    sp.dma_start(bias[:], ins["L0_gnn_bias"].unsqueeze(0).broadcast_to([P, D])).then_inc(x_in, 16)
                    av = dr["agg0"][0:N, :].rearrange("(p t) c -> p t c", t=NT)
                    for g in range(NT // 5):
                        if g >= 2:
                            sp.wait_ge(a_used, g - 1)
                        sp.dma_start(agg[:, g % 2, :, :], av[:, 5 * g:5 * g + 5, :]).then_inc(a_in[g % 2], 16)

                @block.scalar
                def _(act):
                    act.dma_start(wxT[:], ins["L0_ffn_WxT"].rearrange("(h c) i -> c h i", c=G)).then_inc(w_in, 16)
                    act.dma_start(wsl[:], ins["L0_ffn_W_slice"]).then_inc(w_in, 16)
                    act.dma_start(bx[:], ins["L0_ffn_b_x"].rearrange("(h c) -> c h", c=G), allow_slow_non_contiguous=True).then_inc(w_in, 16)
                    act.dma_start(bsl[:], ins["L0_ffn_b_slice"].unsqueeze(0).broadcast_to([P, G])).then_inc(w_in, 16)
                    act.dma_start(temp[:], ins["L0_ffn_temperature"].rearrange("a h b c -> a (h b c)").broadcast_to([128, FH])).then_inc(w_in, 16)
                    act.dma_start(wfx[:], ins["L0_ffn_W_fx"].rearrange("(k p) o -> p k o", p=128)).then_inc(w_in, 16)
                    act.dma_start(wout[:], ins["L0_ffn_W_out"].rearrange("(h c) o -> c h o", c=G)).then_inc(w_in, 16)
                    act.dma_start(bfx[:], ins["L0_ffn_b_fx"].unsqueeze(0)).then_inc(w_in, 16)
                    for q, nm in enumerate("qkv"):
                        act.dma_start(wqkv[:, q, :], ins["L0_ffn_W_" + nm]).then_inc(w_in, 16)
                    act.wait_ge(w_in, 176)
                    act.wait_ge(stats, 1)
                    nc.scalar.activation(norm.rstd[:], norm.rstd[:], ACT.Sqrt).then_inc(sq, 1)

                @block.tensor
                def _(pe):
                    t_ = nc.tensor
                    pe.wait_ge(bxb_ok, 1)
                    for h in range(FH):
                        c = slice(h * G, (h + 1) * G)
                        for k in range(2):
                            t_.matmul(pW[k][:, c], wxT[:, h, k * 128:(k + 1) * 128], wsl[:], start=True, stop=True)
                        last = t_.matmul(pB[:, c], bxb[:, h, :], wsl[:], start=True, stop=True)
                    last.then_inc(w_ok, 1)

                @block.vector
                def _(dve):
                    v = nc.vector
                    ch = Chain(dve, vch)
                    dve.wait_ge(w_in, 176)
                    v.tensor_copy(bxb[:], over(bx[:], 2, P)).then_inc(bxb_ok, 1)
                    ch.link(v.tensor_scalar(temp[:], temp[:], 0.1, 5.0, ALU.max, ALU.min))
                    ch.link(v.reciprocal(temp[:], temp[:]))
                    dve.wait_ge(w_ok, 1)
                    g3 = lambda ap: ap.rearrange("p (h g) -> p h g", h=FH)
                    for k in range(2):
                        v.tensor_tensor(g3(wc[:, k, :]), g3(pW[k][:]), over(temp[:], 2, G), ALU.mult)
                    ch.link(v.tensor_tensor(g3(bc[:]), g3(pB[:]), over(bsl[:], 1, FH), ALU.add))
                    ch.link(v.tensor_tensor(g3(bc[:]), g3(bc[:]), over(temp[0:P, :], 2, G), ALU.mult))
                    dve.wait_ge(x_in, 32)
                    for g in range(NT // 5):
                        dve.wait_ge(a_in[g % 2], 16 * (g // 2 + 1))
                        xs = x1[:, 5 * g:5 * g + 5, :]
                        ch.link(v.tensor_tensor(xs, xs, over(bias[:], 1, 5), ALU.add))
                        v.tensor_tensor(xs, xs, agg[:, g % 2, :, :], ALU.add).then_inc(a_used, 1)
                    dve.wait_ge(a_used, NT // 5)
                    with dve.Fori(0, NT) as t:
                        norm.tile(v, t, x1[:, bass.ds(t, 1), :])
                    ch.link(v.memset(norm.a[:], 0.0))
                    norm.variance(v, ch, stats)
                    dve.wait_ge(sq, 1)
                    norm.scales(v, ch, done)

        st = m.sb("f_sums", [128, 4, D + 1])
        with ExitStack() as s2:
            m2 = Mem(nc, s2)
            T = lambda n: m2.sem("f1_" + n)
            xn = m2.sb("f1_xn", [P, 2, D + 1])
            xnT = m2.sb("f1_xnT", [128, 2, 2, P])
            lg = m2.sb("f1_lg", [P, 2, INNER])
            sw = m2.sb("f1_sw", [P, 2, INNER])
            red = m2.sb("f1_red", [P, 2, FH])
            pT = m2.ps("f1_pT", [128, 2, 2, 128])
            pL = [m2.ps(f"f1_pL{b}", [P, 512]) for b in range(2)]
            pS = m2.ps("f1_pS", [128, 4, 128])
            pTok = [m2.ps(f"f1_pTok{k}", [128, 512]) for k in range(4)]
            one = T("one"); xn_ok = T("xn_ok"); t_ok = T("t_ok"); xnT_ok = T("xnT_ok"); lg_ok = T("lg_ok"); sub_ok = T("sub_ok")
            exp_ok = T("exp_ok"); sw_ok = T("sw_ok"); s_ok = T("s_ok"); swT_ok = T("swT_ok"); vch = T("vch"); pace = T("pace"); tok = T("tok")
            g3 = lambda ap: ap.rearrange("p (h g) -> p h g", h=FH)
            with nc.Block() as block:
                @block.tensor
                def _(pe):
                    t_ = nc.tensor

                    def logits(t, b):
                        pe.wait_ge(xn_ok, t + 1)
                        for k in range(2):
                            last = t_.transpose(pT[:, b, k, 0:P], xn[:, b, k * 128:(k + 1) * 128], K["ident"][0:P, 0:P])
                        last.then_inc(t_ok, 1)
                        pe.wait_ge(xnT_ok, t + 1)
                        for k in range(2):
                            last = t_.matmul(pL[b][:], xnT[:, b, k, :], wc[:, k, :], start=(k == 0), stop=(k == 1))
                        last.then_inc(lg_ok, 1)

                    def group(u, first, last_group):
                        for b in range(2):
                            t = 2 * u + b
                            if b == 0 or not last_group:
                                logits(t + 1, 1 - b)
                            pe.wait_ge(sw_ok, t + 1)
                            for k in range(4):
                                t_.matmul(pTok[k][:, 0:D + 1], sw[:, b, k * 128:(k + 1) * 128], xn[:, b, :],
                                          start=first and b == 0, stop=last_group and b == 1, skip_group_check=True)
                            if not (first and b == 0):
                                pe.wait_ge(swT_ok, t)
                            for k in range(4):
                                last = t_.transpose(pS[:, k, 0:P], sw[:, b, k * 128:(k + 1) * 128], K["ident"][0:P, 0:P])
                            last.then_inc(s_ok, 1)
                    logits(0, 0)
                    paired(pe, NU, group)

                @block.scalar
                def _(act):
                    s = nc.scalar

                    def normed(t, b, early):
                        tc = bass.ds(t, 1)
                        if not early:
                            act.wait_ge(s_ok, t - 1)
                            act.sem_inc(pace, 1)
                        s.activation(xn[:, b, 0:D], flat(x1[:, tc, :]), ACT.Identity, bias=norm.nbias[:, tc],
                                     scale=norm.rstd[:, tc]).then_inc(xn_ok, 1)
                        act.wait_ge(t_ok, t + 1)
                        s.activation(xnT[:, b, :, :], pT[:, b, :, 0:P], ACT.Copy).then_inc(xnT_ok, 1)

                    def keep(t):
                        act.wait_ge(s_ok, t + 1)
                        act.sem_inc(pace, 1)
                        s.activation(swT[:, :, bass.ds(t, 1), :].rearrange("p k a c -> p (k a) c"), pS[:, :, 0:P], ACT.Copy).then_inc(swT_ok, 1)

                    def group(u, first, last_group):
                        for b in range(2):
                            t = 2 * u + b
                            if not (first and b == 0):
                                keep(t - 1)
                            if b == 0 or not last_group:
                                normed(t + 1, 1 - b, first and b == 0)
                            act.wait_ge(sub_ok, t + 1)
                            s.activation(lg[:, b, :], lg[:, b, :], ACT.Exp).then_inc(exp_ok, 1)
                    act.wait_ge(one, 1)
                    normed(0, 0, True)
                    paired(act, NU, group)
                    keep(NT - 1)

                @block.vector
                def _(dve):
                    v = nc.vector
                    v.memset(xn[:, :, D:D + 1], 1.0).then_inc(one, 1)
                    NL = 6

                    def tile(u, b, early):
                        t = 2 * u + b
                        ch = Chain(dve, vch, NL * t)
                        dve.wait_ge(lg_ok, t + 1)
                        dve.sem_inc(pace, 1)
                        ch.link(v.tensor_tensor(lg[:, b, :], pL[b][:], bc[:], ALU.add))
                        ch.link(v.reduce_max(red[:, b, :], g3(lg[:, b, :]), axis=AX))
                        ch.link(v.tensor_tensor(g3(lg[:, b, :]), g3(lg[:, b, :]), over(red[:, b, :], 2, G), ALU.subtract), wait=False)
                        ch.wait()
                        dve.sem_inc(sub_ok, 1)
                        dve.wait_ge(exp_ok, t + 1)
                        dve.sem_inc(pace, 1)
                        ch.link(v.reduce_sum(red[:, b, :], g3(lg[:, b, :]), axis=AX))
                        ch.link(v.reciprocal(red[:, b, :], red[:, b, :]))
                        if not early:
                            dve.wait_ge(s_ok, t - 1)
                            dve.sem_inc(pace, 1)
                        ch.link(v.tensor_tensor(g3(sw[:, b, :]), g3(lg[:, b, :]), over(red[:, b, :], 2, G), ALU.mult))
                        dve.sem_inc(sw_ok, 1)
                        assert ch.n == NL
                    for b in range(2):
                        tile(0, b, True)
                    with dve.Fori(1, NU) as u:
                        for b in range(2):
                            tile(u, b, False)
                    dve.wait_ge(s_ok, NT)
                    for k in range(4):
                        v.tensor_copy(st[:, k, :], pTok[k][:, 0:D + 1])

        with ExitStack() as s2:
            m2 = Mem(nc, s2)
            T = lambda n: m2.sem("f2_" + n)
            rn = m2.sb("f2_rn", [128, 4])
            stT = m2.sb("f2_stT", [128, 2, INNER])
            nrow = m2.sb("f2_nrow", [1, INNER])
            tok = m2.sb("f2_tok", [G, INNER])
            q = m2.sb("f2_q", [G, INNER])
            k_ = m2.sb("f2_k", [G, INNER])
            vv = m2.sb("f2_v", [G, INNER])
            at = m2.sb("f2_at", [G, INNER])
            atT = m2.sb("f2_atT", [G, INNER])
            red = m2.sb("f2_red", [G, FH])
            oz = m2.sb("f2_oz", [G, FH, 128])
            pA = m2.ps("f2_pA", [128, 2, 512])
            pN = m2.ps("f2_pN", [1, 512])
            pq = m2.ps("f2_pq", [G, 512])
            pk = m2.ps("f2_pk", [G, 512])
            pv = m2.ps("f2_pv", [G, 512])
            pM = m2.ps("f2_pM", [128, 2, 512])
            toP = T("toP"); toV = T("toV"); vch = T("vch"); exp_in = T("exp_in"); exp_out = T("exp_out")
            g3 = lambda ap: ap.rearrange("p (h g) -> p h g", h=FH)
            hs = lambda h: slice(h * G, (h + 1) * G)
            with nc.Block() as block:
                @block.tensor
                def _(pe):
                    t_ = nc.tensor
                    pe.wait_ge(toP, 1)
                    for k in range(4):
                        for i in range(2):
                            t_.transpose(pA[:, i, k * 128:(k + 1) * 128], st[:, k, i * 128:(i + 1) * 128], K["ident"][:])
                        last = t_.transpose(pN[:, k * 128:(k + 1) * 128], st[:, k, D:D + 1], K["ident"][:])
                    last.then_inc(toV, 1)
                    pe.wait_ge(toP, 2)
                    for h in range(FH):
                        for i in range(2):
                            t_.matmul(pq[:, hs(h)], wfx[:, i, hs(h)], stT[:, i, hs(h)], start=(i == 0), stop=False)
                        last = t_.matmul(pq[:, hs(h)], bfx[:, hs(h)], nrow[:, hs(h)], start=False, stop=True)
                    last.then_inc(toV, 1)
                    pe.wait_ge(toP, 3)
                    t_.matmul(pq[:], wqkv[:, 0, :], tok[:], start=True, stop=True)
                    t_.matmul(pk[:], wqkv[:, 1, :], tok[:], start=True, stop=True)
                    for h in range(FH):
                        last = t_.matmul(pv[:, hs(h)], tok[:, hs(h)], wqkv[:, 2, :], start=True, stop=True)
                    last.then_inc(toV, 1)
                    pe.wait_ge(toP, 4)
                    for h in range(FH):
                        last = t_.matmul(pq[:, hs(h)], q[:, hs(h)], k_[:, hs(h)], start=True, stop=True)
                    last.then_inc(toV, 1)
                    pe.wait_ge(toP, 5)
                    for h in range(FH):
                        last = t_.transpose(pk[:, hs(h)], at[:, hs(h)], K["ident"][0:G, 0:G])
                    last.then_inc(toV, 1)
                    pe.wait_ge(toP, 6)
                    for h in range(FH):
                        last = t_.matmul(pq[:, hs(h)], vv[:, hs(h)], atT[:, hs(h)], start=True, stop=True)
                    last.then_inc(toV, 1)
                    pe.wait_ge(toP, 7)
                    for k in range(4):
                        for j in range(2):
                            last = t_.matmul(pM[:, k // 2, (k % 2) * D:(k % 2 + 1) * D], oz[:, 2 * k + j, :], wout[:, 2 * k + j, :],
                                             start=(j == 0), stop=(j == 1))
                    last.then_inc(toV, 1)

                @block.scalar
                def _(act):
                    act.wait_ge(exp_in, 1)
                    nc.scalar.activation(at[:], at[:], ACT.Exp, scale=float(G) ** -0.5).then_inc(exp_out, 1)

                @block.vector
                def _(dve):
                    v = nc.vector
                    ch = Chain(dve, vch)
                    v.memset(oz[:], 0.0)
                    ch.link(v.tensor_scalar(rn[:], st[:, :, D], 1e-5, None, ALU.add))
                    ch.link(v.reciprocal(rn[:], rn[:]))
                    for k in range(4):
                        last = v.tensor_scalar(st[:, k, :], st[:, k, :], rn[:, k:k + 1], None, ALU.mult)
                    last.then_inc(toP, 1)
                    dve.wait_ge(toV, 1)
                    v.tensor_copy(stT[:], pA[:])
                    v.tensor_copy(nrow[:], pN[:]).then_inc(toP, 1)
                    dve.wait_ge(toV, 2)
                    v.tensor_copy(tok[:], pq[:]).then_inc(toP, 1)
                    dve.wait_ge(toV, 3)
                    v.tensor_copy(q[:], pq[:])
                    v.tensor_copy(k_[:], pk[:])
                    v.tensor_copy(vv[:], pv[:]).then_inc(toP, 1)
                    dve.wait_ge(toV, 4)
                    ch.link(v.reduce_max(red[:], g3(pq[:]), axis=AX))
                    v.tensor_tensor(g3(at[:]), g3(pq[:]), over(red[:], 2, G), ALU.subtract).then_inc(exp_in, 1)
                    dve.wait_ge(exp_out, 1)
                    ch.link(v.reduce_sum(red[:], g3(at[:]), axis=AX))
                    ch.link(v.reciprocal(red[:], red[:]))
                    v.tensor_tensor(g3(at[:]), g3(at[:]), over(red[:], 2, G), ALU.mult).then_inc(toP, 1)
                    dve.wait_ge(toV, 5)
                    v.tensor_copy(atT[:], pk[:]).then_inc(toP, 1)
                    dve.wait_ge(toV, 6)
                    for h in range(FH):
                        last = v.tensor_copy(oz[:, h, (h % 2) * G:(h % 2 + 1) * G], pq[:, hs(h)])
                    last.then_inc(toP, 1)
                    dve.wait_ge(toV, 7)
                    v.tensor_copy(mm[:].rearrange("p (a b) c -> p a (b c)", a=2), pM[:])

        with ExitStack() as s2:
            m2 = Mem(nc, s2)
            T = lambda n: m2.sem("f3_" + n)
            swb = m2.sb("f3_swb", [128, 2, 4, P])
            bout = m2.sb("f3_bout", [P, D])
            wuv = m2.sb("f3_wuv", [128, 2, 2 * H])
            bu = m2.sb("f3_bu", [P, 2 * H])
            xn = m2.sb("f3_xn", [P, 2, D])
            xnT = m2.sb("f3_xnT", [128, 2, 2, P])
            row = m2.sb("f3_row", [P, 2, RW])
            pY = [m2.ps(f"f3_pY{b}", [P, D]) for b in range(2)]
            pT = [m2.ps(f"f3_pT{b}", [128, 2, 128]) for b in range(2)]
            pU = [m2.ps(f"f3_pU{b}", [P, 2 * H]) for b in range(2)]
            w_in = T("w_in"); init = T("init"); swb_ok = T("swb_ok"); y_ok = T("y_ok"); y_used = T("y_used"); vch = T("vch"); pace = T("pace")
            stats = T("stats"); sq = T("sq"); rst = T("rst"); xn_ok = T("xn_ok"); t_ok = T("t_ok"); xnT_ok = T("xnT_ok"); u_ok = T("u_ok")
            row_ok = T("row_ok"); row_out = [T("row_out0"), T("row_out1")]; x_out = T("x_out")
            rows1 = dr["rows1"][0:N, :].rearrange("(p t) c -> p t c", t=NT)
            sv1 = dr["sv1"][0:N, :].rearrange("(p t) c -> p t c", t=NT)
            with nc.Block() as block:
                @block.sync
                def _(sp):
                    sp.dma_start(bout[:], ins["L0_ffn_b_out"].unsqueeze(0).broadcast_to([P, D])).then_inc(w_in, 16)
                    sp.dma_start(wuv[:, :, 0:H], ins["L1_gnn_WuT"].rearrange("(k p) h -> p k h", p=128)).then_inc(w_in, 16)
                    sp.dma_start(wuv[:, :, H:2 * H], ins["L1_gnn_WvT"].rearrange("(k p) h -> p k h", p=128)).then_inc(w_in, 16)
                    sp.wait_ge(init, 2)
                    sp.dma_start(bu[:, 0:H], ins["L1_gnn_b_u"].unsqueeze(0).broadcast_to([P, H])).then_inc(w_in, 16)
                    sp.wait_ge(stats, 1)
                    sp.dma_start(dr["x2"].rearrange("(p t) c -> p t c", t=NT), x1[:]).then_inc(x_out, 16)
                    with sp.Fori(0, NU) as u:
                        for b in range(2):
                            sp.wait_ge(row_ok, 2 * u + (b + 1))
                            sp.sem_inc(pace, 1)
                            sp.dma_start(rows1[:, bass.ds(2 * u + b, 1), :].rearrange("p a c -> p (a c)"), row[:, b, :]).then_inc(row_out[b], 16)
                            sp.dma_start(sv1[:, bass.ds(2 * u + b, 1), :].rearrange("p a c -> p (a c)"), row[:, b, RW - H:RW]).then_inc(row_out[b], 16)
                    for b in range(2):
                        sp.wait_ge(row_out[b], 32 * NU)
                    sp.wait_ge(x_out, 16)

                @block.gpsimd
                def _(pool):
                    def copy(u, first):
                        for b in range(2):
                            t = 2 * u + b
                            if not first:
                                pool.wait_ge(y_ok, t - 1)
                                pool.sem_inc(pace, 1)
                            nc.gpsimd.tensor_copy(swb[:, b, :, :], swT[:, :, bass.ds(t, 1), :].rearrange("p k a c -> p (k a) c")).then_inc(swb_ok, 1)
                    nc.gpsimd.memset(row[:], 1.0).then_inc(init, 1)
                    nc.gpsimd.memset(bu[:], 0.0).then_inc(init, 1)
                    peeled(pool, NU, copy)

                @block.tensor
                def _(pe):
                    t_ = nc.tensor
                    pe.wait_ge(w_in, 64)

                    def product(u, first):
                        for b in range(2):
                            t = 2 * u + b
                            pe.wait_ge(swb_ok, t + 1)
                            if not first:
                                pe.sem_inc(pace, 1)
                                pe.wait_ge(y_used, t - 1)
                            for k in range(4):
                                last = t_.matmul(pY[b][:], swb[:, b, k, :], mm[:, k, :], start=(k == 0), stop=(k == 3))
                            last.then_inc(y_ok, 1)
                    peeled(pe, NU, product)

                    def turn(t, b):
                        pe.wait_ge(xn_ok, t + 1)
                        for k in range(2):
                            last = t_.transpose(pT[b][:, k, 0:P], xn[:, b, k * 128:(k + 1) * 128], K["ident"][0:P, 0:P])
                        last.then_inc(t_ok, 1)

                    def scores(t, b, early):
                        pe.wait_ge(xnT_ok, t + 1)
                        if not early:
                            pe.sem_inc(pace, 1)
                            pe.wait_ge(row_ok, t - 1)
                        for k in range(2):
                            last = t_.matmul(pU[b][:], xnT[:, b, k, :], wuv[:, k, :], start=(k == 0), stop=(k == 1))
                        last.then_inc(u_ok, 1)

                    def group(u, first, last_group):
                        for b in range(2):
                            if b == 0 or not last_group:
                                turn(2 * u + (b + 1), 1 - b)
                            scores(2 * u + b, b, first)
                    turn(0, 0)
                    paired(pe, NU, group)

                @block.scalar
                def _(act):
                    s = nc.scalar
                    act.wait_ge(stats, 1)
                    s.activation(norm.rstd[:], norm.rstd[:], ACT.Sqrt).then_inc(sq, 1)
                    act.wait_ge(rst, 1)

                    def normed(t, b, early):
                        tc = bass.ds(t, 1)
                        if not early:
                            act.wait_ge(row_ok, t - 1)
                            act.sem_inc(pace, 1)
                        s.activation(xn[:, b, :], flat(x1[:, tc, :]), ACT.Identity, bias=norm.nbias[:, tc],
                                     scale=norm.rstd[:, tc]).then_inc(xn_ok, 1)

                    def turned(t, b, early):
                        act.wait_ge(t_ok, t + 1)
                        if not early:
                            act.sem_inc(pace, 1)
                            act.wait_ge(u_ok, t - 1)
                        s.activation(xnT[:, b, :, :], pT[b][:, :, 0:P], ACT.Copy).then_inc(xnT_ok, 1)

                    def group(u, first, last_group):
                        for b in range(2):
                            if b == 0 or not last_group:
                                normed(2 * u + (b + 1), 1 - b, first and b == 0)
                            turned(2 * u + b, b, first)
                    normed(0, 0, True)
                    paired(act, NU, group)

                @block.vector
                def _(dve):
                    v = nc.vector
                    dve.wait_ge(w_in, 64)
                    with dve.Fori(0, NU) as u:
                        for b in range(2):
                            t = 2 * u + b
                            ch = Chain(dve, vch, 2 * t)
                            xt = flat(x1[:, bass.ds(t, 1), :])
                            ch.link(v.tensor_tensor(xt, xt, bout[:], ALU.add))
                            dve.wait_ge(y_ok, t + 1)
                            dve.sem_inc(pace, 1)
                            ch.link(v.tensor_tensor(xt, xt, pY[b][:], ALU.add))
                            dve.sem_inc(y_used, 1)
                            norm.tile(v, t, x1[:, bass.ds(t, 1), :])
                    ch = Chain(dve, vch, 2 * NT)
                    ch.link(v.memset(norm.a[:], 0.0))
                    norm.variance(v, ch, stats)
                    dve.wait_ge(sq, 1)
                    norm.scales(v, ch, rst)

                    def tile(u, first):
                        for b in range(2):
                            t = 2 * u + b
                            if not first:
                                dve.wait_ge(row_out[b], 32 * u)
                                dve.sem_inc(pace, 1)
                            dve.wait_ge(xn_ok, t + 1)
                            v.tensor_copy(row[:, b, 0:H * VW].rearrange("p (h c) -> p h c", h=H)[:, :, 0:HD],
                                          xn[:, b, :].rearrange("p (c h) -> p h c", h=H))
                            dve.wait_ge(u_ok, t + 1)
                            v.tensor_tensor(row[:, b, H * VW:RW], pU[b][:], bu[:], ALU.add).then_inc(row_ok, 1)
                    peeled(dve, NU, tile)


def experts(nc, K, ins, dr, out):
    with ExitStack() as stack:
        m = Mem(nc, stack)
        NU = NT // 2
        flat = lambda ap: ap.rearrange("p a c -> p (a c)")
        pos = [m.sb(f"e_pos{k}", [P, NT], I32) for k in range(2)]
        wgt = [m.sb(f"e_wgt{k}", [P, NT]) for k in range(2)]
        owner = m.sb("e_owner", [1, MT], I32)
        w1 = m.sb("e_w1", [128, X, 2, HID])
        w1_in = m.sem("e_w1_in")

        with ExitStack() as s2:
            m2 = Mem(nc, s2)
            T = lambda n: m2.sem("e0_" + n)
            x3 = m2.sb("e0_x3", [P, NT, D])
            xt = m2.sb("e0_xt", [P, NT, D])
            agg = m2.sb("e0_agg", [P, 2, 5, D])
            norm1, norm2 = Norm(m2, "e0a"), Norm(m2, "e0b")
            wr = m2.sb("e0_wr", [128, 2, X])
            br = m2.sb("e0_br", [P, X])
            xtT = m2.sb("e0_xtT", [128, 2, 2, P])
            lg = m2.sb("e0_lg", [P, NT, X])
            l2 = m2.sb("e0_l2", [P, NT, X])
            tmp = m2.sb("e0_tmp", [P, NT, X])
            hot = [m2.sb(f"e0_hot{k}", [P, NT, X]) for k in range(2)]
            both = m2.sb("e0_both", [P, NT, X])
            best = [m2.sb(f"e0_best{k}", [P, NT]) for k in range(2)]
            pick = m2.sb("e0_pick", [P, NT])
            rank = m2.sb("e0_rank", [P, NT, X])
            tot = m2.sb("e0_tot", [P, X, NT])
            exc = m2.sb("e0_exc", [P, X, NT])
            zero = m2.sb("e0_zero", [P, X * NT])
            cnt = m2.sb("e0_cnt", [P, X])
            tiles_i = m2.sb("e0_tiles_i", [P, X], I32)
            tiles = m2.sb("e0_tiles", [P, X])
            ends = m2.sb("e0_ends", [P, X])
            shift = m2.sb("e0_shift", [P, X])
            iota_e = m2.sb("e0_iota_e", [P, X])
            iota_t = m2.sb("e0_iota_t", [1, MT])
            own = m2.sb("e0_own", [1, MT, X])
            ownf = m2.sb("e0_ownf", [1, MT])
            posf = m2.sb("e0_posf", [P, NT])
            R = 5
            idx = [[m2.sb(f"e0_idx{r}{k}", [P, 1], I32) for k in range(2)] for r in range(R)]
            xrow = agg[:, 0, :, :]
            pT = [m2.ps(f"e0_pT{b}", [128, 2, 128]) for b in range(2)]
            pG = [m2.ps(f"e0_pG{b}", [P, X]) for b in range(2)]
            pR = m2.ps("e0_pR", [P, 512])
            pC = m2.ps("e0_pC", [P, 512])
            x_in = T("x_in"); a_in = [T("a_in0"), T("a_in1")]; a_used = T("a_used"); w_in = T("w_in"); x_out = T("x_out"); iotas = T("iotas")
            vch = T("vch"); lch = T("lch"); stats1 = T("stats1"); sq1 = T("sq1"); rst1 = T("rst1"); stats2 = T("stats2"); sq2 = T("sq2"); rst2 = T("rst2")
            xt_ok = T("xt_ok"); t_ok = T("t_ok"); xtT_ok = T("xtT_ok"); g_ok = T("g_ok"); g_used = T("g_used"); pace = T("pace")
            both_ok = T("both_ok"); r_ok = T("r_ok"); e_in = T("e_in"); e_out = T("e_out"); row_ok = T("row_ok"); idx_ok = T("idx_ok")
            sent = [T(f"sent{r}") for r in range(R)]
            x3_ok = T("x3_ok")
            with nc.Block() as block:
                @block.sync
                def _(sp):
                    sp.dma_start(x3[:], dr["x2"].rearrange("(p t) c -> p t c", t=NT)).then_inc(x_in, 16)
                    sp.dma_start(wr[:], ins["L1_ffn_Wr"].rearrange("(k p) e -> p k e", p=128)).then_inc(w_in, 16)
                    sp.dma_start(br[:], ins["L1_ffn_br"].unsqueeze(0).broadcast_to([P, X])).then_inc(w_in, 16)
                    av = dr["agg1"][0:N, :].rearrange("(p t) c -> p t c", t=NT)
                    for g in range(NT // 5):
                        if g >= 2:
                            sp.wait_ge(a_used, g - 1)
                        sp.dma_start(agg[:, g % 2, :, :], av[:, 5 * g:5 * g + 5, :]).then_inc(a_in[g % 2], 16)
                    for e in range(X):
                        sp.dma_start(w1[:, e, :, :], ins["L1_ffn_W1"][e].rearrange("(k p) h -> p k h", p=128)).then_inc(w1_in, 16)
                    sp.wait_ge(x3_ok, 1)
                    sp.dma_start(dr["x3"].rearrange("(p t) c -> p t c", t=NT), x3[:]).then_inc(x_out, 16)
                    sp.wait_ge(x_out, 16)
                    sp.wait_ge(w1_in, 16 * X)

                @block.tensor
                def _(pe):
                    t_ = nc.tensor
                    pe.wait_ge(w_in, 32)

                    def turn(t, b):
                        pe.wait_ge(xt_ok, t + 1)
                        for k in range(2):
                            last = t_.transpose(pT[b][:, k, 0:P], xrow[:, b, k * 128:(k + 1) * 128], K["ident"][0:P, 0:P])
                        last.then_inc(t_ok, 1)

                    def product(t, b, early):
                        pe.wait_ge(xtT_ok, t + 1)
                        if not early:
                            pe.sem_inc(pace, 1)
                            pe.wait_ge(g_used, t - 1)
                        for k in range(2):
                            last = t_.matmul(pG[b][:], xtT[:, b, k, :], wr[:, k, :], start=(k == 0), stop=(k == 1))
                        last.then_inc(g_ok, 1)

                    def group(u, first, last_group):
                        for b in range(2):
                            if b == 0 or not last_group:
                                turn(2 * u + (b + 1), 1 - b)
                            product(2 * u + b, b, first)
                    turn(0, 0)
                    paired(pe, NU, group)
                    pe.wait_ge(both_ok, 1)
                    t_.matmul(pR[:, 0:NT * X], K["tri"][0:P, 0:P], both[:].rearrange("p t e -> p (t e)"), start=True, stop=True)
                    t_.matmul(pC[:, 0:NT * X], K["ones"][0:P, 0:P], both[:].rearrange("p t e -> p (t e)"), start=True, stop=True).then_inc(r_ok, 1)

                @block.scalar
                def _(act):
                    s = nc.scalar
                    act.wait_ge(stats1, 1)
                    s.activation(norm1.rstd[:], norm1.rstd[:], ACT.Sqrt).then_inc(sq1, 1)
                    act.wait_ge(rst1, 1)

                    def normed(t, b):
                        tc = bass.ds(t, 1)
                        s.activation(xrow[:, b, :], flat(x3[:, tc, :]), ACT.Identity, bias=norm1.nbias[:, tc], scale=norm1.rstd[:, tc])
                        s.activation(flat(xt[:, tc, :]), flat(x3[:, tc, :]), ACT.Identity, bias=norm1.nbias[:, tc],
                                     scale=norm1.rstd[:, tc]).then_inc(xt_ok, 1)

                    def turned(t, b, early):
                        act.wait_ge(t_ok, t + 1)
                        if not early:
                            act.sem_inc(pace, 1)
                            act.wait_ge(g_ok, t - 1)
                        s.activation(xtT[:, b, :, :], pT[b][:, :, 0:P], ACT.Copy).then_inc(xtT_ok, 1)

                    def group(u, first, last_group):
                        for b in range(2):
                            if b == 0 or not last_group:
                                normed(2 * u + (b + 1), 1 - b)
                            turned(2 * u + b, b, first)
                    normed(0, 0)
                    paired(act, NU, group)
                    act.wait_ge(stats2, 1)
                    s.activation(norm2.rstd[:], norm2.rstd[:], ACT.Sqrt).then_inc(sq2, 1)
                    act.wait_ge(e_in, 1)
                    s.activation(best[1][:], best[1][:], ACT.Exp).then_inc(e_out, 1)
                    act.wait_ge(rst2, 1)

                    def row(u, first):
                        for r in range(R):
                            t = u * R + r
                            tc = bass.ds(t, 1)
                            if not first:
                                act.wait_ge(sent[r], 32 * u)
                                act.sem_inc(pace, 1)
                            s.activation(xrow[:, r, :], flat(xt[:, tc, :]), ACT.Identity, bias=norm2.nbias[:, tc],
                                         scale=norm2.rstd[:, tc]).then_inc(row_ok, 1)
                    peeled(act, NT // R, row)

                @block.vector
                def _(dve):
                    v = nc.vector
                    ch = Chain(dve, vch)
                    dve.wait_ge(x_in, 16)
                    for g in range(NT // 5):
                        dve.wait_ge(a_in[g % 2], 16 * (g // 2 + 1))
                        for j in range(5):
                            xs = x3[:, 5 * g + j, :].rearrange("p (c h) -> p c h", h=H)
                            last = v.tensor_tensor(xs, xs, agg[:, g % 2, j, :].rearrange("p (h c) -> p c h", h=H), ALU.add)
                        last.then_inc(a_used, 1)
                    dve.wait_ge(a_used, NT // 5)
                    dve.sem_inc(x3_ok, 1)
                    with dve.Fori(0, NT) as t:
                        norm1.tile(v, t, x3[:, bass.ds(t, 1), :])
                    ch.link(v.memset(norm1.a[:], 0.0))
                    norm1.variance(v, ch, stats1)
                    dve.wait_ge(sq1, 1)
                    norm1.scales(v, ch, rst1)
                    dve.wait_ge(w_in, 32)
                    with dve.Fori(0, NU) as u:
                        for b in range(2):
                            t = 2 * u + b
                            dve.wait_ge(xt_ok, t + 1)
                            norm2.tile(v, t, xt[:, bass.ds(t, 1), :])
                            dve.wait_ge(g_ok, t + 1)
                            dve.sem_inc(pace, 1)
                            v.tensor_tensor(lg[:, bass.ds(t, 1), :].rearrange("p a c -> p (a c)"), pG[b][:], br[:], ALU.add).then_inc(g_used, 1)
                    ch.link(v.memset(norm2.a[:], 0.0))
                    norm2.variance(v, ch, stats2)
                    dve.wait_ge(iotas, 2)
                    src = lg
                    for k in range(2):
                        ch.link(v.reduce_max(best[k][:], src[:], axis=AX))
                        ch.link(v.tensor_tensor(tmp[:], src[:], over(best[k][:], 2, X), ALU.is_lt))
                        ch.link(v.scalar_tensor_tensor(tmp[:], tmp[:], float(X), over(iota_e[:], 1, NT), ALU.mult, ALU.add))
                        ch.link(v.tensor_reduce(pick[:], tmp[:], AX, ALU.min))
                        ch.link(v.tensor_tensor(hot[k][:], over(iota_e[:], 1, NT), over(pick[:], 2, X), ALU.is_equal))
                        if k == 0:
                            ch.link(v.scalar_tensor_tensor(l2[:], hot[0][:], -BIG, lg[:], ALU.mult, ALU.add))
                            src = l2
                    v.tensor_tensor(both[:], hot[0][:], hot[1][:], ALU.add).then_inc(both_ok, 1)
                    dve.wait_ge(sq2, 1)
                    v.tensor_tensor(best[1][:], best[1][:], best[0][:], ALU.subtract).then_inc(e_in, 1)
                    norm2.scales(v, ch, rst2)
                    dve.wait_ge(e_out, 1)
                    ch.link(v.tensor_scalar(wgt[0][:], best[1][:], 1.0, None, ALU.add))
                    ch.link(v.reciprocal(wgt[0][:], wgt[0][:]))
                    v.tensor_tensor(wgt[1][:], best[1][:], wgt[0][:], ALU.mult)
                    ch.link(v.memset(zero[:], 0.0))
                    dve.wait_ge(r_ok, 1)
                    v.tensor_copy(rank[:].rearrange("p t e -> p (t e)"), pR[:, 0:NT * X])
                    ch.link(v.tensor_copy(tot[:].rearrange("p e t -> p t e"), pC[:, 0:NT * X].rearrange("p (t e) -> p t e", e=X)))
                    fl = "p e t -> p (e t)"
                    ch.link(v.tensor_tensor_scan(exc[:].rearrange(fl), tot[:].rearrange(fl), zero[:], 0.0, ALU.add, ALU.add))
                    ch.link(v.tensor_tensor(exc[:].rearrange(fl), exc[:].rearrange(fl), tot[:].rearrange(fl), ALU.subtract))
                    ch.link(v.reduce_sum(cnt[:], tot[:], axis=AX))
                    ch.link(v.tensor_scalar(tiles_i[:], cnt[:], float(Q - 1), None, ALU.add))
                    ch.link(v.tensor_scalar(tiles_i[:], tiles_i[:], 7, None, ALU.arith_shift_right))
                    ch.link(v.tensor_copy(tiles[:], tiles_i[:]))
                    ch.link(v.tensor_tensor_scan(ends[:], tiles[:], zero[:, 0:X], 0.0, ALU.add, ALU.add))
                    ch.link(v.tensor_tensor(shift[:], ends[:], tiles[:], ALU.subtract))
                    ch.link(v.scalar_tensor_tensor(shift[:], shift[:], float(Q), exc[:, :, 0], ALU.mult, ALU.subtract))
                    ch.link(v.tensor_tensor(exc[:], exc[:], over(shift[:], 2, NT), ALU.add))
                    ch.link(v.tensor_tensor(rank[:], rank[:], exc[:].rearrange("p e t -> p t e"), ALU.add))
                    for k in range(2):
                        ch.link(v.tensor_tensor(tmp[:], rank[:], hot[k][:], ALU.mult))
                        ch.link(v.reduce_sum(posf[:], tmp[:], axis=AX))
                        ch.link(v.tensor_copy(pos[k][:], posf[:]))

                    def index(u, first):
                        for r in range(R):
                            t = u * R + r
                            if not first:
                                dve.wait_ge(sent[r], 32 * u)
                                dve.sem_inc(pace, 1)
                            v.tensor_copy(idx[r][0][:], pos[0][:, bass.ds(t, 1)])
                            v.tensor_copy(idx[r][1][:], pos[1][:, bass.ds(t, 1)]).then_inc(idx_ok, 1)
                    peeled(dve, NT // R, index)
                    ch.link(v.tensor_tensor(own[:], over(iota_t[:], 2, X), over(ends[0:1, :], 1, MT), ALU.is_ge))
                    ch.link(v.reduce_sum(ownf[:], own[:], axis=AX))
                    ch.link(v.tensor_scalar(owner[:], ownf[:], float(X - 1), None, ALU.min))

                @block.gpsimd
                def _(pool):
                    pool.iota(iota_e[:], pattern=[[1, X]], base=0, channel_multiplier=0, allow_small_or_imprecise_dtypes=True).then_inc(iotas, 1)
                    pool.iota(iota_t[:], pattern=[[1, MT]], base=0, channel_multiplier=0, allow_small_or_imprecise_dtypes=True).then_inc(iotas, 1)
                    with pool.Fori(0, NT // R) as u:
                        for r in range(R):
                            pool.wait_ge(idx_ok, u * R + (r + 1))
                            pool.sem_inc(pace, 1)
                            pool.wait_ge(row_ok, u * R + (r + 1))
                            pool.sem_inc(pace, 1)
                            for k in range(2):
                                pool.indirect_dma_start(out=dr["xs"], out_offset=bass.IndirectOffsetOnAxis(ap=idx[r][k][:, 0:1], axis=0),
                                                        in_=xrow[:, r, :], in_offset=None).then_inc(sent[r], 16)
                    for r in range(R):
                        pool.wait_ge(sent[r], 32 * (NT // R))

        with ExitStack() as s2:
            m2 = Mem(nc, s2)
            T = lambda n: m2.sem("e1_" + n)
            w2 = m2.sb("e1_w2", [128, X, KC, D])
            NB1, NB2 = X * HID // 128, X * D // 128
            bf = m2.sb("e1_bf", [128, NB1 + NB2])
            bpart = m2.sb("e1_bpart", [128, 3, NB1 + NB2], BF16)
            b1 = m2.sb("e1_b1", [3, X, HID], BF16)
            b2 = m2.sb("e1_b2", [3, X, D], BF16)
            ones3 = m2.sb("e1_ones3", [3, Q], BF16)
            gl = m2.sb("e1_gl", [128, X, 2])
            bl = m2.sb("e1_bl", [128, X, 2])
            xs = m2.sb("e1_xs", [Q, 2, D])
            xT = m2.sb("e1_xT", [128, 2, 2, Q])
            hh = m2.sb("e1_hh", [Q, 2, HID])
            hT = m2.sb("e1_hT", [128, 2, KC, Q])
            ys = m2.sb("e1_ys", [Q, 2, D])
            pX = m2.ps("e1_pX", [128, 2, Q])
            pH = m2.ps("e1_pH", [Q, HID])
            pHT = m2.ps("e1_pHT", [128, KC, Q])
            pY = [m2.ps(f"e1_pY{b}", [Q, D]) for b in range(2)]
            w_in = T("w_in"); x_in = [T("x_in0"), T("x_in1")]; xT_ps = T("xT_ps"); xT_ok = T("xT_ok"); h_ok = T("h_ok"); g_ok = T("g_ok")
            hT_ps = T("hT_ps"); hT_ok = T("hT_ok"); y_ok = T("y_ok"); ys_ok = T("ys_ok"); y_out = [T("y_out0"), T("y_out1")]; pace = T("pace")
            b_in = T("b_in"); split = T("split"); b_row = T("b_row"); vch = T("vch"); ab_in = T("ab_in")
            MU = MT // 2
            with nc.Block() as block:
                @block.sync
                def _(sp):
                    def load(u, b):
                        sp.dma_start(xs[:, b, :], dr["xs"].rearrange("(t q) c -> t q c", q=Q)[bass.ds(2 * u + b, 1), :, :].rearrange("a q c -> (a q) c")).then_inc(x_in[b], 16)

                    def store(u, b):
                        sp.wait_ge(ys_ok, 2 * u + (b + 1))
                        sp.sem_inc(pace, 1)
                        sp.dma_start(dr["ys"].rearrange("(t q) c -> t q c", q=Q)[bass.ds(2 * u + b, 1), :, :].rearrange("a q c -> (a q) c"), ys[:, b, :]).then_inc(y_out[b], 16)
                    load(0, 0)
                    load(0, 1)
                    for e in range(X):
                        sp.dma_start(w2[:, e, :, :], ins["L1_ffn_W2"][e].rearrange("(k p) o -> p k o", p=128)).then_inc(w_in, 16)

                    def step(u, first):
                        for b in range(2):
                            sp.wait_ge(xT_ps, 2 * u + (b + 1))
                            sp.sem_inc(pace, 1)
                            load(u + 1, b)
                            if not first:
                                store(u - 1, b)
                    peeled(sp, MU - 1, step)
                    for u in range(MU - 2, MU):
                        for b in range(2):
                            store(u, b)
                    for b in range(2):
                        sp.wait_ge(y_out[b], 16 * MU)

                @block.tensor
                def _(pe):
                    t_ = nc.tensor

                    def expert(t):
                        return pe.value_load(owner[0:1, bass.ds(t, 1)], min_val=0, max_val=X - 1)

                    def rows_turn(u, b):
                        t = 2 * u + b
                        pe.wait_ge(x_in[b], 16 * u + 16)
                        if not (isinstance(t, int) and t == 0):
                            pe.sem_inc(pace, 1)
                            pe.wait_ge(xT_ok, t)
                        for k in range(2):
                            last = t_.transpose(pX[:, k, :], xs[:, b, k * 128:(k + 1) * 128], K["ident"][:])
                        last.then_inc(xT_ps, 1)

                    def hidden(t, b, e):
                        pe.wait_ge(xT_ok, t + 1)
                        if not (isinstance(t, int) and t == 0):
                            pe.sem_inc(pace, 1)
                            pe.wait_ge(g_ok, t)
                        for c in range(2):
                            sl = slice(c * 512, (c + 1) * 512)
                            for k in range(2):
                                t_.matmul(pH[:, sl], xT[:, b, k, :], w1[:, bass.ds(e, 1), k, sl].rearrange("p a h -> p (a h)"), start=(k == 0), stop=False)
                            last = t_.matmul(pH[:, sl], ones3[:], b1[:, bass.ds(e, 1), sl].rearrange("p a h -> p (a h)"), start=False, stop=True)
                        last.then_inc(h_ok, 1)

                    def units_turn(t, b):
                        pe.wait_ge(g_ok, t + 1)
                        if not (isinstance(t, int) and t == 0):
                            pe.sem_inc(pace, 1)
                            pe.wait_ge(hT_ok, t)
                        for k in range(KC):
                            last = t_.transpose(pHT[:, k, :], hh[:, b, k * 128:(k + 1) * 128], K["ident"][:])
                        last.then_inc(hT_ps, 1)

                    def outputs(t, b, e):
                        pe.wait_ge(hT_ok, t + 1)
                        if not (isinstance(t, int) and t < 2):
                            pe.sem_inc(pace, 1)
                            pe.wait_ge(ys_ok, t - 1)
                        for k in range(KC):
                            t_.matmul(pY[b][:], hT[:, b, k, :], w2[:, bass.ds(e, 1), k, :].rearrange("p a h -> p (a h)"), start=(k == 0), stop=False)
                        t_.matmul(pY[b][:], ones3[:], b2[:, bass.ds(e, 1), :].rearrange("p a h -> p (a h)"), start=False, stop=True).then_inc(y_ok, 1)

                    def group(u, first, last_group):
                        for b in range(2):
                            t = 2 * u + b
                            more = b == 0 or not last_group
                            if more:
                                e = expert(t + 1)
                            if not last_group:
                                rows_turn(u + 1, b)
                            units_turn(t, b)
                            if more:
                                hidden(t + 1, 1 - b, e)
                            outputs(t, b, expert(t))
                    pe.wait_ge(b_row, 96)
                    rows_turn(0, 0)
                    rows_turn(0, 1)
                    hidden(0, 0, expert(0))
                    pe.wait_ge(w_in, 16 * X)
                    paired(pe, MU, group)

                @block.scalar
                def _(act):
                    s = nc.scalar
                    act.dma_start(bf[:, 0:NB1], ins["L1_ffn_b1"].rearrange("e (a h) -> (e a) h", h=NB1)).then_inc(b_in, 16)
                    act.dma_start(bf[:, NB1:], ins["L1_ffn_b2"].rearrange("e (a h) -> (e a) h", h=NB2)).then_inc(b_in, 16)
                    act.dma_start(gl[:], ins["L1_ffn_ln_g"].rearrange("e (k p) -> p e k", p=128), allow_slow_non_contiguous=True).then_inc(ab_in, 16)
                    act.dma_start(bl[:], ins["L1_ffn_ln_b"].rearrange("e (k p) -> p e k", p=128), allow_slow_non_contiguous=True).then_inc(ab_in, 16)
                    act.wait_ge(split, 1)
                    for j in range(3):
                        act.dma_start(b1[j:j + 1, :, :].rearrange("o e h -> o (e h)").rearrange("o (p h) -> o p h", h=NB1), bpart[:, j, 0:NB1]).then_inc(b_row, 16)
                        act.dma_start(b2[j:j + 1, :, :].rearrange("o e h -> o (e h)").rearrange("o (p h) -> o p h", h=NB2), bpart[:, j, NB1:]).then_inc(b_row, 16)
                    act.wait_ge(ab_in, 32)

                    def affine(t, b):
                        e = act.value_load(owner[0:1, bass.ds(t, 1)], min_val=0, max_val=X - 1)
                        act.wait_ge(xT_ps, t + 1)
                        if not (isinstance(t, int) and t < 2):
                            act.sem_inc(pace, 1)
                            act.wait_ge(h_ok, t - 1)
                        for k in range(2):
                            last = s.activation(xT[:, b, k, :], pX[:, k, :], ACT.Identity, bias=bl[:, bass.ds(e, 1), k], scale=gl[:, bass.ds(e, 1), k])
                        last.then_inc(xT_ok, 1)

                    def units(t, b):
                        act.wait_ge(h_ok, t + 1)
                        if not (isinstance(t, int) and t < 2):
                            act.sem_inc(pace, 1)
                            act.wait_ge(hT_ps, t - 1)
                        s.activation(hh[:, b, :], pH[:], ACT.Gelu).then_inc(g_ok, 1)

                    def group(u, first, last_group):
                        for b in range(2):
                            t = 2 * u + b
                            if not last_group:
                                affine(t + 2, b)
                            if b == 0 or not last_group:
                                units(t + 1, 1 - b)
                    affine(0, 0)
                    affine(1, 1)
                    units(0, 0)
                    paired(act, MU, group)

                @block.vector
                def _(dve):
                    v = nc.vector
                    ch = Chain(dve, vch)
                    v.memset(ones3[:], 1.0)
                    dve.wait_ge(b_in, 32)
                    ch.link(v.tensor_copy(bpart[:, 0, :], bf[:]))
                    ch.link(v.tensor_tensor(bf[:], bf[:], bpart[:, 0, :], ALU.subtract))
                    ch.link(v.tensor_copy(bpart[:, 1, :], bf[:]))
                    ch.link(v.tensor_tensor(bf[:], bf[:], bpart[:, 1, :], ALU.subtract))
                    v.tensor_copy(bpart[:, 2, :], bf[:]).then_inc(split, 1)

                    def group(u, first, last_group):
                        for b in range(2):
                            t = 2 * u + b
                            dve.wait_ge(hT_ps, t + 1)
                            if not first:
                                dve.sem_inc(pace, 1)
                                dve.wait_ge(y_ok, t - 1)
                            v.tensor_copy(hT[:, b, :, :], pHT[:]).then_inc(hT_ok, 1)
                            dve.wait_ge(y_ok, t + 1)
                            if not first:
                                dve.sem_inc(pace, 1)
                                dve.wait_ge(y_out[b], 16 * u)
                            v.tensor_copy(ys[:, b, :], pY[b][:]).then_inc(ys_ok, 1)
                    paired(dve, MU, group)

        with ExitStack() as s2:
            m2 = Mem(nc, s2)
            T = lambda n: m2.sem("e2_" + n)
            R = 5
            x3 = m2.sb("e2_x3", [P, NT, D])
            idx = [[m2.sb(f"e2_idx{r}{k}", [P, 1], I32) for k in range(2)] for r in range(R)]
            yr = m2.sb("e2_yr", [P, R, 2, D])
            x_in = T("x_in"); idx_ok = T("idx_ok"); got = [T(f"got{r}") for r in range(R)]; pace = T("pace"); vch = T("vch"); done = T("done"); o_out = T("o_out")
            with nc.Block() as block:
                @block.sync
                def _(sp):
                    sp.dma_start(x3[:], dr["x3"].rearrange("(p t) c -> p t c", t=NT)).then_inc(x_in, 16)
                    ov = out.rearrange("(p t) c -> p t c", t=NT)
                    for g in range(NT // R):
                        sp.wait_ge(done, g + 1)
                        sp.dma_start(ov[:, g * R:(g + 1) * R, :], x3[:, g * R:(g + 1) * R, :]).then_inc(o_out, 16)
                    sp.wait_ge(o_out, 16 * (NT // R))

                @block.gpsimd
                def _(pool):
                    with pool.Fori(0, NT // R) as u:
                        for r in range(R):
                            pool.wait_ge(idx_ok, u * R + (r + 1))
                            pool.sem_inc(pace, 1)
                            for k in range(2):
                                pool.indirect_dma_start(out=yr[:, r, k, :], out_offset=None, in_=dr["ys"],
                                                        in_offset=bass.IndirectOffsetOnAxis(ap=idx[r][k][:, 0:1], axis=0)).then_inc(got[r], 16)

                @block.vector
                def _(dve):
                    v = nc.vector

                    def index(t, r):
                        v.tensor_copy(idx[r][0][:], pos[0][:, bass.ds(t, 1)])
                        v.tensor_copy(idx[r][1][:], pos[1][:, bass.ds(t, 1)]).then_inc(idx_ok, 1)

                    def add(u, more):
                        for r in range(R):
                            t = u * R + r
                            tc = bass.ds(t, 1)
                            ch = Chain(dve, vch, 2 * t)
                            dve.wait_ge(got[r], 32 * u + 32)
                            dve.sem_inc(pace, 1)
                            xs = flat(x3[:, tc, :])
                            for k in range(2):
                                ch.link(v.scalar_tensor_tensor(xs, yr[:, r, k, :], wgt[k][:, tc], xs, ALU.mult, ALU.add))
                            if more:
                                index(t + R, r)
                        dve.sem_inc(done, 1)
                    dve.wait_ge(x_in, 16)
                    for r in range(R):
                        index(r, r)
                    with dve.Fori(0, NT // R - 1) as u:
                        add(u, True)
                    add(NT // R - 1, False)


def layouts(inputs):
    T = np.ascontiguousarray
    return {
        "L0_gnn_WT": T(np.asarray(inputs["L0_gnn_W"]).T),
        "L0_gnn_edge_WT": T(np.asarray(inputs["L0_gnn_edge_W"]).T),
        "L1_gnn_WuT": T(np.asarray(inputs["L1_gnn_W_u"]).T),
        "L1_gnn_WvT": T(np.asarray(inputs["L1_gnn_W_v"]).T),
        "L0_ffn_WxT": T(np.asarray(inputs["L0_ffn_W_x"]).T),
    }


def program(nc, ins, out):
    with ExitStack() as stack:
        m = Mem(nc, stack)
        K = {"ident": m.sb("k_ident", [128, 128]), "tri": m.sb("k_tri", [128, 128]), "ones": m.sb("k_ones", [128, 128]),
             "iota64": m.sb("k_iota64", [128, NB]), "padrec": m.sb("k_padrec", [NPAD - N, 4], I32), "pt": m.sb("k_pt", [Q, QT, 4], I32), "rp": m.sb("k_rp", [Q, QT]),
             "deg": m.sb("k_deg", [Q, QT]), "ct": m.sb("k_ct", [1, QT + 2], I32)}

        def scratch(name, shape, dt=F32):
            return nc.dram_tensor(name, shape, dt, kind="Internal").ap()
        dr = {"rows0": scratch("rows0", (NPAD, RW)), "rows1": scratch("rows1", (NPAD, RW)), "sv1": scratch("sv1", (NPAD, H)),
              "rec": scratch("rec", (E, REC)), "rp": scratch("rp", (1, N + 1), I32),
              "noderec": scratch("noderec", (NPAD, 4), I32), "slots": scratch("slots", (CMAX, Q, REC)),
              "agg0": scratch("agg0", (NPAD, D)), "agg1": scratch("agg1", (NPAD, D)), "x2": scratch("x2", (N, D)), "x3": scratch("x3", (N, D)),
              "xs": scratch("xs", (MT * Q, D)), "ys": scratch("ys", (MT * Q, D))}
        prepare(nc, K, ins, dr)
        order(nc, K, ins, dr)
        graph(nc, K, ins, dr, 0)
        slice_ffn(nc, K, ins, dr)
        graph(nc, K, ins, dr, 1)
        experts(nc, K, ins, dr, out)


_INS = ["x", "src", "dst", "edge_attr_3", "L0_gnn_W", "L0_gnn_a_src", "L0_gnn_a_dst", "L0_gnn_edge_b", "L0_gnn_bias",
        "L0_ffn_W_fx", "L0_ffn_b_fx", "L0_ffn_b_x", "L0_ffn_W_slice", "L0_ffn_b_slice", "L0_ffn_W_q", "L0_ffn_W_k",
        "L0_ffn_W_v", "L0_ffn_W_out", "L0_ffn_b_out", "L0_ffn_temperature", "L1_gnn_b_u", "L1_ffn_Wr", "L1_ffn_br",
        "L1_ffn_ln_g", "L1_ffn_ln_b", "L1_ffn_W1", "L1_ffn_b1", "L1_ffn_W2", "L1_ffn_b2"]


def kernel(**inputs):
    import concourse.bacc as bacc
    from concourse.bass_utils import run_bass_kernel_spmd

    nc = bacc.Bacc("TRN2", target_bir_lowering=False, num_devices=1)
    given = {name: np.ascontiguousarray(inputs[name]) for name in _INS}
    given.update(layouts(inputs))
    arrays, aps = {}, {}
    for name, a in given.items():
        arrays[f"in_{name}"] = a
        aps[name] = nc.dram_tensor(f"in_{name}", a.shape, mybir.dt.from_np(a.dtype), kind="ExternalInput").ap()
    out = nc.dram_tensor("out_0", (N, D), F32, kind="ExternalOutput").ap()
    program(nc, aps, out)
    r = run_bass_kernel_spmd(nc, [arrays], core_ids=[0])
    return r.results[0]["out_0"]
```

```python
import numpy as np
import concourse.bass as bass
from concourse import mybir
from contextlib import ExitStack

F32 = mybir.dt.float32
BF16 = mybir.dt.bfloat16
I32 = mybir.dt.int32
ALU = mybir.AluOpType
ACT = mybir.ActivationFunctionType
AX = mybir.AxisListType.X

N = 6250
E = 106250
D = 256
H = 8
HD = D // H
P = 125
NT = N // P
EP = E // P
Q = 128
QT = -(-N // Q)
NPAD = QT * Q
C = 7
REC = 4 * C
NB = 64
VW = HD + 1
RW = H * VW + 2 * H
CMAX = (E // C + 2 * QT + 8) // 4 * 4
BLOG = 9
BLK = 1 << BLOG
BIG = 1e30
LN_EPS = 1e-5
G = 64
FH = 8
X = 8
HID = 1024
MT = 106
LEAST = -(-2 * N // Q) // 2 * 2
KC = HID // 128
XW = D + 1


class Chain:

    def __init__(self, eng, sem, base=0):
        self.eng, self.sem, self.base, self.n = eng, sem, base, 0

    def link(self, ins, wait=True):
        ins.then_inc(self.sem, 1)
        self.n += 1
        if wait:
            self.wait()

    def wait(self, n=None):
        self.eng.wait_ge(self.sem, self.base + (self.n if n is None else n))

    def enter(self, i, k):
        self.outer, self.k, self.n0 = self.base, k, self.n
        self.base, self.n = self.base + self.n + i * k, 0

    def leave(self, times):
        assert self.n == self.k, (self.n, self.k)
        self.base, self.n = self.outer, self.n0 + times * self.k


def over(ap, axis, n):
    a = ap.unsqueeze(axis)
    shape = list(a.shape)
    shape[axis] = n
    return a.broadcast_to(shape)


def peeled(eng, n, body):
    body(0, True)
    with eng.Fori(1, n) as u:
        body(u, False)


class Mem:

    def __init__(self, nc, stack):
        self.nc, self.stack, self.sems = nc, stack, []
        stack.callback(self.clear)

    def clear(self):
        if self.sems:
            self.nc.clear_and_free_semaphores(self.sems)
            self.nc.all_engine_barrier()

    def sb(self, name, shape, dt=F32):
        return self.stack.enter_context(self.nc.sbuf_tensor(name, shape, dt))

    def ps(self, name, shape, dt=F32):
        return self.stack.enter_context(self.nc.psum_tensor(name, shape, dt))

    def sem(self, name):
        self.sems.append(self.nc.alloc_semaphore(name))
        return self.sems[-1]


class Norm:

    def __init__(self, m, name):
        self.st = m.sb(name + "_st", [P, NT, 6])
        self.a, self.b, self.rstd, self.nbias = (m.sb(name + s, [P, NT]) for s in ("_na", "_nb", "_rstd", "_nbias"))

    def tile(self, v, t, x):
        return v.bn_stats(self.st[:, bass.ds(t, 1), :].rearrange("p a c -> p (a c)"), x.rearrange("p a c -> p (a c)"))

    def statistics(self, eng, v, x):
        with eng.Fori(0, NT // 5) as u:
            for r in range(5):
                self.tile(v, 5 * u + r, x[:, bass.ds(5 * u + r, 1), :])

    def variance(self, v, ch, done):
        st = self.st
        ch.link(v.tensor_tensor(self.a[:], st[:, :, 1], st[:, :, 4], ALU.subtract))
        ch.link(v.scalar_tensor_tensor(self.a[:], self.a[:], 0.25, self.a[:], ALU.mult, ALU.mult))
        ch.link(v.tensor_tensor(self.b[:], st[:, :, 2], st[:, :, 5], ALU.add))
        ch.link(v.scalar_tensor_tensor(self.a[:], self.b[:], 1.0 / D, self.a[:], ALU.mult, ALU.add))
        ch.link(v.tensor_scalar(self.rstd[:], self.a[:], LN_EPS, None, ALU.add))
        ch.link(v.tensor_tensor(self.b[:], st[:, :, 1], st[:, :, 4], ALU.add))
        v.tensor_scalar(self.nbias[:], self.b[:], -0.5, None, ALU.mult).then_inc(done, 1)

    def scales(self, v, ch, done):
        ch.link(v.reciprocal(self.rstd[:], self.rstd[:]))
        v.tensor_tensor(self.nbias[:], self.nbias[:], self.rstd[:], ALU.mult).then_inc(done, 1)


class Kept:

    def __init__(self, m):
        self.RB = 5
        self.x = m.sb("p_x", [P, NT, D])
        self.row = m.sb("p_row", [P, self.RB, RW])
        self.norm = Norm(m, "p")
        self.wx = m.sb("p_wx", [128, 2, D + 2 * H])


def sort_nodes(nc, K, ins, dr):
    with ExitStack() as stack:
        m = Mem(nc, stack)
        kept = Kept(m)
        prepare(nc, K, ins, dr, kept)
        order(nc, K, dr, kept)


def prepare(nc, K, ins, dr, kept):
    with ExitStack() as stack:
        m = Mem(nc, stack)
        x, row, norm, wx = kept.x, kept.row, kept.norm, kept.wx
        srcw = m.sb("p_srcw", [P, EP + C - 1], I32)
        attrw = m.sb("p_attrw", [P, 3 * (EP + C - 1)])
        PIECE = EP // 5
        rec = m.sb("p_rec", [P, 2, PIECE, REC])
        dst0 = m.sb("p_dst0", [P, 1], I32)
        dst0f = m.sb("p_dst0f", [P, 1])
        iota_n = m.sb("p_iota_n", [P, N])
        below = m.sb("p_below", [P, N], BF16)
        ones = m.sb("p_ones", [P, 1], BF16)
        node = m.sb("p_node", [P, NT])
        blk = m.sb("p_blk", [P, NT])
        cnt = m.sb("p_cnt", [P, NT])
        blk_i = m.sb("p_blk_i", [P, NT], I32)
        R = 5
        idx = [m.sb(f"p_idx{r}", [P, 1], I32) for r in range(R)]
        drow = m.sb("p_drow", [P, R, EP], I32)
        rp = m.sb("p_rp", [P, NT], I32)
        e_end = m.sb("p_eend", [1, 1], I32)
        zrow = m.sb("p_zrow", [NPAD - N, RW])
        wn = m.sb("p_wn", [128, 2, D])
        aa = m.sb("p_aa", [128, 2, 2])
        amask = m.sb("p_amask", [128, 4])
        ablk = m.sb("p_ablk", [128, 2, 2 * H])
        rstd = norm.rstd
        pW = m.ps("p_pW", [128, 2, 256])
        pC = m.ps("p_pC", [P, 64])

        x_in = m.sem("p_x_in"); e_in = m.sem("p_e_in"); w_in = m.sem("p_w_in"); d_in = m.sem("p_d_in")
        zeroed = m.sem("p_zeroed"); rec_made = m.sem("p_rec_made"); rec_out = [m.sem(f"p_rec_out{b}") for b in range(2)]
        misc_out = m.sem("p_misc_out")
        consts = m.sem("p_consts"); below_ok = m.sem("p_below_ok"); counted = m.sem("p_counted")
        idx_ok = m.sem("p_idx_ok"); landed = [m.sem(f"p_landed{r}") for r in range(R)]
        vch = m.sem("p_vchain"); stats = m.sem("p_stats"); sq = m.sem("p_sqrt"); rst = m.sem("p_rstd_ok")
        ablk_ok = m.sem("p_ablk_ok"); wa_ok = m.sem("p_wa_ok"); wx_ok = m.sem("p_wx_ok")
        rp_ok = m.sem("p_rp_ok"); rp_out = m.sem("p_rp_out"); pace = m.sem("p_pace")

        recs = dr["rec"].rearrange("(p g e) c -> p g (e c)", p=P, g=5)

        with nc.Block() as block:
            @block.sync
            def _(sp):
                sp.dma_start(dst0[:], ins["dst"].rearrange("(p e) -> p e", p=P)[:, 0:1], allow_slow_non_contiguous=True).then_inc(d_in, 16)
                sp.dma_start(x[:], ins["x"].rearrange("(p t) c -> p t c", t=NT)).then_inc(x_in, 16)
                sp.wait_ge(zeroed, 2)
                s, a = ins["src"], ins["edge_attr_3"].rearrange("e c -> (e c)")
                sp.dma_start(srcw[0:P - 1, :], bass.AP(s.tensor, 0, [[EP, P - 1], [1, EP + C - 1]])).then_inc(e_in, 16)
                sp.dma_start(srcw[P - 1:P, 0:EP], s[E - EP:E].unsqueeze(0)).then_inc(e_in, 16)
                sp.dma_start(attrw[0:P - 1, :], bass.AP(a.tensor, 0, [[3 * EP, P - 1], [1, 3 * (EP + C - 1)]])).then_inc(e_in, 16)
                sp.dma_start(attrw[P - 1:P, 0:3 * EP], a[3 * (E - EP):3 * E].unsqueeze(0)).then_inc(e_in, 16)
                for g in range(5):
                    sp.wait_ge(rec_made, 2 * g + 2)
                    sp.dma_start(recs[:, g, :], rec[:, g % 2, :, :].rearrange("p e c -> p (e c)")).then_inc(rec_out[g % 2], 16)
                sp.wait_ge(zeroed, 6)
                sp.dma_start(dr["rows0"][N:NPAD, :], zrow[:]).then_inc(misc_out, 16)
                sp.dma_start(dr["rows1"][N:NPAD, :], zrow[:]).then_inc(misc_out, 16)
                sp.dma_start(dr["sv1"][N:NPAD, :], zrow[:, 0:H]).then_inc(misc_out, 16)
                sp.wait_ge(rp_ok, 1)
                sp.dma_start(dr["rp"][:, 0:N].rearrange("o (p t) -> (o p) t", t=NT), rp[:]).then_inc(rp_out, 16)
                sp.dma_start(dr["rp"][:, N:N + 1], e_end[:]).then_inc(rp_out, 16)
                sp.wait_ge(rp_out, 32)
                sp.wait_ge(rec_out[0], 48)
                sp.wait_ge(rec_out[1], 32)
                sp.wait_ge(misc_out, 48)

            @block.gpsimd
            def _(pool):
                pool.memset(srcw[:], 0).then_inc(zeroed, 1)
                pool.memset(attrw[:], 0.0).then_inc(zeroed, 1)
                pool.iota(iota_n[:], pattern=[[1, N]], base=0, channel_multiplier=0,
                          allow_small_or_imprecise_dtypes=True).then_inc(consts, 1)
                pool.iota(node[:], pattern=[[1, NT]], base=0, channel_multiplier=NT,
                          allow_small_or_imprecise_dtypes=True).then_inc(consts, 1)
                pool.memset(ones[:], 1.0).then_inc(consts, 1)
                pool.memset(K["ident"][:], 0.0)
                pool.memset(K["tri"][:], 1.0)
                pool.memset(K["ones"][:], 1.0)
                pool.memset(amask[:], 1.0)
                pool.memset(row[:], 1.0)
                pool.iota(K["iota64"][:], pattern=[[1, NB]], base=0, channel_multiplier=0,
                          allow_small_or_imprecise_dtypes=True)
                pool.memset(zrow[:], 0.0).then_inc(consts, 1)
                pool.wait_ge(consts, 4)
                pool.affine_select(out=K["ident"][:], in_=K["ident"][:], compare_op=ALU.not_equal, fill=1.0, base=0,
                                   pattern=[[-1, 128]], channel_multiplier=1)
                pool.affine_select(out=K["tri"][:], in_=K["tri"][:], compare_op=ALU.is_gt, fill=0.0, base=0,
                                   pattern=[[1, 128]], channel_multiplier=-1)
                pool.affine_select(out=amask[:], in_=amask[:], compare_op=ALU.is_ge, fill=0.0, base=0,
                                   pattern=[[-HD, 4]], channel_multiplier=1).then_inc(consts, 1)
                pool.wait_ge(consts, 5)
                pool.affine_select(out=amask[:], in_=amask[:], compare_op=ALU.is_ge, fill=0.0, base=HD - 1,
                                   pattern=[[HD, 4]], channel_multiplier=-1)
                pool.iota(e_end[:], pattern=[[0, 1]], base=E, channel_multiplier=0).then_inc(consts, 1)
                pool.wait_ge(consts, 6)
                pool.iota(K["padrec"][:], pattern=[[0, 4]], base=N, channel_multiplier=1).then_inc(consts, 1)
                pool.wait_ge(consts, 7)
                pool.memset(K["padrec"][:, 1:4], 0).then_inc(zeroed, 4)
                pool.wait_ge(zeroed, 6)
                dview = ins["dst"].rearrange("(p e) -> p e", p=P)

                def gather(u, r):
                    pool.wait_ge(idx_ok, u * R + (r + 1))
                    pool.sem_inc(pace, 1)
                    pool.indirect_dma_start(out=drow[:, r, :], out_offset=None, in_=dview,
                                            in_offset=bass.IndirectOffsetOnAxis(ap=idx[r][:, 0:1], axis=0)
                                            ).then_inc(landed[r], 16)
                with pool.Fori(0, NT // R) as u:
                    for r in range(R):
                        gather(u, r)

            @block.vector
            def _(dve):
                v = nc.vector
                ch = Chain(dve, vch)
                dve.wait_ge(consts, 7)
                dve.wait_ge(d_in, 16)
                ch.link(v.tensor_copy(dst0f[:], dst0[:]))
                v.tensor_scalar(below[:], iota_n[:], dst0f[:], None, ALU.is_gt).then_inc(below_ok, 1)
                dve.wait_ge(w_in, 64)
                for k in range(2):
                    for s in range(2):
                        if k == 0 and s == 0:
                            ch.link(v.memset(ablk[:], 0.0))
                        last = v.tensor_scalar(ablk[:, k, s * H + 4 * k:s * H + 4 * k + 4], amask[:], aa[:, k, s:s + 1], None, ALU.mult)
                last.then_inc(ablk_ok, 1)
                def record(g):
                    if g >= 2:
                        dve.wait_ge(rec_out[g % 2], 16 * (g // 2))
                    o = rec[:, g % 2, :, :]
                    sw = bass.AP(srcw, g * PIECE, [[EP + C - 1, P], [1, PIECE], [1, C]])
                    aw = bass.AP(attrw, 3 * g * PIECE, [[3 * (EP + C - 1), P], [3, PIECE], [1, 3 * C]])
                    v.tensor_copy(o[:, :, 0:C].bitcast(I32), sw).then_inc(rec_made, 1)
                    v.tensor_copy(o[:, :, C:REC], aw).then_inc(rec_made, 1)
                dve.wait_ge(e_in, 64)
                record(0)
                record(1)
                dve.wait_ge(x_in, 16)
                norm.statistics(dve, v, x)
                ch.link(v.memset(norm.a[:], 0.0))
                norm.variance(v, ch, stats)
                dve.wait_ge(sq, 1)
                norm.scales(v, ch, rst)
                dve.wait_ge(counted, 1)
                ch.link(v.tensor_scalar(blk[:], pC[:, 0:NT], -1.0, 0.0, ALU.add, ALU.max))
                ch.link(v.tensor_copy(blk_i[:], blk[:]))
                for r in range(R):
                    v.tensor_copy(idx[r][:], blk_i[:, r:r + 1]).then_inc(idx_ok, 1)

                def count(u, r, more):
                    t = u * R + r
                    dve.wait_ge(landed[r], 16 * u + 16)
                    dve.sem_inc(pace, 1)
                    tc = bass.ds(t, 1)
                    last = v.tensor_scalar(drow[:, r, :], drow[:, r, :], node[:, tc], 0.0, ALU.is_lt, ALU.add, accum_out=cnt[:, tc])
                    if more:
                        v.tensor_copy(idx[r][:], blk_i[:, bass.ds(t + R, 1)]).then_inc(idx_ok, 1)
                    return last
                record(2)
                record(3)
                with dve.Fori(0, 2) as u:
                    for r in range(R):
                        count(u, r, True)
                record(4)
                with dve.Fori(2, NT // R - 1) as u:
                    for r in range(R):
                        count(u, r, True)
                for r in range(R):
                    last = count(NT // R - 1, r, False)
                ch.link(last)
                ch.link(v.scalar_tensor_tensor(cnt[:], blk[:], float(EP), cnt[:], ALU.mult, ALU.add))
                v.tensor_copy(rp[:], cnt[:]).then_inc(rp_ok, 1)

            @block.scalar
            def _(act):
                s = nc.scalar
                act.dma_start(wn[:], ins["L0_gnn_W"].rearrange("(k p) i -> p k i", p=128)).then_inc(w_in, 16)
                for q, nm in enumerate(("L0_gnn_a_src", "L0_gnn_a_dst")):
                    act.dma_start(aa[:, :, q:q + 1], ins[nm].rearrange("h (d o) -> (h d) o", o=1).rearrange("(k p) o -> p k o", p=128), allow_slow_non_contiguous=True).then_inc(w_in, 16)
                act.dma_start(wx[:, :, 0:D], ins["L0_gnn_WT"].rearrange("(k p) o -> p k o", p=128), allow_slow_non_contiguous=True).then_inc(w_in, 16)
                act.wait_ge(stats, 1)
                s.activation(rstd[:], rstd[:], ACT.Sqrt).then_inc(sq, 1)
                act.wait_ge(w_in, 64)
                act.wait_ge(wa_ok, 1)
                s.activation(wx[:, :, D:D + 2 * H], pW[:, :, 0:2 * H], ACT.Copy).then_inc(wx_ok, 1)

            @block.tensor
            def _(pe):
                t_ = nc.tensor
                pe.wait_ge(below_ok, 1)
                bl = below[:, :].rearrange("p (n t) -> p t n", t=NT)
                for t in range(NT):
                    last = t_.matmul(pC[:, t:t + 1], bl[:, t, :], ones[:], start=True, stop=True)
                last.then_inc(counted, 1)
                pe.wait_ge(ablk_ok, 1)
                for i in range(2):
                    for k in range(2):
                        last = t_.matmul(pW[:, i, 0:2 * H], wn[:, k, i * 128:(i + 1) * 128], ablk[:, k, :], start=(k == 0), stop=(k == 1))
                last.then_inc(wa_ok, 1)


def order(nc, K, dr, kept):
    with ExitStack() as stack:
        m = Mem(nc, stack)
        x, row, wx, RB = kept.x, kept.row, kept.wx, kept.RB
        rstd, nbias = kept.norm.rstd, kept.norm.nbias
        W = 2 * RB
        OHW = NT * NB
        xn = m.sb("o_xn", [P, 2, D])
        xnT = m.sb("o_xnT", [128, 2, 2, P])
        rec = m.sb("o_rec", [P, NT, 4], I32)
        nxt = m.sb("o_nxt", [P, NT], I32)
        rpi = m.sb("o_rpi", [P, NT], I32)
        deg = m.sb("o_deg", [P, NT])
        bkt = m.sb("o_bkt", [P, NT])
        hot = m.sb("o_hot", [P, NT, NB])
        tot = m.sb("o_tot", [P, NB, NT])
        exc = m.sb("o_exc", [P, NB, NT])
        rank = m.sb("o_rank", [P, NT, NB])
        posf = m.sb("o_posf", [P, NT])
        pos = m.sb("o_pos", [P, NT], I32)
        zero = m.sb("o_zero", [P, OHW])
        R = 5
        idx = [m.sb(f"o_idx{r}", [P, 1], I32) for r in range(R)]
        srow = [m.sb(f"o_srow{r}", [P, 4], I32) for r in range(R)]
        dmax = m.sb("o_dmax", [QT, 1])
        ci = m.sb("o_ci", [QT, 1], I32)
        cf = m.sb("o_cf", [QT, 1])
        cr = m.sb("o_cr", [QT, 1])
        tail = m.sb("o_tail", [1, 4], I32)
        pT = [m.ps(f"o_pT{r}", [128, 2, 256]) for r in range(2)]
        pH = [m.ps(f"o_pH{r}", [P, 512]) for r in range(2)]
        pR = m.ps("o_pR", [P, 512])
        pTt = m.ps("o_pTt", [P, 512])
        pD = m.ps("o_pD", [QT, Q])
        pC = m.ps("o_pC", [1, 64])

        r_in = m.sem("o_r_in"); vch = m.sem("o_vch"); hot_ok = m.sem("o_hot_ok"); mm_ok = m.sem("o_mm_ok"); taken = m.sem("o_taken")
        ready = m.sem("o_ready"); sent = [m.sem(f"o_sent{r}") for r in range(R)]; pads = m.sem("o_pads"); pt_in = m.sem("o_pt_in")
        deg_ok = m.sem("o_deg_ok"); dT_ok = m.sem("o_dT_ok"); cnt_ok = m.sem("o_cnt_ok"); pre_ok = m.sem("o_pre_ok"); pace = m.sem("o_pace")
        iota_ok = m.sem("o_iota_ok")
        xn_ok = m.sem("o_xn_ok"); t_ok = m.sem("o_t_ok"); xnT_ok = m.sem("o_xnT_ok"); h_ok = m.sem("o_h_ok")
        row_ok = m.sem("o_row_ok"); row_out = [m.sem(f"o_row_out{j}") for j in range(RB)]
        rows0 = dr["rows0"][0:N, :].rearrange("(p t) c -> p t c", t=NT)
        cols = [(a, min(a + 8, NT)) for a in range(0, NT, 8)]

        with nc.Block() as block:
            @block.sync
            def _(sp):
                sp.dma_start(rpi[:], dr["rp"][:, 0:N].rearrange("o (p t) -> (o p) t", t=NT)).then_inc(r_in, 16)
                sp.dma_start(nxt[:], dr["rp"][:, 1:N + 1].rearrange("o (p t) -> (o p) t", t=NT)).then_inc(r_in, 16)
                sp.dma_start(dr["noderec"][N:NPAD, :], K["padrec"][:]).then_inc(pads, 16)
                with sp.Fori(0, NT // W) as u:
                    for r in range(W):
                        sp.wait_ge(row_ok, W * u + (r + 1))
                        sp.dma_start(rows0[:, bass.ds(W * u + r, 1), :].rearrange("p a c -> p (a c)"), row[:, r % RB, :]).then_inc(row_out[r % RB], 16)
                for j in range(RB):
                    sp.wait_ge(row_out[j], 16 * (NT // RB))
                sp.wait_ge(pads, 16)
                for r in range(R):
                    sp.wait_ge(sent[r], 16 * (NT // R))
                sp.dma_start(K["pt"][:], dr["noderec"].rearrange("(t q) c -> q t c", q=Q)).then_inc(pt_in, 16)
                sp.wait_ge(pt_in, 16)

            @block.scalar
            def _(act):
                s = nc.scalar

                def normed(u, r):
                    tc = bass.ds(W * u + r, 1)
                    s.activation(xn[:, r % 2, :], x[:, tc, :].rearrange("p a c -> p (a c)"), ACT.Identity,
                                 bias=nbias[:, tc], scale=rstd[:, tc]).then_inc(xn_ok, 1)

                def turned(u, r):
                    act.wait_ge(t_ok, W * u + (r + 1))
                    s.activation(xnT[:, r % 2, :, :], pT[r % 2][:, :, 0:P], ACT.Copy).then_inc(xnT_ok, 1)

                def rows(u, r, early):
                    act.wait_ge(h_ok, W * u + (r + 1))
                    if not early:
                        act.sem_inc(pace, 1)
                        act.wait_ge(row_out[r % RB], 16 * (W // RB) * u + 16 * (r // RB))
                    s.activation(row[:, r % RB, 0:H * VW].rearrange("p (h c) -> p h c", h=H)[:, :, 0:HD],
                                 pH[r % 2][:, 0:D].rearrange("p (h c) -> p h c", h=H), ACT.Copy)
                    s.activation(row[:, r % RB, H * VW:RW], pH[r % 2][:, D:D + 2 * H], ACT.Copy).then_inc(row_ok, 1)

                def group(u, first, last_group):
                    for r in range(W):
                        if r < W - 1 or not last_group:
                            normed(u, r + 1)
                        turned(u, r)
                        if r > 0:
                            rows(u, r - 1, first and r - 1 < RB)
                    rows(u, W - 1, False)
                normed(0, 0)
                paired(act, NT // W, group)

            @block.gpsimd
            def _(pool):
                pool.iota(rec[:, :, 0], pattern=[[1, NT]], base=0, channel_multiplier=NT).then_inc(iota_ok, 1)

                def scatter(u, r):
                    pool.wait_ge(ready, u * R + (r + 1))
                    pool.sem_inc(pace, 1)
                    pool.indirect_dma_start(out=dr["noderec"], out_offset=bass.IndirectOffsetOnAxis(ap=idx[r][:, 0:1], axis=0),
                                            in_=srow[r][:], in_offset=None).then_inc(sent[r], 16)
                with pool.Fori(0, NT // R) as u:
                    for r in range(R):
                        scatter(u, r)

            @block.vector
            def _(dve):
                v = nc.vector
                ch = Chain(dve, vch)
                v.memset(zero[:], 0.0)
                dve.wait_ge(r_in, 32)
                dve.wait_ge(iota_ok, 1)
                ch.link(v.tensor_tensor(deg[:], nxt[:], rpi[:], ALU.subtract))
                v.tensor_copy(rec[:, :, 1], rpi[:])
                v.tensor_copy(rec[:, :, 2], deg[:])
                ch.link(v.tensor_copy(rec[:, :, 3], deg[:]))
                ch.link(v.tensor_scalar(bkt[:], deg[:], float(NB - 1), None, ALU.min))
                v.tensor_tensor(hot[:], over(bkt[:], 2, NB), over(K["iota64"][0:P, :], 1, NT), ALU.is_equal).then_inc(hot_ok, 1)
                for j, (a, b) in enumerate(cols):
                    w = (b - a) * NB
                    dve.wait_ge(mm_ok, j + 1)
                    v.tensor_copy(rank[:, a:b, :].rearrange("p t b -> p (t b)"), pR[:, 0:w])
                    v.tensor_copy(tot[:, :, a:b].rearrange("p b t -> p t b"), pTt[:, 0:w].rearrange("p (t b) -> p t b", b=NB)).then_inc(taken, 1)
                dve.wait_ge(taken, len(cols))
                flat = "p b t -> p (b t)"
                ch.link(v.tensor_tensor_scan(exc[:].rearrange(flat), tot[:].rearrange(flat), zero[:], 0.0, ALU.add, ALU.add))
                ch.link(v.tensor_tensor(exc[:].rearrange(flat), exc[:].rearrange(flat), tot[:].rearrange(flat), ALU.subtract))
                ch.link(v.tensor_tensor(rank[:], rank[:], exc[:].rearrange("p b t -> p t b"), ALU.add))
                ch.link(v.tensor_tensor(rank[:], rank[:], hot[:], ALU.mult))
                ch.link(v.reduce_sum(posf[:], rank[:], axis=AX))
                ch.link(v.tensor_copy(pos[:], posf[:]))

                def stage(u, first):
                    for r in range(R):
                        t = u * R + r
                        if not first:
                            dve.wait_ge(sent[r], 16 * u)
                            dve.sem_inc(pace, 1)
                        v.tensor_copy(srow[r][:], rec[:, bass.ds(t, 1), :].rearrange("p a c -> p (a c)"))
                        v.tensor_copy(idx[r][:], pos[:, bass.ds(t, 1)]).then_inc(ready, 1)
                peeled(dve, NT // R, stage)
                dve.wait_ge(pt_in, 16)
                v.tensor_copy(K["rp"][:], K["pt"][:, :, 1])
                v.tensor_copy(K["deg"][:], K["pt"][:, :, 2]).then_inc(deg_ok, 1)
                dve.wait_ge(dT_ok, 1)
                ch.link(v.reduce_max(dmax[:], pD[:], axis=AX))
                ch.link(v.tensor_scalar(dmax[:], dmax[:], float(C - 1), None, ALU.add))
                ch.link(v.tensor_scalar(ci[:], dmax[:], 1.0 / C, None, ALU.mult))
                ch.link(v.tensor_copy(cf[:], ci[:]))
                ch.link(v.scalar_tensor_tensor(cr[:], cf[:], -float(C), dmax[:], ALU.mult, ALU.add))
                ch.link(v.tensor_scalar(dmax[:], cr[:], 0.0, None, ALU.is_lt))
                ch.link(v.tensor_tensor(cf[:], cf[:], dmax[:], ALU.subtract))
                ch.link(v.tensor_scalar(dmax[:], cr[:], float(C), None, ALU.is_ge))
                ch.link(v.tensor_tensor(cf[:], cf[:], dmax[:], ALU.add))
                v.tensor_scalar(cf[:], cf[:], 2.0, None, ALU.max).then_inc(cnt_ok, 1)
                dve.wait_ge(pre_ok, 1)
                v.tensor_copy(K["ct"][:, 0:QT], pC[:, 0:QT])
                ch.link(v.tensor_scalar(tail[:, 0:1], pC[:, QT:QT + 1], 3.0, None, ALU.add))
                ch.link(v.tensor_scalar(tail[:, 1:2], tail[:, 0:1], 2, None, ALU.arith_shift_right))
                v.tensor_scalar(K["ct"][:, QT + 1:QT + 2], tail[:, 1:2], -2.0, None, ALU.add)
                ch.link(v.tensor_scalar(K["ct"][:, QT:QT + 1], tail[:, 1:2], 4.0, None, ALU.mult))

            @block.tensor
            def _(pe):
                t_ = nc.tensor
                pe.wait_ge(hot_ok, 1)
                for j, (a, b) in enumerate(cols):
                    w = (b - a) * NB
                    h = hot[:, a:b, :].rearrange("p t b -> p (t b)")
                    if j:
                        pe.wait_ge(taken, j)
                    t_.matmul(pR[:, 0:w], K["tri"][0:P, 0:P], h, start=True, stop=True)
                    t_.matmul(pTt[:, 0:w], K["ones"][0:P, 0:P], h, start=True, stop=True).then_inc(mm_ok, 1)

                def turn(t, b):
                    pe.wait_ge(xn_ok, t + 1)
                    for k in range(2):
                        last = t_.transpose(pT[b][:, k, 0:P], xn[:, b, k * 128:(k + 1) * 128], K["ident"][0:P, 0:P])
                    last.then_inc(t_ok, 1)

                def product(t, b, early):
                    pe.wait_ge(xnT_ok, t + 1)
                    if not early:
                        pe.sem_inc(pace, 1)
                        pe.wait_ge(row_ok, t - 1)
                    for k in range(2):
                        last = t_.matmul(pH[b][:, 0:D + 2 * H], xnT[:, b, k, :], wx[:, k, :], start=(k == 0), stop=(k == 1))
                    last.then_inc(h_ok, 1)

                def group(u, first, last_group):
                    for r in range(W):
                        if r < W - 1 or not last_group:
                            turn(W * u + (r + 1), (r + 1) % 2)
                        product(W * u + r, r % 2, first and r < 2)
                turn(0, 0)
                paired(pe, NT // W, group)
                pe.wait_ge(deg_ok, 1)
                t_.transpose(pD[:], K["deg"][:], K["ident"][:]).then_inc(dT_ok, 1)
                pe.wait_ge(cnt_ok, 1)
                t_.matmul(pC[0:1, 0:QT + 1], cf[:], K["tri"][0:QT, 0:QT + 1], start=True, stop=True).then_inc(pre_ok, 1)


def groups(eng, K):
    return eng.value_load(K["ct"][0:1, QT + 1:QT + 2], min_val=1, max_val=CMAX // 4 - 3)


def edge_index(nc, K, eidx):
    with ExitStack() as stack:
        m = Mem(nc, stack)
        T = lambda n: m.sem("x_" + n)
        start = m.sb("x_start", [1, QT])
        v_ = m.sb("x_v", [Q, QT])
        dv = m.sb("x_dv", [Q, QT])
        dvT = m.sb("x_dvT", [QT, Q])
        lo = m.sb("x_lo", [QT, 1])
        nb_i = m.sb("x_nb", [1, 1], I32)
        iota = m.sb("x_iota", [Q, BLK])
        edge = m.sb("x_edge", [Q, BLK])
        step = m.sb("x_step", [QT, BLK])
        iota_ok = T("iota_ok"); s_ok = T("s_ok"); b_ok = T("b_ok"); d_ok = T("d_ok"); t_ok = T("t_ok"); nb_ok = T("nb_ok")
        step_ok = T("step_ok"); e_ok = T("e_ok"); vch = T("vch"); bch = T("bch"); pace = T("pace")
        pB = m.ps("x_pB", [Q, QT])
        pV = m.ps("x_pV", [QT, Q])
        pL = m.ps("x_pL", [QT, 1])
        pE = m.ps("x_pE", [Q, BLK])
        blocks = lambda eng: eng.value_load(nb_i[0:1, 0:1], min_val=1, max_val=-(-CMAX // BLK))
        with nc.Block() as block:
            @block.gpsimd
            def _(pool):
                pool.iota(iota[:], pattern=[[1, BLK]], base=0, channel_multiplier=0, allow_small_or_imprecise_dtypes=True).then_inc(iota_ok, 1)

            @block.tensor
            def _(pe):
                t_ = nc.tensor
                pe.wait_ge(s_ok, 1)
                t_.matmul(pB[:], K["ones"][0:1, :], start[:], start=True, stop=True)
                t_.matmul(pL[:], start[:], K["ones"][0:1, 0:1], start=True, stop=True).then_inc(b_ok, 1)
                pe.wait_ge(d_ok, 1)
                t_.transpose(pV[:], dv[:], K["ident"][:]).then_inc(t_ok, 1)
                pe.wait_ge(nb_ok, 1)
                with pe.Fori(0, blocks(pe)) as k:
                    pe.wait_ge(step_ok, k + 1)
                    t_.matmul(pE[:], dvT[:], step[:], start=True, stop=True).then_inc(e_ok, 1)

            @block.vector
            def _(dve):
                v = nc.vector
                ch = Chain(dve, vch)
                v.tensor_copy(start[:], K["ct"][0:1, 0:QT]).then_inc(s_ok, 1)
                ch.link(v.tensor_scalar(nb_i[:], K["ct"][0:1, QT:QT + 1], float(BLK - 1), None, ALU.add))
                ch.link(v.tensor_scalar(nb_i[:], nb_i[:], BLOG, None, ALU.arith_shift_right))
                dve.sem_inc(nb_ok, 1)
                dve.wait_ge(b_ok, 1)
                ch.link(v.scalar_tensor_tensor(v_[:], pB[:], -float(C), K["rp"][:], ALU.mult, ALU.add))
                v.tensor_copy(lo[:], pL[:])
                v.tensor_copy(dv[:, 0:1], v_[:, 0:1])
                v.tensor_tensor(dv[:, 1:QT], v_[:, 1:QT], v_[:, 0:QT - 1], ALU.subtract).then_inc(d_ok, 1)
                dve.wait_ge(iota_ok, 1)
                v.tensor_scalar(edge[:], iota[:], float(C), None, ALU.mult)
                dve.wait_ge(t_ok, 1)
                ch.link(v.tensor_copy(dvT[:], pV[:]))
                NL = 4
                with dve.Fori(0, blocks(dve)) as k:
                    bc = Chain(dve, bch, NL * k)
                    v.tensor_scalar(step[:], iota[0:QT, :], lo[:], None, ALU.is_ge).then_inc(step_ok, 1)
                    dve.wait_ge(e_ok, k + 1)
                    dve.sem_inc(pace, 1)
                    e = eidx[:, bass.ds(k * BLK, BLK)]
                    bc.link(v.tensor_tensor(e, pE[:], edge[:], ALU.add))
                    bc.link(v.tensor_scalar(e, e, float(E - 1), None, ALU.min))
                    bc.link(v.tensor_scalar(lo[:], lo[:], -float(BLK), None, ALU.add))
                    bc.link(v.tensor_scalar(edge[:], edge[:], float(C * BLK), None, ALU.add))


def graph(nc, K, ins, dr, layer):
    first_layer = layer == 0
    rows_d, agg_d = dr[f"rows{layer}"], dr[f"agg{layer}"]
    L = f"g{layer}_"
    with ExitStack() as stack:
        m = Mem(nc, stack)
        if first_layer:
            eidx = m.sb(L + "eidx", [Q, -(-CMAX // BLK) * BLK])
            edge_index(nc, K, eidx)
        R = 4
        HR = 4
        DW = RW if first_layer else H
        dall = m.sb(L + "dall", [Q, QT, DW if first_layer else D])
        sdst = m.sb(L + "sdst", [Q, QT, H])
        nidx = [m.sb(f"{L}nidx{r}", [Q, 1], I32) for r in range(HR)]
        nrow = m.sb(L + "nrow", [Q, HR, DW])
        orow = m.sb(L + "orow", [Q, HR, D])
        recs = m.sb(L + "recs", [Q, R, REC])
        rows = m.sb(L + "rows", [Q, R, C, RW])
        msg = m.sb(L + "msg", [Q, 2, C, H * VW])
        al = m.sb(L + "al", [Q, 2, (C + 1) * H])
        part = m.sb(L + "part", [Q, C * H])
        lowest = m.sb(L + "lowest", [Q, H])
        mask = m.sb(L + "mask", [Q, C])
        left = m.sb(L + "left", [Q, 1])
        dd = m.sb(L + "dd", [Q, 2, (C + 1) * H])
        pp = m.sb(L + "pp", [Q, 2, (C + 1) * H])
        acc = m.sb(L + "acc", [Q, H * VW])
        den = m.sb(L + "den", [Q, H])
        pA = m.ps(L + "pA", [Q, 2, 512])
        if first_layer:
            ew = m.sb(L + "ew", [REC + 1, C, D])
            prod = m.sb(L + "prod", [Q, 2, C * D])
            recT = m.sb(L + "recT", [REC + 1, 2, Q])
            pE = m.ps(L + "pE", [Q, C * D])
            pRT = m.ps(L + "pRT", [REC, 2, 512])

        S = lambda n: m.sem(L + n)
        nready = S("nready"); ngot = [S(f"ngot{r}") for r in range(HR)]
        rec_in = [S(f"rec_in{r}") for r in range(R)]; rows_in = [S(f"rows_in{r}") for r in range(R)]
        rows_ok = S("rows_ok"); w_in = S("w_in"); w_zero = S("w_zero"); pace = S("pace"); vch = S("vch"); tch = S("tch"); cch = S("cch"); och = S("och"); uch = S("uch")
        recT_ps = S("recT_ps"); recT_ok = S("recT_ok"); enc_ok = S("enc_ok"); enc_free = S("enc_free")
        dd_ok = S("dd_ok"); pp_ok = S("pp_ok"); msg_ok = S("msg_ok"); agg_ok = S("agg_ok")
        oready = S("oready"); oput = [S(f"oput{r}") for r in range(HR)]
        NG = QT // HR
        TAIL = QT - NG * HR

        if first_layer:
            ridx = [m.sb(f"{L}ridx{r}", [Q, 1], I32) for r in range(R)]
            ridx_ok = S("ridx_ok"); rec_free = S("rec_free"); rec_put = [S(f"rec_put{r}") for r in range(R)]
        with nc.Block() as block:
            src_d = rows_d if first_layer else dr["sv1"]

            @block.gpsimd
            def _(pool):
                def gather(u, r):
                    pool.wait_ge(nready, u * HR + (r + 1))
                    pool.sem_inc(pace, 1)
                    pool.indirect_dma_start(out=nrow[:, r, :], out_offset=None, in_=src_d,
                                            in_offset=bass.IndirectOffsetOnAxis(ap=nidx[r][:, 0:1], axis=0)
                                            ).then_inc(ngot[r], 16)
                with pool.Fori(0, NG) as u:
                    for r in range(HR):
                        gather(u, r)
                for r in range(TAIL):
                    gather(NG, r)

            @block.vector
            def _(dve):
                v = nc.vector

                def put_index(t, r):
                    v.tensor_copy(nidx[r][:], K["pt"][:, bass.ds(t, 1), 0]).then_inc(nready, 1)

                def keep(u, r, more):
                    t = u * HR + r
                    dve.wait_ge(ngot[r], 16 * u + 16)
                    dve.sem_inc(pace, 1)
                    row = nrow[:, r:r + 1, :]
                    if first_layer:
                        v.tensor_copy(dall[:, bass.ds(t, 1), :], row)
                    else:
                        v.tensor_copy(sdst[:, bass.ds(t, 1), :], row)
                    if more:
                        put_index(t + HR, r)
                for r in range(HR):
                    put_index(r, r)
                with dve.Fori(0, NG - 1) as u:
                    for r in range(HR):
                        keep(u, r, True)
                for r in range(HR):
                    keep(NG - 1, r, r < TAIL)
                for r in range(TAIL):
                    keep(NG, r, False)
                Chain(dve, vch).link(v.memset(lowest[:], -BIG / 10))
                if first_layer:
                    v.tensor_copy(sdst[:], dall[:, :, H * VW + H:RW])

        with nc.Block() as block:
            @block.sync
            def _(sp):
                n2 = groups(sp, K)
                if first_layer:
                    sp.wait_ge(w_zero, 1)
                    for j in range(C):
                        sp.dma_start(ew[C + 3 * j:C + 3 * j + 3, j, :], ins["L0_gnn_edge_WT"]).then_inc(w_in, 16)
                        sp.dma_start(ew[REC:REC + 1, j, :], ins["L0_gnn_edge_b"].unsqueeze(0)).then_inc(w_in, 16)

                def load(u, r):
                    sp.dma_start(recs[:, r, :], dr["slots"][bass.ds(4 * u + r, 1), :, :].rearrange("a q c -> (a q) c")).then_inc(rec_in[r], 16)

                def relay(u, r):
                    sp.wait_ge(rows_in[r], 16 * C * (u + 1))
                    sp.sem_inc(rows_ok, 1)
                if not first_layer:
                    for r in range(R):
                        load(0, r)
                    with sp.Fori(0, n2 + 1) as u:
                        for r in range(R):
                            relay(u, r)
                            load(u + 1, r)
                    for r in range(R):
                        relay(n2 + 1, r)

                def keep(u, first):
                    for r in range(R):
                        relay(u, r)
                        sp.dma_start(dr["slots"][bass.ds(4 * u + r, 1), :, :].rearrange("a q c -> (a q) c"), recs[:, r, :]).then_inc(rec_put[r], 16)
                        sp.wait_ge(recT_ps, 4 * u + (r + 1))
                        sp.sem_inc(pace, 1)
                        if r > 0:
                            sp.wait_ge(rec_put[r - 1], 16 * u + 16)
                            sp.sem_inc(rec_free, 1)
                        elif not first:
                            sp.wait_ge(rec_put[R - 1], 16 * u)
                            sp.sem_inc(rec_free, 1)
                if first_layer:
                    peeled(sp, n2 + 2, keep)
                    for r in range(R):
                        sp.wait_ge(rec_put[r], 16 * (n2 + 2))
                        sp.sem_inc(pace, 1)

            @block.gpsimd
            def _(pool):
                n2 = groups(pool, K)

                def record(u, r, early):
                    u, r = u + r // R, r % R
                    pool.wait_ge(ridx_ok, 4 * u + (r + 1))
                    pool.sem_inc(pace, 1)
                    if not early:
                        pool.wait_ge(rec_free, 4 * (u - 1) + (r + 1))
                        pool.sem_inc(pace, 1)
                    pool.indirect_dma_start(out=recs[:, r, :], out_offset=None, in_=dr["rec"],
                                            in_offset=bass.IndirectOffsetOnAxis(ap=ridx[r][:, 0:1], axis=0)
                                            ).then_inc(rec_in[r], 16)

                def gather(u, first, last_group):
                    for r in range(R):
                        pool.wait_ge(rec_in[r], 16 * u + 16)
                        pool.sem_inc(pace, 1)
                        if not first:
                            pool.wait_ge(msg_ok, 4 * (u - 1) + (r + 1))
                            pool.sem_inc(pace, 1)
                        for j in range(C):
                            pool.indirect_dma_start(out=rows[:, r, j, :], out_offset=None, in_=rows_d,
                                                    in_offset=bass.IndirectOffsetOnAxis(ap=recs[:, r, j:j + 1].bitcast(I32), axis=0)
                                                    ).then_inc(rows_in[r], 16)
                        if first_layer and (r < R - 2 or not last_group):
                            record(u, r + 2, first and r < 2)
                if first_layer:
                    record(0, 0, True)
                    record(0, 1, True)
                gather(0, True, False)
                with pool.Fori(1, n2 + 1) as u:
                    gather(u, False, False)
                gather(n2 + 1, False, True)

            @block.tensor
            def _(pe):
                t_ = nc.tensor
                n2 = groups(pe, K)

                def transpose(u, r):
                    u, r = u + r // R, r % R
                    pe.wait_ge(rec_in[r], 16 * u + 16)
                    t_.transpose(pRT[:, r % 2, 0:Q], recs[:, r, :], K["ident"][:]).then_inc(recT_ps, 1)

                def encode(i, b, first):
                    pe.wait_ge(recT_ok, i + 1)
                    if not first:
                        pe.wait_ge(enc_free, i)
                    for c in range(0, C * D, 512):
                        cols = slice(c, min(c + 512, C * D))
                        last = t_.matmul(pE[:, cols], recT[:, b, :], ew[:].rearrange("p c d -> p (c d)")[:, cols], start=True, stop=True)
                    last.then_inc(enc_ok, 1)

                def aggregate(u, r):
                    pe.wait_ge(msg_ok, 4 * u + (r + 1))
                    for j in range(C):
                        last = t_.matmul(pA[:, r % 2, 0:H * VW], K["ident"][:], msg[:, r % 2, j, :], start=(j == 0), stop=(j == C - 1))
                    last.then_inc(agg_ok, 1)

                def group(u, first, last_group):
                    for r in range(R):
                        if first_layer:
                            if r < R - 2 or not last_group:
                                transpose(u, r + 2)
                            if r < R - 1 or not last_group:
                                encode(4 * u + (r + 1), (r + 1) % 2, False)
                        if r > 0:
                            aggregate(u, r - 1)
                        elif not first:
                            aggregate(u - 1, R - 1)
                if first_layer:
                    pe.wait_ge(w_in, 32 * C)
                    transpose(0, 0)
                    transpose(0, 1)
                    encode(0, 0, True)
                group(0, True, False)
                with pe.Fori(1, n2 + 1) as u:
                    group(u, False, False)
                group(n2 + 1, False, True)
                aggregate(n2 + 1, R - 1)

            @block.scalar
            def _(act):
                s = nc.scalar
                n2 = groups(act, K)

                def index(u, r, early):
                    u, r = u + r // R, r % R
                    if not early:
                        act.wait_ge(rec_in[r], 16 * u)
                        act.sem_inc(pace, 1)
                    s.activation(ridx[r][:], eidx[:, bass.ds(4 * u + r, 1)], ACT.Copy).then_inc(ridx_ok, 1)

                def record(i, b, early):
                    act.wait_ge(recT_ps, i + 1)
                    if not early:
                        act.sem_inc(pace, 1)
                        act.wait_ge(enc_ok, i - 1)
                    s.activation(recT[0:REC, b, :], pRT[:, b, 0:Q], ACT.Copy).then_inc(recT_ok, 1)

                def encoding(i, b):
                    act.wait_ge(enc_ok, i + 1)
                    act.sem_inc(pace, 1)
                    s.activation(prod[:, b, :], pE[:], ACT.Relu).then_inc(enc_free, 1)

                def group(u, last_group):
                    for r in range(R):
                        i = 4 * u + r
                        if first_layer:
                            if r < R - 2 or not last_group:
                                record(4 * u + (r + 2), r % 2, False)
                            if r < R - 1 or not last_group:
                                encoding(4 * u + (r + 1), (r + 1) % 2)
                        act.wait_ge(dd_ok, 4 * u + (r + 1))
                        s.activation(pp[:, r % 2, :], dd[:, r % 2, :], ACT.Exp).then_inc(pp_ok, 1)
                        if first_layer and not last_group:
                            index(u + 1, r, False)
                if first_layer:
                    act.wait_ge(w_zero, 2)
                    for r in range(R):
                        index(0, r, True)
                    record(0, 0, True)
                    record(1, 1, True)
                    encoding(0, 0)
                group(0, False)
                with act.Fori(1, n2 + 1) as u:
                    group(u, False)
                group(n2 + 1, True)

            @block.vector
            def _(dve):
                v = nc.vector
                if first_layer:
                    v.memset(ew[:], 0.0).then_inc(w_zero, 1)
                    v.memset(recT[:], 1.0).then_inc(w_zero, 1)
                NL = 8 if first_layer else 5
                TL = 4
                heads = lambda ap: ap.rearrange("p (c h) -> p c h", h=H)
                row_of = lambda ap: ap.rearrange("p a h -> p (a h)")
                iota = K["iota64"][:, 0:C]
                acc3 = acc[:].rearrange("p (h c) -> p h c", h=H)

                def messages(i):
                    b2, b4 = bass.ds(i % 2, 1), bass.ds(i % R, 1)
                    dve.wait_ge(pp_ok, i + 1)
                    dve.sem_inc(pace, 1)
                    pv = heads(row_of(pp[:, b2, 0:C * H]))
                    row4 = rows[:, b4, :, 0:H * VW].rearrange("p a c (h w) -> p (a c) h w", h=H)
                    out4 = msg[:, b2, :, :].rearrange("p a c (h w) -> p (a c) h w", h=H)
                    v.tensor_tensor(out4, row4, over(pv, 3, VW), ALU.mult).then_inc(msg_ok, 1)

                def rescale(i):
                    dve.wait_ge(uch, 2 * i + 3)
                    dve.sem_inc(pace, 1)
                    v.tensor_tensor(acc3, acc3, over(row_of(pp[:, bass.ds(i % 2, 1), C * H:]), 2, VW), ALU.mult).then_inc(uch, 1)

                def gather_in(i):
                    dve.wait_ge(agg_ok, i + 1)
                    dve.sem_inc(pace, 1)
                    dve.wait_ge(uch, 2 * i + 4)
                    dve.sem_inc(pace, 1)
                    v.tensor_tensor(acc[:], acc[:], row_of(pA[:, bass.ds(i % 2, 1), 0:H * VW]), ALU.add).then_inc(uch, 1)

                def finish(t, i):
                    dve.wait_ge(uch, 2 * i + 5)
                    dve.sem_inc(pace, 1)
                    tc = Chain(dve, tch, t * TL)
                    tc.link(v.tensor_scalar(den[:], acc3[:, :, HD], 1e-10, None, ALU.max))
                    tc.link(v.reciprocal(den[:], den[:]))
                    tc.link(v.tensor_tensor(dall[:, bass.ds(t, 1), 0:D].rearrange("p a (h c) -> p (a h) c", h=H),
                                            acc3[:, :, 0:HD], over(den[:], 2, HD), ALU.mult))
                    tc.link(v.memset(acc[:], 0.0))

                def chunk(t, i, opens, closes=None):
                    start = isinstance(i, int) and i == 0
                    b2 = bass.ds(i % 2, 1)
                    ch = Chain(dve, cch, i * NL)
                    alb = row_of(al[:, b2, :])
                    mnb = row_of(al[:, bass.ds((i + 1) % 2, 1), C * H:])
                    sc = heads(alb[:, 0:C * H])
                    sd = over(row_of(sdst[:, bass.ds(t, 1), :]), 1, C)
                    src = rows[:, bass.ds(i % R, 1), :, H * VW:H * VW + H].rearrange("p a c w -> p (a c) w")
                    if opens:
                        if not start:
                            dve.wait_ge(dd_ok, i)
                            dve.sem_inc(pace, 1)
                        v.tensor_copy(alb[:, C * H:], lowest[:])
                        Chain(dve, och, t).link(v.tensor_copy(left[:], K["deg"][:, bass.ds(t, 1)]))
                    v.tensor_scalar(mask[:], iota, left[:], -BIG, ALU.is_ge, ALU.mult)
                    if first_layer:
                        dst = dall[:, bass.ds(t, 1), 0:H * VW].rearrange("p a (h c) -> p (a h) c", h=H)[:, :, 0:HD]
                        pr = row_of(prod[:, b2, :])
                        p4 = pr.rearrange("p (c h w) -> p c h w", c=C, h=H)
                        dve.wait_ge(enc_free, i + 1)
                        dve.sem_inc(pace, 1)
                        ch.link(v.tensor_tensor(p4, p4, over(dst, 1, C), ALU.mult), wait=False)
                    ssc = heads(part[:]) if first_layer else sc
                    dve.wait_ge(rows_ok, i + 1)
                    dve.sem_inc(pace, 1)
                    ch.link(v.tensor_tensor(ssc, src, sd, ALU.add), wait=False)
                    if first_layer:
                        ch.wait(1)
                        ch.link(v.reduce_sum(alb[:, 0:C * H], pr.rearrange("p (g c) -> p g c", c=HD), axis=AX), wait=False)
                    ch.wait(2 if first_layer else 1)
                    ch.link(v.tensor_tensor(ssc, ssc, over(mask[:], 2, H), ALU.add), wait=False)
                    if first_layer:
                        if not start:
                            rescale(i - 1)
                        ch.wait()
                        ch.link(v.tensor_tensor(sc, sc, ssc, ALU.add), wait=False)
                    ch.wait()
                    ch.link(v.scalar_tensor_tensor(sc, sc, 0.2, sc, ALU.mult, ALU.max))
                    ch.link(v.reduce_max(mnb, alb.rearrange("p (c h) -> p h c", h=H), axis=AX), wait=False)
                    ch.wait()
                    v.tensor_tensor(heads(row_of(dd[:, b2, :])), heads(alb), over(mnb, 1, C + 1), ALU.subtract).then_inc(dd_ok, 1)
                    ch.link(v.tensor_scalar(left[:], left[:], -float(C), None, ALU.add), wait=False)
                    assert ch.n == NL, ch.n
                    if first_layer:
                        if not start:
                            gather_in(i - 1)
                        if closes is not None:
                            finish(closes, i - 1)
                        messages(i)
                    else:
                        if not start:
                            rescale(i - 1)
                        messages(i)
                        if not start:
                            gather_in(i - 1)
                        if closes is not None:
                            finish(closes, i - 1)
                    ch.wait()

                def bounds(t):
                    return (dve.value_load(K["ct"][0:1, bass.ds(t, 1)], min_val=0, max_val=CMAX - 2),
                            dve.value_load(K["ct"][0:1, bass.ds(t + 1, 1)], min_val=2, max_val=CMAX))

                v.memset(acc[:], 0.0).then_inc(uch, 3)
                chunk(0, 0, True)
                with dve.Fori(0, QT - 1) as t:
                    lo, hi = bounds(t)
                    with dve.Fori(lo + 1, hi) as i:
                        chunk(t, i, False)
                    chunk(t + 1, hi, True, closes=t)
                lo, hi = bounds(QT - 1)
                with dve.Fori(lo + 1, hi) as i:
                    chunk(QT - 1, i, False)
                rescale(hi - 1)
                gather_in(hi - 1)
                finish(QT - 1, hi - 1)

        with nc.Block() as block:
            @block.gpsimd
            def _(pool):
                def scatter(u, r):
                    pool.wait_ge(oready, u * HR + (r + 1))
                    pool.sem_inc(pace, 1)
                    pool.indirect_dma_start(out=agg_d, out_offset=bass.IndirectOffsetOnAxis(ap=nidx[r][:, 0:1], axis=0),
                                            in_=orow[:, r, :], in_offset=None).then_inc(oput[r], 16)
                with pool.Fori(0, NG) as u:
                    for r in range(HR):
                        scatter(u, r)
                for r in range(TAIL):
                    scatter(NG, r)
                for r in range(HR):
                    pool.wait_ge(oput[r], 16 * (NG + (r < TAIL)))

            @block.vector
            def _(dve):
                v = nc.vector

                def stage(u, r, first):
                    t = u * HR + r
                    if not first:
                        dve.wait_ge(oput[r], 16 * u)
                        dve.sem_inc(pace, 1)
                    v.tensor_copy(orow[:, r:r + 1, :], dall[:, bass.ds(t, 1), 0:D])
                    v.tensor_copy(nidx[r][:], K["pt"][:, bass.ds(t, 1), 0]).then_inc(oready, 1)

                def group(u, first):
                    for r in range(HR):
                        stage(u, r, first)
                peeled(dve, NG, group)
                for r in range(TAIL):
                    stage(NG, r, False)


def paired(eng, n, body):
    body(0, True, False)
    with eng.Fori(1, n - 1) as u:
        body(u, False, False)
    body(n - 1, False, True)


def slice_ffn(nc, K, ins, dr):
    with ExitStack() as stack:
        m = Mem(nc, stack)
        INNER = FH * G
        NU = NT // 2
        x1 = m.sb("f_x1", [P, NT, D])
        swT = m.sb("f_swT", [128, 4, NT, P])
        bias = m.sb("f_bias", [P, D])
        norm = Norm(m, "f")
        wfx = m.sb("f_wfx", [128, 2, INNER])
        wout = m.sb("f_wout", [G, FH, D])
        wc = m.sb("f_wc", [128, 2, INNER])
        bc = m.sb("f_bc", [P, INNER])
        mm = m.sb("f_mm", [128, 4, D])
        bfx = m.sb("f_bfx", [1, INNER])
        wqkv = m.sb("f_wqkv", [G, 3, G])
        flat = lambda ap: ap.rearrange("p a c -> p (a c)")

        with ExitStack() as s2:
            m2 = Mem(nc, s2)
            T = lambda n: m2.sem("f0_" + n)
            AB = 3
            agg = m2.sb("f0_agg", [P, AB, 5, D])
            wxT = m2.sb("f0_wxT", [G, FH, D])
            wsl = m2.sb("f0_wsl", [G, G])
            bx = m2.sb("f0_bx", [G, FH])
            bxb = m2.sb("f0_bxb", [G, FH, P])
            bsl = m2.sb("f0_bsl", [P, G])
            temp = m2.sb("f0_temp", [128, FH])
            pW = [m2.ps(f"f0_pW{k}", [128, 512]) for k in range(2)]
            pB = m2.ps("f0_pB", [P, 512])
            x_in = T("x_in"); a_in = [T(f"a_in{j}") for j in range(AB)]; w_in = T("w_in"); a_used = T("a_used")
            bxb_ok = T("bxb_ok"); w_ok = T("w_ok"); vch = T("vch"); stats = T("stats"); sq = T("sq"); done = T("done")
            with nc.Block() as block:
                @block.sync
                def _(sp):
                    sp.dma_start(bias[:], ins["L0_gnn_bias"].unsqueeze(0).broadcast_to([P, D])).then_inc(x_in, 16)
                    xv = ins["x"].rearrange("(p t) c -> p t c", t=NT)
                    av = dr["agg0"][0:N, :].rearrange("(p t) c -> p t c", t=NT)
                    for g in range(NT // 5):
                        if g >= AB:
                            sp.wait_ge(a_used, g - AB + 1)
                        sp.dma_start(x1[:, 5 * g:5 * g + 5, :], xv[:, 5 * g:5 * g + 5, :]).then_inc(a_in[g % AB], 16)
                        sp.dma_start(agg[:, g % AB, :, :], av[:, 5 * g:5 * g + 5, :]).then_inc(a_in[g % AB], 16)

                @block.scalar
                def _(act):
                    act.dma_start(wxT[:], ins["L0_ffn_WxT"].rearrange("(h c) i -> c h i", c=G)).then_inc(w_in, 16)
                    act.dma_start(wsl[:], ins["L0_ffn_W_slice"]).then_inc(w_in, 16)
                    act.dma_start(bx[:], ins["L0_ffn_b_x"].rearrange("(h c) -> c h", c=G), allow_slow_non_contiguous=True).then_inc(w_in, 16)
                    act.dma_start(bsl[:], ins["L0_ffn_b_slice"].unsqueeze(0).broadcast_to([P, G])).then_inc(w_in, 16)
                    act.dma_start(temp[:], ins["L0_ffn_temperature"].rearrange("a h b c -> a (h b c)").broadcast_to([128, FH])).then_inc(w_in, 16)
                    act.dma_start(wfx[:], ins["L0_ffn_W_fx"].rearrange("(k p) o -> p k o", p=128)).then_inc(w_in, 16)
                    act.dma_start(wout[:], ins["L0_ffn_W_out"].rearrange("(h c) o -> c h o", c=G)).then_inc(w_in, 16)
                    act.dma_start(bfx[:], ins["L0_ffn_b_fx"].unsqueeze(0)).then_inc(w_in, 16)
                    for q, nm in enumerate("qkv"):
                        act.dma_start(wqkv[:, q, :], ins["L0_ffn_W_" + nm]).then_inc(w_in, 16)
                    act.wait_ge(w_in, 176)
                    act.wait_ge(stats, 1)
                    nc.scalar.activation(norm.rstd[:], norm.rstd[:], ACT.Sqrt).then_inc(sq, 1)

                @block.tensor
                def _(pe):
                    t_ = nc.tensor
                    pe.wait_ge(bxb_ok, 1)
                    for h in range(FH):
                        c = slice(h * G, (h + 1) * G)
                        for k in range(2):
                            t_.matmul(pW[k][:, c], wxT[:, h, k * 128:(k + 1) * 128], wsl[:], start=True, stop=True)
                        last = t_.matmul(pB[:, c], bxb[:, h, :], wsl[:], start=True, stop=True)
                    last.then_inc(w_ok, 1)

                @block.vector
                def _(dve):
                    v = nc.vector
                    ch = Chain(dve, vch)
                    dve.wait_ge(x_in, 16)
                    for g in range(NT // 5):
                        dve.wait_ge(a_in[g % AB], 32 * (g // AB + 1))
                        xs = x1[:, 5 * g:5 * g + 5, :]
                        ch.link(v.tensor_tensor(xs, xs, over(bias[:], 1, 5), ALU.add))
                        v.tensor_tensor(xs, xs, agg[:, g % AB, :, :], ALU.add).then_inc(a_used, 1)
                    dve.wait_ge(a_used, NT // 5)
                    dve.wait_ge(w_in, 176)
                    v.tensor_copy(bxb[:], over(bx[:], 2, P)).then_inc(bxb_ok, 1)
                    ch.link(v.tensor_scalar(temp[:], temp[:], 0.1, 5.0, ALU.max, ALU.min))
                    ch.link(v.reciprocal(temp[:], temp[:]))
                    norm.statistics(dve, v, x1)
                    dve.wait_ge(w_ok, 1)
                    g3 = lambda ap: ap.rearrange("p (h g) -> p h g", h=FH)
                    for k in range(2):
                        v.tensor_tensor(g3(wc[:, k, :]), g3(pW[k][:]), over(temp[:], 2, G), ALU.mult)
                    ch.link(v.tensor_tensor(g3(bc[:]), g3(pB[:]), over(bsl[:], 1, FH), ALU.add))
                    ch.link(v.tensor_tensor(g3(bc[:]), g3(bc[:]), over(temp[0:P, :], 2, G), ALU.mult))
                    ch.link(v.memset(norm.a[:], 0.0))
                    norm.variance(v, ch, stats)
                    dve.wait_ge(sq, 1)
                    norm.scales(v, ch, done)

        st = m.sb("f_sums", [128, 4, D + 1])
        with ExitStack() as s2:
            m2 = Mem(nc, s2)
            T = lambda n: m2.sem("f1_" + n)
            XB, W = 5, 10
            xn = m2.sb("f1_xn", [P, XB, D + 1])
            xnT = m2.sb("f1_xnT", [128, 2, 2, P])
            lg = m2.sb("f1_lg", [P, 2, INNER])
            sw = m2.sb("f1_sw", [P, 2, INNER])
            top = m2.sb("f1_top", [P, 2, FH])
            den = m2.sb("f1_den", [P, 2, FH])
            pT = m2.ps("f1_pT", [128, 2, 128])
            pL = [m2.ps(f"f1_pL{b}", [P, 512]) for b in range(2)]
            pS = m2.ps("f1_pS", [128, 4, 128])
            pTok = [m2.ps(f"f1_pTok{k}", [128, 512]) for k in range(4)]
            zero = m2.sb("f1_zero", [Q, XW])
            zeroed = T("zeroed"); z_out = T("z_out")
            one = T("one"); xn_ok = T("xn_ok"); t_ok = T("t_ok"); xnT_ok = T("xnT_ok"); lg_ok = T("lg_ok"); sub_ok = T("sub_ok")
            exp_ok = T("exp_ok"); sw_ok = T("sw_ok"); s_ok = T("s_ok"); swT_ok = T("swT_ok"); fch = T("fch"); bch = T("bch"); pace = T("pace"); tok = T("tok")
            g3 = lambda ap: ap.rearrange("p (h g) -> p h g", h=FH)
            with nc.Block() as block:
                @block.gpsimd
                def _(pool):
                    pool.memset(zero[:], 0.0).then_inc(zeroed, 1)
                    pool.wait_ge(zeroed, 1)
                    pool.iota(zero[:, D:XW].bitcast(I32), pattern=[[0, 1]], base=2 * N, channel_multiplier=1).then_inc(zeroed, 1)

                @block.sync
                def _(sp):
                    sp.wait_ge(zeroed, 2)
                    sp.dma_start(dr["xs"].rearrange("(t p) c -> p t c", p=Q), over(zero[:], 1, MT)).then_inc(z_out, 16)
                    sp.wait_ge(z_out, 16)

                @block.tensor
                def _(pe):
                    t_ = nc.tensor

                    def turn(u, r):
                        pe.wait_ge(xn_ok, W * u + (r + 1))
                        if not (isinstance(u, int) and u == 0 and r == 0):
                            pe.sem_inc(pace, 1)
                            pe.wait_ge(xnT_ok, W * u + r)
                        for k in range(2):
                            last = t_.transpose(pT[:, k, 0:P], xn[:, r % XB, k * 128:(k + 1) * 128], K["ident"][0:P, 0:P])
                        last.then_inc(t_ok, 1)

                    def logits(u, r, early):
                        pe.wait_ge(xnT_ok, W * u + (r + 1))
                        if not early:
                            pe.sem_inc(pace, 1)
                            pe.wait_ge(sub_ok, W * u + (r - 1))
                        for k in range(2):
                            last = t_.matmul(pL[r % 2][:], xnT[:, r % 2, k, :], wc[:, k, :], start=(k == 0), stop=(k == 1))
                        last.then_inc(lg_ok, 1)

                    def group(u, first, last_group):
                        for r in range(W):
                            if r + 3 < W or not last_group:
                                turn(u, r + 3)
                            if r + 2 < W or not last_group:
                                logits(u, r + 2, False)
                            pe.wait_ge(sw_ok, W * u + (r + 1))
                            for k in range(4):
                                t_.matmul(pTok[k][:, 0:D + 1], sw[:, r % 2, k * 128:(k + 1) * 128], xn[:, r % XB, :],
                                          start=first and r == 0, stop=last_group and r == W - 1, skip_group_check=True)
                            if not (first and r == 0):
                                pe.wait_ge(swT_ok, W * u + r)
                            for k in range(4):
                                last = t_.transpose(pS[:, k, 0:P], sw[:, r % 2, k * 128:(k + 1) * 128], K["ident"][0:P, 0:P])
                            last.then_inc(s_ok, 1)
                    turn(0, 0)
                    turn(0, 1)
                    logits(0, 0, True)
                    turn(0, 2)
                    logits(0, 1, True)
                    paired(pe, NT // W, group)

                @block.scalar
                def _(act):
                    s = nc.scalar

                    def normed(u, r, early):
                        tc = bass.ds(W * u + r, 1)
                        if not early:
                            act.wait_ge(s_ok, W * u + (r - XB + 1))
                            act.sem_inc(pace, 1)
                        s.activation(xn[:, r % XB, 0:D], flat(x1[:, tc, :]), ACT.Identity, bias=norm.nbias[:, tc],
                                     scale=norm.rstd[:, tc]).then_inc(xn_ok, 1)

                    def turned(u, r):
                        act.wait_ge(t_ok, W * u + (r + 1))
                        s.activation(xnT[:, r % 2, :, :], pT[:, :, 0:P], ACT.Copy).then_inc(xnT_ok, 1)

                    def keep(u, r):
                        t = W * u + r
                        act.wait_ge(s_ok, t + 1)
                        act.sem_inc(pace, 1)
                        s.activation(swT[:, :, bass.ds(t, 1), :].rearrange("p k a c -> p (k a) c"), pS[:, :, 0:P], ACT.Copy).then_inc(swT_ok, 1)

                    def exponentials(u, r):
                        act.wait_ge(sub_ok, W * u + (r + 1))
                        s.activation(lg[:, r % 2, :], lg[:, r % 2, :], ACT.Exp).then_inc(exp_ok, 1)

                    def group(u, first, last_group):
                        for r in range(W):
                            if r + 3 < W or not last_group:
                                turned(u, r + 3)
                            if r + 4 < W or not last_group:
                                normed(u, r + 4, first and r + 4 < XB)
                            if not (first and r == 0):
                                keep(u, r - 1)
                            if r + 1 < W or not last_group:
                                exponentials(u, r + 1)
                    act.wait_ge(one, 1)
                    for r in range(4):
                        normed(0, r, True)
                    for r in range(3):
                        turned(0, r)
                    exponentials(0, 0)
                    paired(act, NT // W, group)
                    keep(NT // W - 1, W - 1)

                @block.vector
                def _(dve):
                    v = nc.vector
                    v.memset(xn[:, :, D:D + 1], 1.0).then_inc(one, 1)

                    def front(u, r, early):
                        t, b = W * u + r, r % 2
                        ch = Chain(dve, fch, 2 * t)
                        dve.wait_ge(lg_ok, t + 1)
                        dve.sem_inc(pace, 1)
                        if not early:
                            dve.wait_ge(sw_ok, t - 1)
                            dve.sem_inc(pace, 1)
                        ch.link(v.tensor_tensor(lg[:, b, :], pL[b][:], bc[:], ALU.add))
                        ch.link(v.reduce_max(top[:, b, :], g3(lg[:, b, :]), axis=AX))
                        v.tensor_tensor(g3(lg[:, b, :]), g3(lg[:, b, :]), over(top[:, b, :], 2, G), ALU.subtract).then_inc(sub_ok, 1)

                    def back(u, r, early):
                        t, b = W * u + r, r % 2
                        ch = Chain(dve, bch, 2 * t)
                        dve.wait_ge(exp_ok, t + 1)
                        dve.sem_inc(pace, 1)
                        ch.link(v.reduce_sum(den[:, b, :], g3(lg[:, b, :]), axis=AX))
                        ch.link(v.reciprocal(den[:, b, :], den[:, b, :]))
                        if not early:
                            dve.wait_ge(s_ok, t - 1)
                            dve.sem_inc(pace, 1)
                        v.tensor_tensor(g3(sw[:, b, :]), g3(lg[:, b, :]), over(den[:, b, :], 2, G), ALU.mult).then_inc(sw_ok, 1)

                    def group(u, first, last_group):
                        for r in range(W):
                            if r + 1 < W or not last_group:
                                front(u, r + 1, first and r + 1 < 2)
                            back(u, r, first and r < 2)
                    front(0, 0, True)
                    paired(dve, NT // W, group)
                    dve.wait_ge(s_ok, NT)
                    for k in range(4):
                        v.tensor_copy(st[:, k, :], pTok[k][:, 0:D + 1])

        with ExitStack() as s2:
            m2 = Mem(nc, s2)
            T = lambda n: m2.sem("f2_" + n)
            rn = m2.sb("f2_rn", [128, 4])
            stT = m2.sb("f2_stT", [128, 2, INNER])
            nrow = m2.sb("f2_nrow", [1, INNER])
            tok = m2.sb("f2_tok", [G, INNER])
            q = m2.sb("f2_q", [G, INNER])
            k_ = m2.sb("f2_k", [G, INNER])
            vv = m2.sb("f2_v", [G, INNER])
            at = m2.sb("f2_at", [G, INNER])
            atT = m2.sb("f2_atT", [G, INNER])
            red = m2.sb("f2_red", [G, FH])
            oz = m2.sb("f2_oz", [G, FH, 128])
            pA = m2.ps("f2_pA", [128, 2, 512])
            pN = m2.ps("f2_pN", [1, 512])
            pq = m2.ps("f2_pq", [G, 512])
            pk = m2.ps("f2_pk", [G, 512])
            pv = m2.ps("f2_pv", [G, 512])
            pM = m2.ps("f2_pM", [128, 2, 512])
            toP = T("toP"); toV = T("toV"); vch = T("vch"); exp_in = T("exp_in"); exp_out = T("exp_out")
            g3 = lambda ap: ap.rearrange("p (h g) -> p h g", h=FH)
            hs = lambda h: slice(h * G, (h + 1) * G)
            with nc.Block() as block:
                @block.tensor
                def _(pe):
                    t_ = nc.tensor
                    pe.wait_ge(toP, 1)
                    for k in range(4):
                        for i in range(2):
                            t_.transpose(pA[:, i, k * 128:(k + 1) * 128], st[:, k, i * 128:(i + 1) * 128], K["ident"][:])
                        last = t_.transpose(pN[:, k * 128:(k + 1) * 128], st[:, k, D:D + 1], K["ident"][:])
                    last.then_inc(toV, 1)
                    pe.wait_ge(toP, 2)
                    for h in range(FH):
                        for i in range(2):
                            t_.matmul(pq[:, hs(h)], wfx[:, i, hs(h)], stT[:, i, hs(h)], start=(i == 0), stop=False)
                        last = t_.matmul(pq[:, hs(h)], bfx[:, hs(h)], nrow[:, hs(h)], start=False, stop=True)
                    last.then_inc(toV, 1)
                    pe.wait_ge(toP, 3)
                    t_.matmul(pq[:], wqkv[:, 0, :], tok[:], start=True, stop=True)
                    t_.matmul(pk[:], wqkv[:, 1, :], tok[:], start=True, stop=True)
                    for h in range(FH):
                        last = t_.matmul(pv[:, hs(h)], tok[:, hs(h)], wqkv[:, 2, :], start=True, stop=True)
                    last.then_inc(toV, 1)
                    pe.wait_ge(toP, 4)
                    for h in range(FH):
                        last = t_.matmul(pq[:, hs(h)], q[:, hs(h)], k_[:, hs(h)], start=True, stop=True)
                    last.then_inc(toV, 1)
                    pe.wait_ge(toP, 5)
                    for h in range(FH):
                        last = t_.transpose(pk[:, hs(h)], at[:, hs(h)], K["ident"][0:G, 0:G])
                    last.then_inc(toV, 1)
                    pe.wait_ge(toP, 6)
                    for h in range(FH):
                        last = t_.matmul(pq[:, hs(h)], vv[:, hs(h)], atT[:, hs(h)], start=True, stop=True)
                    last.then_inc(toV, 1)
                    pe.wait_ge(toP, 7)
                    for k in range(4):
                        for j in range(2):
                            last = t_.matmul(pM[:, k // 2, (k % 2) * D:(k % 2 + 1) * D], oz[:, 2 * k + j, :], wout[:, 2 * k + j, :],
                                             start=(j == 0), stop=(j == 1))
                    last.then_inc(toV, 1)

                @block.scalar
                def _(act):
                    act.wait_ge(exp_in, 1)
                    nc.scalar.activation(at[:], at[:], ACT.Exp, scale=float(G) ** -0.5).then_inc(exp_out, 1)

                @block.vector
                def _(dve):
                    v = nc.vector
                    ch = Chain(dve, vch)
                    v.memset(oz[:], 0.0)
                    ch.link(v.tensor_scalar(rn[:], st[:, :, D], 1e-5, None, ALU.add))
                    ch.link(v.reciprocal(rn[:], rn[:]))
                    for k in range(4):
                        last = v.tensor_scalar(st[:, k, :], st[:, k, :], rn[:, k:k + 1], None, ALU.mult)
                    last.then_inc(toP, 1)
                    dve.wait_ge(toV, 1)
                    v.tensor_copy(stT[:], pA[:])
                    v.tensor_copy(nrow[:], pN[:]).then_inc(toP, 1)
                    dve.wait_ge(toV, 2)
                    v.tensor_copy(tok[:], pq[:]).then_inc(toP, 1)
                    dve.wait_ge(toV, 3)
                    v.tensor_copy(q[:], pq[:])
                    v.tensor_copy(k_[:], pk[:])
                    v.tensor_copy(vv[:], pv[:]).then_inc(toP, 1)
                    dve.wait_ge(toV, 4)
                    ch.link(v.reduce_max(red[:], g3(pq[:]), axis=AX))
                    v.tensor_tensor(g3(at[:]), g3(pq[:]), over(red[:], 2, G), ALU.subtract).then_inc(exp_in, 1)
                    dve.wait_ge(exp_out, 1)
                    ch.link(v.reduce_sum(red[:], g3(at[:]), axis=AX))
                    ch.link(v.reciprocal(red[:], red[:]))
                    v.tensor_tensor(g3(at[:]), g3(at[:]), over(red[:], 2, G), ALU.mult).then_inc(toP, 1)
                    dve.wait_ge(toV, 5)
                    v.tensor_copy(atT[:], pk[:]).then_inc(toP, 1)
                    dve.wait_ge(toV, 6)
                    for h in range(FH):
                        last = v.tensor_copy(oz[:, h, (h % 2) * G:(h % 2 + 1) * G], pq[:, hs(h)])
                    last.then_inc(toP, 1)
                    dve.wait_ge(toV, 7)
                    v.tensor_copy(mm[:].rearrange("p (a b) c -> p a (b c)", a=2), pM[:])

        with ExitStack() as s2:
            m2 = Mem(nc, s2)
            T = lambda n: m2.sem("f3_" + n)
            swb = m2.sb("f3_swb", [128, 2, 4, P])
            bout = m2.sb("f3_bout", [P, D])
            wuv = m2.sb("f3_wuv", [128, 2, 2 * H])
            bu = m2.sb("f3_bu", [P, 2 * H])
            xn = m2.sb("f3_xn", [P, 2, D])
            xnT = m2.sb("f3_xnT", [128, 2, 2, P])
            RB, W = 5, 10
            row = m2.sb("f3_row", [P, RB, RW])
            pY = [m2.ps(f"f3_pY{b}", [P, D]) for b in range(2)]
            pT = [m2.ps(f"f3_pT{b}", [128, 2, 128]) for b in range(2)]
            pU = [m2.ps(f"f3_pU{b}", [P, 2 * H]) for b in range(2)]
            w_in = T("w_in"); init = T("init"); swb_ok = T("swb_ok"); y_ok = T("y_ok"); y_used = T("y_used"); vch = T("vch"); pace = T("pace")
            stats = T("stats"); sq = T("sq"); rst = T("rst"); xn_ok = T("xn_ok"); t_ok = T("t_ok"); xnT_ok = T("xnT_ok"); u_ok = T("u_ok")
            row_ok = T("row_ok"); row_out = [T(f"row_out{j}") for j in range(RB)]; copied = T("copied"); x_out = T("x_out")
            rows1 = dr["rows1"][0:N, :].rearrange("(p t) c -> p t c", t=NT)
            sv1 = dr["sv1"][0:N, :].rearrange("(p t) c -> p t c", t=NT)
            with nc.Block() as block:
                @block.sync
                def _(sp):
                    sp.dma_start(bout[:], ins["L0_ffn_b_out"].unsqueeze(0).broadcast_to([P, D])).then_inc(w_in, 16)
                    sp.dma_start(wuv[:, :, 0:H], ins["L1_gnn_WuT"].rearrange("(k p) h -> p k h", p=128)).then_inc(w_in, 16)
                    sp.dma_start(wuv[:, :, H:2 * H], ins["L1_gnn_WvT"].rearrange("(k p) h -> p k h", p=128)).then_inc(w_in, 16)
                    sp.wait_ge(init, 2)
                    sp.dma_start(bu[:, 0:H], ins["L1_gnn_b_u"].unsqueeze(0).broadcast_to([P, H])).then_inc(w_in, 16)
                    sp.wait_ge(stats, 1)
                    sp.dma_start(dr["x2"].rearrange("(p t) c -> p t c", t=NT), x1[:]).then_inc(x_out, 16)
                    with sp.Fori(0, NT // W) as u:
                        for r in range(W):
                            sp.wait_ge(row_ok, W * u + (r + 1))
                            sp.sem_inc(pace, 1)
                            sp.dma_start(rows1[:, bass.ds(W * u + r, 1), :].rearrange("p a c -> p (a c)"), row[:, r % RB, :]).then_inc(row_out[r % RB], 16)
                            sp.dma_start(sv1[:, bass.ds(W * u + r, 1), :].rearrange("p a c -> p (a c)"), row[:, r % RB, RW - H:RW]).then_inc(row_out[r % RB], 16)
                    for j in range(RB):
                        sp.wait_ge(row_out[j], 32 * (NT // RB))
                    sp.wait_ge(x_out, 16)

                @block.gpsimd
                def _(pool):
                    def copy(u, first):
                        for b in range(2):
                            t = 2 * u + b
                            if not first:
                                pool.wait_ge(y_ok, t - 1)
                                pool.sem_inc(pace, 1)
                            nc.gpsimd.tensor_copy(swb[:, b, :, :], swT[:, :, bass.ds(t, 1), :].rearrange("p k a c -> p (k a) c")).then_inc(swb_ok, 1)
                    nc.gpsimd.memset(row[:], 1.0).then_inc(init, 1)
                    nc.gpsimd.memset(bu[:], 0.0).then_inc(init, 1)
                    peeled(pool, NU, copy)

                @block.tensor
                def _(pe):
                    t_ = nc.tensor
                    pe.wait_ge(w_in, 64)

                    def product(u, first):
                        for b in range(2):
                            t = 2 * u + b
                            pe.wait_ge(swb_ok, t + 1)
                            if not first:
                                pe.sem_inc(pace, 1)
                                pe.wait_ge(y_used, t - 1)
                            for k in range(4):
                                last = t_.matmul(pY[b][:], swb[:, b, k, :], mm[:, k, :], start=(k == 0), stop=(k == 3))
                            last.then_inc(y_ok, 1)
                    peeled(pe, NU, product)

                    def turn(t, b):
                        pe.wait_ge(xn_ok, t + 1)
                        for k in range(2):
                            last = t_.transpose(pT[b][:, k, 0:P], xn[:, b, k * 128:(k + 1) * 128], K["ident"][0:P, 0:P])
                        last.then_inc(t_ok, 1)

                    def scores(t, b, early):
                        pe.wait_ge(xnT_ok, t + 1)
                        if not early:
                            pe.sem_inc(pace, 1)
                            pe.wait_ge(row_ok, t - 1)
                        for k in range(2):
                            last = t_.matmul(pU[b][:], xnT[:, b, k, :], wuv[:, k, :], start=(k == 0), stop=(k == 1))
                        last.then_inc(u_ok, 1)

                    def group(u, first, last_group):
                        for b in range(2):
                            if b == 0 or not last_group:
                                turn(2 * u + (b + 1), 1 - b)
                            scores(2 * u + b, b, first)
                    turn(0, 0)
                    paired(pe, NU, group)

                @block.scalar
                def _(act):
                    s = nc.scalar
                    act.wait_ge(stats, 1)
                    s.activation(norm.rstd[:], norm.rstd[:], ACT.Sqrt).then_inc(sq, 1)
                    act.wait_ge(rst, 1)

                    def normed(t, b, early):
                        tc = bass.ds(t, 1)
                        if not early:
                            act.wait_ge(copied, t - 1)
                            act.sem_inc(pace, 1)
                        s.activation(xn[:, b, :], flat(x1[:, tc, :]), ACT.Identity, bias=norm.nbias[:, tc],
                                     scale=norm.rstd[:, tc]).then_inc(xn_ok, 1)

                    def turned(t, b, early):
                        act.wait_ge(t_ok, t + 1)
                        if not early:
                            act.sem_inc(pace, 1)
                            act.wait_ge(u_ok, t - 1)
                        s.activation(xnT[:, b, :, :], pT[b][:, :, 0:P], ACT.Copy).then_inc(xnT_ok, 1)

                    def group(u, first, last_group):
                        for b in range(2):
                            if b == 0 or not last_group:
                                normed(2 * u + (b + 1), 1 - b, first and b == 0)
                            turned(2 * u + b, b, first)
                    normed(0, 0, True)
                    paired(act, NU, group)

                @block.vector
                def _(dve):
                    v = nc.vector
                    dve.wait_ge(w_in, 64)
                    with dve.Fori(0, NU) as u:
                        for b in range(2):
                            t = 2 * u + b
                            ch = Chain(dve, vch, 2 * t)
                            xt = flat(x1[:, bass.ds(t, 1), :])
                            ch.link(v.tensor_tensor(xt, xt, bout[:], ALU.add))
                            dve.wait_ge(y_ok, t + 1)
                            dve.sem_inc(pace, 1)
                            ch.link(v.tensor_tensor(xt, xt, pY[b][:], ALU.add))
                            dve.sem_inc(y_used, 1)
                            norm.tile(v, t, x1[:, bass.ds(t, 1), :])
                    ch = Chain(dve, vch, 2 * NT)
                    ch.link(v.memset(norm.a[:], 0.0))
                    norm.variance(v, ch, stats)
                    dve.wait_ge(sq, 1)
                    norm.scales(v, ch, rst)

                    def copy(u, r, early):
                        u, r = u + r // W, r % W
                        if not early:
                            dve.wait_ge(row_out[r % RB], 32 * (W // RB) * u + 32 * (r // RB))
                            dve.sem_inc(pace, 1)
                        dve.wait_ge(xn_ok, W * u + (r + 1))
                        dve.sem_inc(pace, 1)
                        v.tensor_copy(row[:, r % RB, 0:H * VW].rearrange("p (h c) -> p h c", h=H)[:, :, 0:HD],
                                      xn[:, r % 2, :].rearrange("p (c h) -> p h c", h=H)).then_inc(copied, 1)

                    def group(u, first, last_group):
                        for r in range(W):
                            if r < W - 1 or not last_group:
                                copy(u, r + 1, first and r + 1 < RB)
                            dve.wait_ge(u_ok, W * u + (r + 1))
                            dve.sem_inc(pace, 1)
                            v.tensor_tensor(row[:, r % RB, H * VW:RW], pU[r % 2][:], bu[:], ALU.add).then_inc(row_ok, 1)
                    copy(0, 0, True)
                    paired(dve, NT // W, group)


def experts(nc, K, ins, dr, out):
    with ExitStack() as stack:
        m = Mem(nc, stack)
        NU = NT // 2
        flat = lambda ap: ap.rearrange("p a c -> p (a c)")
        pos = [m.sb(f"e_pos{k}", [P, NT], I32) for k in range(2)]
        wgt = [m.sb(f"e_wgt{k}", [P, NT]) for k in range(2)]
        owner = m.sb("e_owner", [1, MT + 1], I32)
        w1 = m.sb("e_w1", [128, X, 2, HID])
        w1_in = m.sem("e_w1_in")

        with ExitStack() as s2:
            m2 = Mem(nc, s2)
            T = lambda n: m2.sem("e0_" + n)
            x3 = m2.sb("e0_x3", [P, NT, D])
            xt = m2.sb("e0_xt", [P, NT, D])
            R = 5
            space = m2.sb("e0_space", [P, R * 2 * XW])
            agg = space[:, 0:2 * 5 * D].rearrange("p (b j c) -> p b j c", b=2, j=5)
            norm1, norm2 = Norm(m2, "e0a"), Norm(m2, "e0b")
            wr = m2.sb("e0_wr", [128, 2, X])
            br = m2.sb("e0_br", [P, X])
            xtT = m2.sb("e0_xtT", [128, 2, 2, P])
            lg = m2.sb("e0_lg", [P, NT, X])
            l2 = m2.sb("e0_l2", [P, NT, X])
            tmp = m2.sb("e0_tmp", [P, NT, X])
            hot = [m2.sb(f"e0_hot{k}", [P, NT, X]) for k in range(2)]
            both = m2.sb("e0_both", [P, NT, X])
            best = [m2.sb(f"e0_best{k}", [P, NT]) for k in range(2)]
            pick = m2.sb("e0_pick", [P, NT])
            rank = m2.sb("e0_rank", [P, NT, X])
            tot = m2.sb("e0_tot", [P, X, NT])
            exc = m2.sb("e0_exc", [P, X, NT])
            zero = m2.sb("e0_zero", [P, X * NT])
            cnt = m2.sb("e0_cnt", [P, X])
            tiles_i = m2.sb("e0_tiles_i", [P, X], I32)
            tiles = m2.sb("e0_tiles", [P, X])
            ends = m2.sb("e0_ends", [P, X])
            shift = m2.sb("e0_shift", [P, X])
            iota_e = m2.sb("e0_iota_e", [P, X])
            iota_t = m2.sb("e0_iota_t", [1, MT])
            own = m2.sb("e0_own", [1, MT, X])
            ownf = m2.sb("e0_ownf", [1, MT])
            posf = m2.sb("e0_posf", [P, NT])
            idx = [[m2.sb(f"e0_idx{r}{k}", [P, 1], I32) for k in range(2)] for r in range(R)]
            xrow = space[:].rearrange("p (r k c) -> p r k c", r=R, k=2)
            ids = m2.sb("e0_ids", [P, 2, NT], I32)
            pT = [m2.ps(f"e0_pT{b}", [128, 2, 128]) for b in range(2)]
            pG = [m2.ps(f"e0_pG{b}", [P, X]) for b in range(2)]
            pR = m2.ps("e0_pR", [P, 512])
            pC = m2.ps("e0_pC", [P, 512])
            a_in = [T("a_in0"), T("a_in1")]; a_used = T("a_used"); w_in = T("w_in"); x_out = T("x_out"); iotas = T("iotas")
            vch = T("vch"); stats1 = T("stats1"); sq1 = T("sq1"); rst1 = T("rst1"); stats2 = T("stats2"); sq2 = T("sq2"); rst2 = T("rst2")
            xt_ok = T("xt_ok"); t_ok = T("t_ok"); xtT_ok = T("xtT_ok"); g_ok = T("g_ok"); g_used = T("g_used"); pace = T("pace")
            both_ok = T("both_ok"); r_ok = T("r_ok"); e_in = T("e_in"); e_out = T("e_out"); row_ok = T("row_ok"); idx_ok = T("idx_ok")
            sent = [T(f"sent{r}") for r in range(R)]
            x3_ok = T("x3_ok")
            with nc.Block() as block:
                @block.sync
                def _(sp):
                    xv = dr["x2"].rearrange("(p t) c -> p t c", t=NT)
                    sp.dma_start(wr[:], ins["L1_ffn_Wr"].rearrange("(k p) e -> p k e", p=128)).then_inc(w_in, 16)
                    sp.dma_start(br[:], ins["L1_ffn_br"].unsqueeze(0).broadcast_to([P, X])).then_inc(w_in, 16)
                    av = dr["agg1"][0:N, :].rearrange("(p t) c -> p t c", t=NT)
                    for g in range(NT // 5):
                        if g >= 2:
                            sp.wait_ge(a_used, g - 1)
                        sp.dma_start(x3[:, 5 * g:5 * g + 5, :], xv[:, 5 * g:5 * g + 5, :]).then_inc(a_in[g % 2], 16)
                        sp.dma_start(agg[:, g % 2, :, :], av[:, 5 * g:5 * g + 5, :]).then_inc(a_in[g % 2], 16)
                    for e in range(X):
                        sp.dma_start(w1[:, e, :, :], ins["L1_ffn_W1"][e].rearrange("(k p) h -> p k h", p=128)).then_inc(w1_in, 16)
                    sp.wait_ge(x3_ok, 1)
                    sp.dma_start(dr["x3"].rearrange("(p t) c -> p t c", t=NT), x3[:]).then_inc(x_out, 16)
                    sp.wait_ge(x_out, 16)
                    sp.wait_ge(w1_in, 16 * X)

                @block.tensor
                def _(pe):
                    t_ = nc.tensor
                    pe.wait_ge(w_in, 32)

                    def turn(t, b):
                        pe.wait_ge(xt_ok, t + 1)
                        for k in range(2):
                            last = t_.transpose(pT[b][:, k, 0:P], xrow[:, b, 0, k * 128:(k + 1) * 128], K["ident"][0:P, 0:P])
                        last.then_inc(t_ok, 1)

                    def product(t, b, early):
                        pe.wait_ge(xtT_ok, t + 1)
                        if not early:
                            pe.sem_inc(pace, 1)
                            pe.wait_ge(g_used, t - 1)
                        for k in range(2):
                            last = t_.matmul(pG[b][:], xtT[:, b, k, :], wr[:, k, :], start=(k == 0), stop=(k == 1))
                        last.then_inc(g_ok, 1)

                    def group(u, first, last_group):
                        for b in range(2):
                            if b == 0 or not last_group:
                                turn(2 * u + (b + 1), 1 - b)
                            product(2 * u + b, b, first)
                    turn(0, 0)
                    paired(pe, NU, group)
                    pe.wait_ge(both_ok, 1)
                    t_.matmul(pR[:, 0:NT * X], K["tri"][0:P, 0:P], both[:].rearrange("p t e -> p (t e)"), start=True, stop=True)
                    t_.matmul(pC[:, 0:NT * X], K["ones"][0:P, 0:P], both[:].rearrange("p t e -> p (t e)"), start=True, stop=True).then_inc(r_ok, 1)

                @block.scalar
                def _(act):
                    s = nc.scalar
                    act.wait_ge(stats1, 1)
                    s.activation(norm1.rstd[:], norm1.rstd[:], ACT.Sqrt).then_inc(sq1, 1)
                    act.wait_ge(rst1, 1)

                    def normed(t, b):
                        tc = bass.ds(t, 1)
                        s.activation(xrow[:, b, 0, 0:D], flat(x3[:, tc, :]), ACT.Identity, bias=norm1.nbias[:, tc], scale=norm1.rstd[:, tc])
                        s.activation(flat(xt[:, tc, :]), flat(x3[:, tc, :]), ACT.Identity, bias=norm1.nbias[:, tc],
                                     scale=norm1.rstd[:, tc]).then_inc(xt_ok, 1)

                    def turned(t, b, early):
                        act.wait_ge(t_ok, t + 1)
                        if not early:
                            act.sem_inc(pace, 1)
                            act.wait_ge(g_ok, t - 1)
                        s.activation(xtT[:, b, :, :], pT[b][:, :, 0:P], ACT.Copy).then_inc(xtT_ok, 1)

                    def group(u, first, last_group):
                        for b in range(2):
                            if b == 0 or not last_group:
                                normed(2 * u + (b + 1), 1 - b)
                            turned(2 * u + b, b, first)
                    normed(0, 0)
                    paired(act, NU, group)
                    act.wait_ge(stats2, 1)
                    s.activation(norm2.rstd[:], norm2.rstd[:], ACT.Sqrt).then_inc(sq2, 1)
                    act.wait_ge(e_in, 1)
                    s.activation(best[1][:], best[1][:], ACT.Exp).then_inc(e_out, 1)
                    act.wait_ge(rst2, 1)

                    def row(u, first):
                        for r in range(R):
                            t = u * R + r
                            tc = bass.ds(t, 1)
                            if not first:
                                act.wait_ge(sent[r], 32 * u)
                                act.sem_inc(pace, 1)
                            for k in range(2):
                                last = s.activation(xrow[:, r, k, 0:D], flat(xt[:, tc, :]), ACT.Identity, bias=norm2.nbias[:, tc],
                                                    scale=norm2.rstd[:, tc])
                            last.then_inc(row_ok, 1)
                    peeled(act, NT // R, row)

                @block.vector
                def _(dve):
                    v = nc.vector
                    ch = Chain(dve, vch)
                    for g in range(NT // 5):
                        dve.wait_ge(a_in[g % 2], 32 * (g // 2 + 1))
                        for j in range(5):
                            xs = x3[:, 5 * g + j, :].rearrange("p (c h) -> p c h", h=H)
                            last = v.tensor_tensor(xs, xs, agg[:, g % 2, j, :].rearrange("p (h c) -> p c h", h=H), ALU.add)
                        last.then_inc(a_used, 1)
                    dve.wait_ge(a_used, NT // 5)
                    dve.sem_inc(x3_ok, 1)
                    norm1.statistics(dve, v, x3)
                    ch.link(v.memset(norm1.a[:], 0.0))
                    norm1.variance(v, ch, stats1)
                    dve.wait_ge(sq1, 1)
                    norm1.scales(v, ch, rst1)
                    dve.wait_ge(w_in, 32)
                    with dve.Fori(0, NU) as u:
                        for b in range(2):
                            t = 2 * u + b
                            dve.wait_ge(xt_ok, t + 1)
                            norm2.tile(v, t, xt[:, bass.ds(t, 1), :])
                            dve.wait_ge(g_ok, t + 1)
                            dve.sem_inc(pace, 1)
                            v.tensor_tensor(lg[:, bass.ds(t, 1), :].rearrange("p a c -> p (a c)"), pG[b][:], br[:], ALU.add).then_inc(g_used, 1)
                    ch.link(v.memset(norm2.a[:], 0.0))
                    norm2.variance(v, ch, stats2)
                    dve.wait_ge(iotas, 4)
                    src = lg
                    for k in range(2):
                        ch.link(v.reduce_max(best[k][:], src[:], axis=AX))
                        ch.link(v.tensor_tensor(tmp[:], src[:], over(best[k][:], 2, X), ALU.is_lt))
                        ch.link(v.scalar_tensor_tensor(tmp[:], tmp[:], float(X), over(iota_e[:], 1, NT), ALU.mult, ALU.add))
                        ch.link(v.tensor_reduce(pick[:], tmp[:], AX, ALU.min))
                        ch.link(v.tensor_tensor(hot[k][:], over(iota_e[:], 1, NT), over(pick[:], 2, X), ALU.is_equal))
                        if k == 0:
                            ch.link(v.scalar_tensor_tensor(l2[:], hot[0][:], -BIG, lg[:], ALU.mult, ALU.add))
                            src = l2
                    v.tensor_tensor(both[:], hot[0][:], hot[1][:], ALU.add).then_inc(both_ok, 1)
                    dve.wait_ge(sq2, 1)
                    v.tensor_tensor(best[1][:], best[1][:], best[0][:], ALU.subtract).then_inc(e_in, 1)
                    norm2.scales(v, ch, rst2)
                    dve.wait_ge(e_out, 1)
                    ch.link(v.tensor_scalar(wgt[0][:], best[1][:], 1.0, None, ALU.add))
                    ch.link(v.reciprocal(wgt[0][:], wgt[0][:]))
                    v.tensor_tensor(wgt[1][:], best[1][:], wgt[0][:], ALU.mult)
                    ch.link(v.memset(zero[:], 0.0))
                    dve.wait_ge(r_ok, 1)
                    v.tensor_copy(rank[:].rearrange("p t e -> p (t e)"), pR[:, 0:NT * X])
                    ch.link(v.tensor_copy(tot[:].rearrange("p e t -> p t e"), pC[:, 0:NT * X].rearrange("p (t e) -> p t e", e=X)))
                    fl = "p e t -> p (e t)"
                    ch.link(v.tensor_tensor_scan(exc[:].rearrange(fl), tot[:].rearrange(fl), zero[:], 0.0, ALU.add, ALU.add))
                    ch.link(v.tensor_tensor(exc[:].rearrange(fl), exc[:].rearrange(fl), tot[:].rearrange(fl), ALU.subtract))
                    ch.link(v.reduce_sum(cnt[:], tot[:], axis=AX))
                    ch.link(v.tensor_scalar(tiles_i[:], cnt[:], float(Q - 1), None, ALU.add))
                    ch.link(v.tensor_scalar(tiles_i[:], tiles_i[:], 7, None, ALU.arith_shift_right))
                    ch.link(v.tensor_copy(tiles[:], tiles_i[:]))
                    ch.link(v.tensor_tensor_scan(ends[:], tiles[:], zero[:, 0:X], 0.0, ALU.add, ALU.add))
                    ch.link(v.tensor_tensor(shift[:], ends[:], tiles[:], ALU.subtract))
                    ch.link(v.scalar_tensor_tensor(shift[:], shift[:], float(Q), exc[:, :, 0], ALU.mult, ALU.subtract))
                    ch.link(v.tensor_tensor(exc[:], exc[:], over(shift[:], 2, NT), ALU.add))
                    ch.link(v.tensor_tensor(rank[:], rank[:], exc[:].rearrange("p e t -> p t e"), ALU.add))
                    for k in range(2):
                        ch.link(v.tensor_tensor(tmp[:], rank[:], hot[k][:], ALU.mult))
                        ch.link(v.reduce_sum(posf[:], tmp[:], axis=AX))
                        ch.link(v.tensor_copy(pos[k][:], posf[:]))

                    def index(u, first):
                        for r in range(R):
                            t = u * R + r
                            if not first:
                                dve.wait_ge(sent[r], 32 * u)
                                dve.sem_inc(pace, 1)
                            v.tensor_copy(idx[r][0][:], pos[0][:, bass.ds(t, 1)])
                            v.tensor_copy(idx[r][1][:], pos[1][:, bass.ds(t, 1)])
                            v.tensor_copy(xrow[:, r, :, D:XW].bitcast(I32), ids[:, :, bass.ds(t, 1)]).then_inc(idx_ok, 1)
                    peeled(dve, NT // R, index)
                    ch.link(v.tensor_tensor(own[:], over(iota_t[:], 2, X), over(ends[0:1, :], 1, MT), ALU.is_ge))
                    ch.link(v.reduce_sum(ownf[:], own[:], axis=AX))
                    ch.link(v.tensor_scalar(owner[:, 0:MT], ownf[:], float(X - 1), None, ALU.min))
                    pairs = owner[:, MT:MT + 1]
                    ch.link(v.tensor_scalar(pairs, ends[0:1, X - 1:X], 1.0, None, ALU.add))
                    ch.link(v.tensor_scalar(pairs, pairs, 1, None, ALU.arith_shift_right))
                    ch.link(v.tensor_scalar(pairs, pairs, -2.0, None, ALU.add))

                @block.gpsimd
                def _(pool):
                    pool.iota(iota_e[:], pattern=[[1, X]], base=0, channel_multiplier=0, allow_small_or_imprecise_dtypes=True).then_inc(iotas, 1)
                    pool.iota(iota_t[:], pattern=[[1, MT]], base=0, channel_multiplier=0, allow_small_or_imprecise_dtypes=True).then_inc(iotas, 1)
                    for k in range(2):
                        pool.iota(ids[:, k, :], pattern=[[1, NT]], base=k * N, channel_multiplier=NT).then_inc(iotas, 1)
                    with pool.Fori(0, NT // R) as u:
                        for r in range(R):
                            pool.wait_ge(idx_ok, u * R + (r + 1))
                            pool.sem_inc(pace, 1)
                            pool.wait_ge(row_ok, u * R + (r + 1))
                            pool.sem_inc(pace, 1)
                            for k in range(2):
                                pool.indirect_dma_start(out=dr["xs"], out_offset=bass.IndirectOffsetOnAxis(ap=idx[r][k][:, 0:1], axis=0),
                                                        in_=xrow[:, r, k, :], in_offset=None).then_inc(sent[r], 16)
                    for r in range(R):
                        pool.wait_ge(sent[r], 32 * (NT // R))

        with ExitStack() as s2:
            m2 = Mem(nc, s2)
            T = lambda n: m2.sem("e1_" + n)
            w2 = m2.sb("e1_w2", [128, X, KC, D])
            b1 = m2.sb("e1_b1", [Q, X, HID])
            b2 = m2.sb("e1_b2", [Q, X, D])
            gl = m2.sb("e1_gl", [128, X, 2])
            bl = m2.sb("e1_bl", [128, X, 2])
            xs = m2.sb("e1_xs", [Q, 2, D])
            goal = m2.sb("e1_goal", [Q, MT])
            goal_b = [m2.sb(f"e1_goal{b}", [Q, 1], I32) for b in range(2)]
            xT = m2.sb("e1_xT", [128, 2, 2, Q])
            hh = m2.sb("e1_hh", [Q, 2, HID])
            hT = m2.sb("e1_hT", [128, 2, KC, Q])
            ys = m2.sb("e1_ys", [Q, 2, D])
            pX = m2.ps("e1_pX", [128, 2, Q])
            pH = m2.ps("e1_pH", [Q, HID])
            pHT = m2.ps("e1_pHT", [128, KC, Q])
            pY = [m2.ps(f"e1_pY{b}", [Q, D]) for b in range(2)]
            w_in = T("w_in"); x_in = [T("x_in0"), T("x_in1")]; xT_ps = T("xT_ps"); xT_ok = T("xT_ok"); h_ok = T("h_ok"); g_ok = T("g_ok")
            hT_ps = T("hT_ps"); hT_ok = T("hT_ok"); y_ok = T("y_ok"); ys_ok = T("ys_ok"); y_out = [T("y_out0"), T("y_out1")]; pace = T("pace")
            goal_in = T("goal_in"); b_in = T("b_in"); hb_ok = T("hb_ok"); ab_in = T("ab_in")
            last_pair = lambda eng: eng.value_load(owner[0:1, MT:MT + 1], min_val=LEAST // 2 - 2, max_val=MT // 2 - 2) + 1

            def pairs_of_tiles(eng, n, body):
                body(0, True, False)
                with eng.Fori(1, n) as u:
                    body(u, False, False)
                body(n, False, True)
            with nc.Block() as block:
                @block.sync
                def _(sp):
                    def load(u, b):
                        sp.dma_start(xs[:, b, :], dr["xs"].rearrange("(t q) c -> t q c", q=Q)[bass.ds(2 * u + b, 1), :, 0:D].rearrange("a q c -> (a q) c")).then_inc(x_in[b], 16)
                    n = last_pair(sp)
                    load(0, 0)
                    load(0, 1)
                    for e in range(X):
                        sp.dma_start(w2[:, e, :, :], ins["L1_ffn_W2"][e].rearrange("(k p) o -> p k o", p=128)).then_inc(w_in, 16)

                    def step(u, first):
                        for b in range(2):
                            sp.wait_ge(xT_ps, 2 * u + (b + 1))
                            sp.sem_inc(pace, 1)
                            load(u + 1, b)
                    peeled(sp, n, step)

                @block.gpsimd
                def _(pool):
                    n = last_pair(pool)
                    pool.dma_start(goal[:], dr["xs"][:, D:XW].rearrange("(t q) o -> q (t o)", q=Q), allow_slow_non_contiguous=True).then_inc(goal_in, 16)
                    with pool.Fori(0, n + 1) as u:
                        for b in range(2):
                            pool.wait_ge(ys_ok, 2 * u + (b + 1))
                            pool.sem_inc(pace, 1)
                            pool.indirect_dma_start(out=dr["ys"], out_offset=bass.IndirectOffsetOnAxis(ap=goal_b[b][:, 0:1], axis=0),
                                                    in_=ys[:, b, :], in_offset=None).then_inc(y_out[b], 16)
                    for b in range(2):
                        pool.wait_ge(y_out[b], 16 * (n + 1))
                        pool.sem_inc(pace, 1)

                @block.tensor
                def _(pe):
                    t_ = nc.tensor

                    def expert(t):
                        return pe.value_load(owner[0:1, bass.ds(t, 1)], min_val=0, max_val=X - 1)

                    def rows_turn(u, b):
                        t = 2 * u + b
                        pe.wait_ge(x_in[b], 16 * u + 16)
                        if not (isinstance(t, int) and t == 0):
                            pe.sem_inc(pace, 1)
                            pe.wait_ge(xT_ok, t)
                        for k in range(2):
                            last = t_.transpose(pX[:, k, :], xs[:, b, k * 128:(k + 1) * 128], K["ident"][:])
                        last.then_inc(xT_ps, 1)

                    def hidden(t, b, e):
                        pe.wait_ge(xT_ok, t + 1)
                        if not (isinstance(t, int) and t == 0):
                            pe.sem_inc(pace, 1)
                            pe.wait_ge(hb_ok, t)
                        for c in range(2):
                            sl = slice(c * 512, (c + 1) * 512)
                            for k in range(2):
                                last = t_.matmul(pH[:, sl], xT[:, b, k, :], w1[:, bass.ds(e, 1), k, sl].rearrange("p a h -> p (a h)"), start=(k == 0), stop=(k == 1))
                        last.then_inc(h_ok, 1)

                    def units_turn(t, b):
                        pe.wait_ge(g_ok, t + 1)
                        if not (isinstance(t, int) and t == 0):
                            pe.sem_inc(pace, 1)
                            pe.wait_ge(hT_ok, t)
                        for k in range(KC):
                            last = t_.transpose(pHT[:, k, :], hh[:, b, k * 128:(k + 1) * 128], K["ident"][:])
                        last.then_inc(hT_ps, 1)

                    def outputs(t, b, e):
                        pe.wait_ge(hT_ok, t + 1)
                        if not (isinstance(t, int) and t < 2):
                            pe.sem_inc(pace, 1)
                            pe.wait_ge(ys_ok, t - 1)
                        for k in range(KC):
                            last = t_.matmul(pY[b][:], hT[:, b, k, :], w2[:, bass.ds(e, 1), k, :].rearrange("p a h -> p (a h)"), start=(k == 0), stop=(k == KC - 1))
                        last.then_inc(y_ok, 1)

                    def group(u, first, last_group):
                        for b in range(2):
                            t = 2 * u + b
                            more = b == 0 or not last_group
                            if more:
                                e = expert(t + 1)
                            if not last_group:
                                rows_turn(u + 1, b)
                            units_turn(t, b)
                            if more:
                                hidden(t + 1, 1 - b, e)
                            outputs(t, b, expert(t))
                    rows_turn(0, 0)
                    rows_turn(0, 1)
                    hidden(0, 0, expert(0))
                    pe.wait_ge(w_in, 16 * X)
                    pairs_of_tiles(pe, last_pair(pe), group)

                @block.scalar
                def _(act):
                    s = nc.scalar
                    act.dma_start(gl[:], ins["L1_ffn_ln_g"].rearrange("e (k p) -> p e k", p=128), allow_slow_non_contiguous=True).then_inc(ab_in, 16)
                    act.dma_start(bl[:], ins["L1_ffn_ln_b"].rearrange("e (k p) -> p e k", p=128), allow_slow_non_contiguous=True).then_inc(ab_in, 16)
                    act.dma_start(b1[:].rearrange("q e h -> q (e h)"), ins["L1_ffn_b1"].rearrange("e h -> (e h)").unsqueeze(0).broadcast_to([Q, X * HID])).then_inc(b_in, 16)
                    act.dma_start(b2[:].rearrange("q e h -> q (e h)"), ins["L1_ffn_b2"].rearrange("e h -> (e h)").unsqueeze(0).broadcast_to([Q, X * D])).then_inc(b_in, 16)
                    act.wait_ge(ab_in, 32)

                    def affine(t, b):
                        e = act.value_load(owner[0:1, bass.ds(t, 1)], min_val=0, max_val=X - 1)
                        act.wait_ge(xT_ps, t + 1)
                        if not (isinstance(t, int) and t < 2):
                            act.sem_inc(pace, 1)
                            act.wait_ge(h_ok, t - 1)
                        for k in range(2):
                            last = s.activation(xT[:, b, k, :], pX[:, k, :], ACT.Identity, bias=bl[:, bass.ds(e, 1), k], scale=gl[:, bass.ds(e, 1), k])
                        last.then_inc(xT_ok, 1)

                    def units(t, b):
                        act.wait_ge(hb_ok, t + 1)
                        s.activation(hh[:, b, :], hh[:, b, :], ACT.Gelu).then_inc(g_ok, 1)

                    def group(u, first, last_group):
                        for b in range(2):
                            t = 2 * u + b
                            if not last_group:
                                affine(t + 2, b)
                            if b == 0 or not last_group:
                                units(t + 1, 1 - b)
                    affine(0, 0)
                    affine(1, 1)
                    units(0, 0)
                    pairs_of_tiles(act, last_pair(act), group)

                @block.vector
                def _(dve):
                    v = nc.vector
                    dve.wait_ge(goal_in, 16)
                    dve.wait_ge(b_in, 32)

                    def expert(t):
                        return dve.value_load(owner[0:1, bass.ds(t, 1)], min_val=0, max_val=X - 1)

                    def biased(t, b):
                        e = expert(t)
                        dve.wait_ge(h_ok, t + 1)
                        if not (isinstance(t, int) and t < 2):
                            dve.sem_inc(pace, 1)
                            dve.wait_ge(hT_ps, t - 1)
                        v.tensor_tensor(hh[:, b, :], pH[:], flat(b1[:, bass.ds(e, 1), :]), ALU.add).then_inc(hb_ok, 1)

                    def group(u, first, last_group):
                        for b in range(2):
                            t = 2 * u + b
                            dve.wait_ge(hT_ps, t + 1)
                            if not first:
                                dve.sem_inc(pace, 1)
                                dve.wait_ge(y_ok, t - 1)
                            v.tensor_copy(hT[:, b, :, :], pHT[:]).then_inc(hT_ok, 1)
                            if b == 0 or not last_group:
                                biased(t + 1, 1 - b)
                            e = expert(t)
                            dve.wait_ge(y_ok, t + 1)
                            if not first:
                                dve.sem_inc(pace, 1)
                                dve.wait_ge(y_out[b], 16 * u)
                            v.tensor_copy(goal_b[b][:], goal[:, bass.ds(t, 1)].bitcast(I32))
                            v.tensor_tensor(ys[:, b, :], pY[b][:], flat(b2[:, bass.ds(e, 1), :]), ALU.add).then_inc(ys_ok, 1)
                    biased(0, 0)
                    pairs_of_tiles(dve, last_pair(dve), group)

        with ExitStack() as s2:
            m2 = Mem(nc, s2)
            T = lambda n: m2.sem("e2_" + n)
            R, B = 5, 3
            x3 = m2.sb("e2_x3", [P, NT, D])
            yr = m2.sb("e2_yr", [P, B, 2, R, D])
            y_in = [T(f"y_in{b}") for b in range(B)]; vch = T("vch"); done = T("done"); o_out = T("o_out")
            with nc.Block() as block:
                @block.sync
                def _(sp):
                    xv = dr["x3"].rearrange("(p t) c -> p t c", t=NT)
                    yv = [dr["ys"][k * N:(k + 1) * N, :].rearrange("(p t) c -> p t c", t=NT) for k in range(2)]
                    for g in range(NT // R):
                        if g >= B:
                            sp.wait_ge(done, g - B + 1)
                        ts = slice(g * R, (g + 1) * R)
                        sp.dma_start(x3[:, ts, :], xv[:, ts, :]).then_inc(y_in[g % B], 16)
                        for k in range(2):
                            sp.dma_start(yr[:, g % B, k, :, :], yv[k][:, ts, :]).then_inc(y_in[g % B], 16)

                @block.scalar
                def _(act):
                    ov = out.rearrange("(p t) c -> p t c", t=NT)
                    for g in range(NT // R):
                        act.wait_ge(done, g + 1)
                        act.dma_start(ov[:, g * R:(g + 1) * R, :], x3[:, g * R:(g + 1) * R, :]).then_inc(o_out, 16)
                    act.wait_ge(o_out, 16 * (NT // R))

                @block.vector
                def _(dve):
                    v = nc.vector
                    ch = Chain(dve, vch)
                    for g in range(NT // R):
                        dve.wait_ge(y_in[g % B], 48 * (g // B + 1))
                        for k in range(2):
                            for r in range(R):
                                t = g * R + r
                                last = v.scalar_tensor_tensor(x3[:, t, :], yr[:, g % B, k, r, :], wgt[k][:, t:t + 1], x3[:, t, :], ALU.mult, ALU.add)
                            if k == 0:
                                ch.link(last)
                            else:
                                last.then_inc(done, 1)


def layouts(inputs):
    T = np.ascontiguousarray
    return {
        "L0_gnn_WT": T(np.asarray(inputs["L0_gnn_W"]).T),
        "L0_gnn_edge_WT": T(np.asarray(inputs["L0_gnn_edge_W"]).T),
        "L1_gnn_WuT": T(np.asarray(inputs["L1_gnn_W_u"]).T),
        "L1_gnn_WvT": T(np.asarray(inputs["L1_gnn_W_v"]).T),
        "L0_ffn_WxT": T(np.asarray(inputs["L0_ffn_W_x"]).T),
    }


def program(nc, ins, out):
    with ExitStack() as stack:
        m = Mem(nc, stack)
        K = {"ident": m.sb("k_ident", [128, 128]), "tri": m.sb("k_tri", [128, 128]), "ones": m.sb("k_ones", [128, 128]),
             "iota64": m.sb("k_iota64", [128, NB]), "padrec": m.sb("k_padrec", [NPAD - N, 4], I32), "pt": m.sb("k_pt", [Q, QT, 4], I32), "rp": m.sb("k_rp", [Q, QT]),
             "deg": m.sb("k_deg", [Q, QT]), "ct": m.sb("k_ct", [1, QT + 2], I32)}

        def scratch(name, shape, dt=F32):
            return nc.dram_tensor(name, shape, dt, kind="Internal").ap()
        dr = {"rows0": scratch("rows0", (NPAD, RW)), "rows1": scratch("rows1", (NPAD, RW)), "sv1": scratch("sv1", (NPAD, H)),
              "rec": scratch("rec", (E, REC)), "rp": scratch("rp", (1, N + 1), I32),
              "noderec": scratch("noderec", (NPAD, 4), I32), "slots": scratch("slots", (CMAX, Q, REC)),
              "agg0": scratch("agg0", (NPAD, D)), "agg1": scratch("agg1", (NPAD, D)), "x2": scratch("x2", (N, D)), "x3": scratch("x3", (N, D)),
              "xs": scratch("xs", (MT * Q, XW)),
              "ys": scratch("ys", (2 * N + Q, D))}
        sort_nodes(nc, K, ins, dr)
        graph(nc, K, ins, dr, 0)
        slice_ffn(nc, K, ins, dr)
        graph(nc, K, ins, dr, 1)
        experts(nc, K, ins, dr, out)


_INS = ["x", "src", "dst", "edge_attr_3", "L0_gnn_W", "L0_gnn_a_src", "L0_gnn_a_dst", "L0_gnn_edge_b", "L0_gnn_bias",
        "L0_ffn_W_fx", "L0_ffn_b_fx", "L0_ffn_b_x", "L0_ffn_W_slice", "L0_ffn_b_slice", "L0_ffn_W_q", "L0_ffn_W_k",
        "L0_ffn_W_v", "L0_ffn_W_out", "L0_ffn_b_out", "L0_ffn_temperature", "L1_gnn_b_u", "L1_ffn_Wr", "L1_ffn_br",
        "L1_ffn_ln_g", "L1_ffn_ln_b", "L1_ffn_W1", "L1_ffn_b1", "L1_ffn_W2", "L1_ffn_b2"]


def kernel(**inputs):
    import concourse.bacc as bacc
    from concourse.bass_utils import run_bass_kernel_spmd

    nc = bacc.Bacc("TRN2", target_bir_lowering=False, num_devices=1)
    given = {name: np.ascontiguousarray(inputs[name]) for name in _INS}
    given.update(layouts(inputs))
    arrays, aps = {}, {}
    for name, a in given.items():
        arrays[f"in_{name}"] = a
        aps[name] = nc.dram_tensor(f"in_{name}", a.shape, mybir.dt.from_np(a.dtype), kind="ExternalInput").ap()
    out = nc.dram_tensor("out_0", (N, D), F32, kind="ExternalOutput").ap()
    program(nc, aps, out)
    r = run_bass_kernel_spmd(nc, [arrays], core_ids=[0])
    return r.results[0]["out_0"]
```
